# Optimizing a Trainium2 kernel written in Bass

```python
import numpy as np
import jax
import jax.numpy as jnp

def _softmax(x, axis=-1):
    return jax.nn.softmax(x, axis=axis)

def _gelu(x):
    return jax.nn.gelu(x, approximate=True)

def _silu(x):
    return jax.nn.silu(x)

def _sigmoid(x):
    return jax.nn.sigmoid(x)

def _layernorm(x, axis=-1, eps=1e-05):
    m = jnp.mean(x, axis=axis, keepdims=True)
    v = jnp.var(x, axis=axis, keepdims=True)
    return (x - m) / jnp.sqrt(v + eps)

def _scatter_add(tgt, idx, src, axis=0):
    return tgt.at[idx].add(src)

def _segment_sum(src, seg, n):
    return jax.ops.segment_sum(src, seg, n)
kernel_name = 'mk_recurrent_d1_jaxref_r4_bee71b'

def setup_inputs(seed: int=0):
    np.random.seed(seed)
    _w = jnp.asarray

    def _L0_attn_setup():
        import jax, jax.numpy as jnp
        import numpy as np
        D_MODEL = 512
        D_STATE = 16
        D_CONV = 4
        EXPAND = 2
        D_INNER = D_MODEL * EXPAND
        BATCH = 4
        SEQ = 512

        def _silu(v):
            return v * jax.nn.sigmoid(v)
        key = jax.random.key(seed)
        ks = jax.random.split(key, 8)
        s = 0.02
        x = jax.random.normal(ks[0], (BATCH, SEQ, D_MODEL), jnp.float32)
        W_in = jax.random.normal(ks[1], (2 * D_INNER, D_MODEL), jnp.float32) * s
        conv_w = jax.random.normal(ks[2], (D_INNER, 1, D_CONV), jnp.float32) * 0.2
        conv_b = jnp.zeros((D_INNER,), jnp.float32)
        W_x = jax.random.normal(ks[3], (2 * D_STATE + 1, D_INNER), jnp.float32) * s
        A_log = jnp.broadcast_to(jnp.log(jnp.arange(1, D_STATE + 1, dtype=jnp.float32)), (D_INNER, D_STATE)) + jnp.zeros((D_INNER, D_STATE), jnp.float32)
        dt_bias = jax.random.uniform(ks[4], (D_INNER,), jnp.float32, minval=float(np.log(0.001)), maxval=float(np.log(0.1)))
        out_W = jax.random.normal(ks[5], (D_MODEL, D_INNER), jnp.float32) * s
        D = jnp.ones((D_INNER,), jnp.float32)
        return {'x': x, 'W_in': W_in, 'conv_w': conv_w, 'conv_b': conv_b, 'W_x': W_x, 'A_log': A_log, 'dt_bias': dt_bias, 'out_W': out_W, 'D': D}
    _L0_attn_in = _L0_attn_setup()

    def _L0_ffn_setup():
        import jax, jax.numpy as jnp
        import numpy as np
        B_, S, D = (2, 512, 512)
        F_ = 2048
        R = 16
        H = 16
        HD = D // H
        MOD_SCALE = 0.1
        EPS = 1e-06

        def _rmsnorm(x, w):
            v = jnp.mean(x * x, axis=-1, keepdims=True)
            return x * jax.lax.rsqrt(v + EPS) * w

        def _attention(x, Wq, Wk, Wv, Wo):
            b, s, d = x.shape
            q = (x @ Wq.T).reshape(b, s, H, HD)
            k = (x @ Wk.T).reshape(b, s, H, HD)
            v = (x @ Wv.T).reshape(b, s, H, HD)
            scores = jnp.einsum('bqhd,bkhd->bhqk', q, k) / np.sqrt(HD).astype(np.float32)
            causal = jnp.tril(jnp.ones((s, s), bool))
            scores = jnp.where(causal, scores, jnp.finfo(scores.dtype).min)
            probs = jax.nn.softmax(scores, axis=-1)
            out = jnp.einsum('bhqk,bkhd->bqhd', probs, v).reshape(b, s, d)
            return out @ Wo.T
        key = jax.random.key(seed)
        ks = jax.random.split(key, 12)
        sd = 0.02
        return {'hidden_states': jax.random.normal(ks[0], (B_, S, D), jnp.float32), 'ln1_w': jnp.ones((D,), jnp.float32), 'ln2_w': jnp.ones((D,), jnp.float32), 'Wq': jax.random.normal(ks[1], (D, D), jnp.float32) * sd, 'Wk': jax.random.normal(ks[2], (D, D), jnp.float32) * sd, 'Wv': jax.random.normal(ks[3], (D, D), jnp.float32) * sd, 'Wo': jax.random.normal(ks[4], (D, D), jnp.float32) * sd, 'A': jax.random.normal(ks[5], (D, R), jnp.float32) * (0.01 / np.sqrt(D)), 'B': jax.random.normal(ks[6], (R, F_), jnp.float32) * (0.01 / np.sqrt(R)), 'W_in_base': jax.random.normal(ks[7], (F_, D), jnp.float32) * sd, 'W_up_base': jax.random.normal(ks[8], (F_, D), jnp.float32) * sd, 'W_down': jax.random.normal(ks[9], (D, F_), jnp.float32) * sd}
    _L0_ffn_in = _L0_ffn_setup()
    _d = {'L0_attn_x': _L0_attn_in['x'], 'L0_attn_W_in': _L0_attn_in['W_in'], 'L0_attn_conv_w': _L0_attn_in['conv_w'], 'L0_attn_conv_b': _L0_attn_in['conv_b'], 'L0_attn_W_x': _L0_attn_in['W_x'], 'L0_attn_A_log': _L0_attn_in['A_log'], 'L0_attn_dt_bias': _L0_attn_in['dt_bias'], 'L0_attn_out_W': _L0_attn_in['out_W'], 'L0_attn_D': _L0_attn_in['D'], 'L0_ffn_ln1_w': _L0_ffn_in['ln1_w'], 'L0_ffn_ln2_w': _L0_ffn_in['ln2_w'], 'L0_ffn_Wq': _L0_ffn_in['Wq'], 'L0_ffn_Wk': _L0_ffn_in['Wk'], 'L0_ffn_Wv': _L0_ffn_in['Wv'], 'L0_ffn_Wo': _L0_ffn_in['Wo'], 'L0_ffn_A': _L0_ffn_in['A'], 'L0_ffn_B': _L0_ffn_in['B'], 'L0_ffn_W_in_base': _L0_ffn_in['W_in_base'], 'L0_ffn_W_up_base': _L0_ffn_in['W_up_base'], 'L0_ffn_W_down': _L0_ffn_in['W_down']}
    _x0 = _d['L0_attn_x']
    _d['L0_attn_x'] = jax.random.normal(jax.random.fold_in(jax.random.key(seed), 1), (8, 512, 512), dtype=_x0.dtype)
    del _x0
    return _d

def reference(L0_attn_x, L0_attn_W_in, L0_attn_conv_w, L0_attn_conv_b, L0_attn_W_x, L0_attn_A_log, L0_attn_dt_bias, L0_attn_out_W, L0_attn_D, L0_ffn_ln1_w, L0_ffn_ln2_w, L0_ffn_Wq, L0_ffn_Wk, L0_ffn_Wv, L0_ffn_Wo, L0_ffn_A, L0_ffn_B, L0_ffn_W_in_base, L0_ffn_W_up_base, L0_ffn_W_down):

    def _L0_attn_ref(x, W_in, conv_w, conv_b, W_x, A_log, dt_bias, out_W, D):
        import jax, jax.numpy as jnp
        import numpy as np
        D_MODEL = 512
        D_STATE = 16
        D_CONV = 4
        EXPAND = 2
        D_INNER = D_MODEL * EXPAND
        BATCH = 4
        SEQ = 512

        def _silu(v):
            return v * jax.nn.sigmoid(v)
        B, S, _ = x.shape
        xz = x @ W_in.T
        x_ssm, z = jnp.split(xz, 2, axis=-1)
        xc = jnp.transpose(x_ssm, (0, 2, 1))
        xc = jax.lax.conv_general_dilated(xc, conv_w, window_strides=(1,), padding=[(D_CONV - 1, 0)], dimension_numbers=('NCH', 'OIH', 'NCH'), feature_group_count=D_INNER) + conv_b[None, :, None]
        x_conv = _silu(jnp.transpose(xc, (0, 2, 1)))
        p = x_conv @ W_x.T
        Bm = p[..., :D_STATE]
        Cm = p[..., D_STATE:2 * D_STATE]
        dt = jax.nn.softplus(p[..., -1] + jnp.mean(dt_bias))
        A = -jnp.exp(A_log)

        def step(h, inp):
            x_t, B_t, C_t, dt_t = inp
            dts = dt_t[:, None, None]
            A_bar = jnp.exp(A[None] * dts)
            h = A_bar * h + dts * B_t[:, None, :] * x_t[:, :, None]
            y_t = jnp.einsum('bds,bs->bd', h, C_t)
            return (h, y_t)
        h0 = jnp.zeros((B, D_INNER, D_STATE), x.dtype)
        xs = (jnp.swapaxes(x_conv, 0, 1), jnp.swapaxes(Bm, 0, 1), jnp.swapaxes(Cm, 0, 1), dt.T)
        _, ys = jax.lax.scan(step, h0, xs)
        y = jnp.swapaxes(ys, 0, 1) + D[None, None, :] * x_conv
        y = y * _silu(z)
        return y @ out_W.T

    def _L0_ffn_ref(hidden_states, ln1_w, ln2_w, Wq, Wk, Wv, Wo, A, B, W_in_base, W_up_base, W_down):
        import jax, jax.numpy as jnp
        import numpy as np
        B_, S, D = (2, 512, 512)
        F_ = 2048
        R = 16
        H = 16
        HD = D // H
        MOD_SCALE = 0.1
        EPS = 1e-06

        def _rmsnorm(x, w):
            v = jnp.mean(x * x, axis=-1, keepdims=True)
            return x * jax.lax.rsqrt(v + EPS) * w

        def _attention(x, Wq, Wk, Wv, Wo):
            b, s, d = x.shape
            q = (x @ Wq.T).reshape(b, s, H, HD)
            k = (x @ Wk.T).reshape(b, s, H, HD)
            v = (x @ Wv.T).reshape(b, s, H, HD)
            scores = jnp.einsum('bqhd,bkhd->bhqk', q, k) / np.sqrt(HD).astype(np.float32)
            causal = jnp.tril(jnp.ones((s, s), bool))
            scores = jnp.where(causal, scores, jnp.finfo(scores.dtype).min)
            probs = jax.nn.softmax(scores, axis=-1)
            out = jnp.einsum('bhqk,bkhd->bqhd', probs, v).reshape(b, s, d)
            return out @ Wo.T
        residual = hidden_states
        x = _rmsnorm(hidden_states, ln1_w)
        attn = _attention(x, Wq, Wk, Wv, Wo)
        mod = MOD_SCALE * jnp.tanh(attn @ A)
        h = _rmsnorm(residual, ln2_w)
        gate_pre = h @ W_in_base.T + mod * (h @ A) @ B
        gate = jax.nn.silu(gate_pre)
        up = h @ W_up_base.T
        mlp_out = gate * up @ W_down.T
        return residual + mlp_out
    x = L0_attn_x
    xn = _layernorm(x, axis=-1)
    s = _L0_attn_ref(xn, L0_attn_W_in, L0_attn_conv_w, L0_attn_conv_b, L0_attn_W_x, L0_attn_A_log, L0_attn_dt_bias, L0_attn_out_W, L0_attn_D)
    g = _silu(_L0_ffn_ref(xn, L0_ffn_ln1_w, L0_ffn_ln2_w, L0_ffn_Wq, L0_ffn_Wk, L0_ffn_Wv, L0_ffn_Wo, L0_ffn_A, L0_ffn_B, L0_ffn_W_in_base, L0_ffn_W_up_base, L0_ffn_W_down))
    x = x + s * g
    return x

_drawn_inputs = setup_inputs


def setup_inputs(seed=0):
    import zlib

    import numpy as np

    out = dict(_drawn_inputs(seed))
    spreads = {'L0_attn_conv_b': (0.0, 0.1),
     'L0_attn_D': (1.0, 0.2),
     'L0_ffn_ln1_w': (1.0, 0.2),
     'L0_ffn_ln2_w': (1.0, 0.2)}
    factors = {}
    for name, (base, spread) in spreads.items():
        noise = np.random.default_rng([zlib.crc32(name.encode()), seed]).standard_normal(out[name].shape)
        drawn = base * np.exp(spread * noise) if base else spread * noise
        out[name] = jnp.asarray(drawn.astype(out[name].dtype))
    for name, factor in factors.items():
        out[name] = (out[name] * factor).astype(out[name].dtype)
    return out
```

```python
from contextlib import ExitStack

import numpy as np

import concourse.bass as bass
from concourse import mybir

F32 = mybir.dt.float32
F32R = mybir.dt.float32r
BF16 = mybir.dt.bfloat16
F16 = mybir.dt.float16
ALU = mybir.AluOpType
ACT = mybir.ActivationFunctionType
AX = mybir.AxisListType

NB, S, DM, DI, NS, FF, NH, HD, R = 8, 512, 512, 1024, 16, 2048, 16, 32, 16
T = NB * S
NEG = -1.0e30


class Queue:

    def __init__(self, sem):
        self.sem, self.ops = sem, []

    def add(self, fn, waits):
        tok = Token(self, len(self.ops))
        for w in waits:
            w.wanted()
        self.ops.append([fn, waits, False, None])
        return tok

    def count(self):
        n = 0
        for op in self.ops:
            n += op[2]
            op[3] = n

    def emit(self, eng):
        seen = {}
        for fn, waits, marked, _ in self.ops:
            for w in waits:
                sem, value = w.value()
                if seen.get(id(sem), 0) < value:
                    eng.wait_ge(sem, value)
                    seen[id(sem)] = value
            ins = fn(eng)
            if marked:
                ins.then_inc(self.sem, 1)


class Token:
    def __init__(self, queue, at):
        self.queue, self.at = queue, at

    def wanted(self):
        self.queue.ops[self.at][2] = True

    def value(self):
        return self.queue.sem, self.queue.ops[self.at][3]


class Landed:

    def __init__(self, sem, n):
        self.sem, self.n = sem, n

    def wanted(self):
        pass

    def value(self):
        return self.sem, self.n


class Sem:
    def __init__(self, handle):
        self.handle, self.n = handle, 0


def build(nc, x, WinT, convw, convb, WxT, Alog, dtb, outWT, Dp, ln1, ln2, WqT, WkT, Wv, Wo, Aw, Bw, WgT, WuT, WdT,
          ident, umask, arow, maskt, maskT, out):
    ctx = ExitStack()
    with ctx:
        def sem(name):
            return ctx.enter_context(nc.semaphore(name))

        class Part:

            def __init__(self, name):
                self.pe, self.act, self.dve, self.pool, self.sp = (
                    Queue(sem(f"{name}_{n}")) for n in ("pe", "act", "dve", "pool", "sp"))

            def queues(self):
                return [self.pe, self.act, self.dve, self.pool, self.sp]

        now = [None]

        def part(name):
            now[0] = Part(name)
            for i in range(8):
                free[i] = []
            turn.clear()
            return now[0]

        def dma(s, dst, src, *waits):
            dst, src = (v.bitcast(F32) if v.dtype == F32R else v for v in (dst, src))
            s.n += 16
            n = s.n

            def go(e):
                e.dma_start(dst, src).then_inc(s.handle, 16)
            for w in waits:
                w.wanted()
            now[0].sp.ops.append([go, list(waits), False, None])
            return Landed(s.handle, n)

        def mm(o, l, r, a, z, *waits):
            return now[0].pe.add(lambda e: e.matmul(o, l, r, start=a, stop=z, skip_group_check=True), list(waits))

        def tr(o, i, idt, *waits):
            return now[0].pe.add(lambda e: e.transpose(o, i, idt), list(waits))

        def activate(o, i, f, *waits, bias=0.0, scale=1.0):
            return now[0].act.add(lambda e: e.activation(o, i, f, bias=bias, scale=scale), list(waits))

        def acopy(o, i, *waits):
            return now[0].act.add(lambda e: e.copy(o, i), list(waits))

        def tt(o, a, b, op, *waits, q=None):
            return (q or now[0].dve).add(lambda e: e.tensor_tensor(o, a, b, op), list(waits))

        def ts(o, a, s1, s2, op0, op1, *waits, q=None):
            if s2 is None:
                return (q or now[0].dve).add(lambda e: e.tensor_scalar(o, a, s1, None, op0), list(waits))
            return (q or now[0].dve).add(lambda e: e.tensor_scalar(o, a, s1, s2, op0, op1), list(waits))

        def stt(o, a, s, b, op0, op1, *waits):
            return now[0].dve.add(lambda e: e.scalar_tensor_tensor(out=o, in0=a, scalar=s, in1=b, op0=op0, op1=op1), list(waits))

        def vcopy(o, i, *waits, q=None):
            return (q or now[0].dve).add(lambda e: e.tensor_copy(o, i), list(waits))

        def total(o, i, op, axis, *waits):
            return now[0].dve.add(lambda e: e.tensor_reduce(o, i, axis, op), list(waits))

        def scan(o, a, b, *waits):
            return now[0].dve.add(lambda e: e.tensor_tensor_scan(o, a, b, 0.0, ALU.mult, ALU.add), list(waits))

        def fill(o, v, *waits, q=None):
            o = o.bitcast(F32) if o.dtype == F32R else o
            return (q or now[0].dve).add(lambda e: e.memset(o, v), list(waits))

        def sbp(c, name, shape, dt):
            return c.enter_context(nc.sbuf_tensor(name, shape, dt))

        PS = [ctx.enter_context(nc.psum_tensor(f"PS{i}", [128, 512], F32)) for i in range(8)]
        free = [[] for _ in range(8)]
        turn = {}

        def bank(group):
            k = turn.get(group, 0)
            turn[group] = k + 1
            i = group[k % len(group)]
            return i, PS[i], free[i]

        def drains(i, *toks):
            free[i] = list(toks)

        rh_d = nc.dram_tensor("rh_scratch", [NB, 128, 4, S], F32R, kind="Internal").ap()
        rl_d = nc.dram_tensor("rl_scratch", [NB, 128, 4, S], F32R, kind="Internal").ap()
        s_d = nc.dram_tensor("s_scratch", [T, DM], F32, kind="Internal").ap()
        m_d = nc.dram_tensor("m_scratch", [T, DM], F32, kind="Internal").ap()

        idn = sbp(ctx, "idn", [128, 128], F32)
        idr = sbp(ctx, "idr", [128, 128], F32R)
        UM = sbp(ctx, "UM", [128, 2, 128], F32)
        MEAN = sbp(ctx, "MEAN", [128, 32], F32)
        RSTD = sbp(ctx, "RSTD", [128, 32], F32)
        RMS = sbp(ctx, "RMS", [128, 32], F32)
        FLAG = sbp(ctx, "FLAG", [1, 1], mybir.dt.int32)
        joined = sem("joined")
        s_c = Sem(sem("s_c"))
        MHALF = sbp(ctx, "MHALF", [128, 4], F32)

        first = part("first")
        p0 = ExitStack()
        AL = sbp(p0, "AL", [128, 8, NS], F32)
        AR = sbp(p0, "AR", [128, NS], F32)
        NE = sbp(p0, "NE", [128, 2], F32)
        dma(s_c, idn[:, :], ident)
        dma(s_c, UM[:, :, :], umask)
        dma(s_c, AL[:, :, :], Alog.rearrange("(k p) j -> p k j", p=128))
        ld = dma(s_c, AR[:, :], Alog[0:1, :].to_broadcast([128, NS]))
        t_idr = vcopy(idr[:, :], idn[:, :], ld)
        t_mh = fill(MHALF[:, :], -0.5)
        v1 = fill(NE[:, 1:2], 1.0)
        v = tt(AL[:, :, :], AL[:, :, :], AR[:, :].unsqueeze(1).to_broadcast([128, 8, NS]), ALU.not_equal, ld)
        v = total(NE[:, 0:1], AL[:, :, :], ALU.max, AX.XY, v)
        t = mm(PS[0][0:1, 0:1], NE[:, 0:1], NE[:, 1:2], True, True, v, v1)
        t_flag = vcopy(FLAG[:, :], PS[0][0:1, 0:1], t)
        t_flag.wanted()
        p0.close()
        consts = [t_idr, t_mh, t_flag, ld]

        class Stage:

            def __init__(self, slots, name):
                self.slots, self.n = slots, 0
                self.sems = [Sem(sem(f"{name}{i}")) for i in range(len(slots))]
                self.free = [[] for _ in slots]

            def load(self, src, n, *waits):
                i = self.n % len(self.slots)
                self.n += 1
                dst = self.slots[i][:, 0:n]
                if len(src.shape) == 3:
                    dst = dst.rearrange("p (k m) -> p k m", k=src.shape[1])
                return i, dma(self.sems[i], dst, src, *self.free[i], *waits)

        def split(hi, lo, w, *waits, q=None):
            a = acopy(hi, w, *waits)
            return [a, tt(lo, w, hi.bitcast(F32), ALU.subtract, a, q=q)]

        def split_weights(stage, src, n, hi, lo, *waits):
            i, d = stage.load(src, n, *waits)
            stage.free[i] = split(hi, lo, stage.slots[i][:, 0:n], d)
            return stage.free[i]

        def three(pt, lh, ll, xh, xl, nk, waits, close=True):
            n, first = 3 * nk, True
            t = None
            for k in range(nk):
                for a, b in ((lh, xh), (lh, xl), (ll, xh)):
                    n -= 1
                    t = mm(pt, a(k), b(k), first, close and n == 0, *(waits if first else []))
                    first = False
            return t

        def stats(X, k, n, BST, AGG, VT, *waits):
            v = now[0].dve.add(lambda e: e.bn_stats(BST[:, :], X), list(waits))
            v = now[0].dve.add(lambda e: e.bn_aggr(AGG[:, :], BST[:, :]), [v])
            t1 = vcopy(MEAN[:, n:n + 1], AGG[:, 0:1], v)
            t2 = ts(VT[:, 0:1], AGG[:, 1:2], 1e-5, None, ALU.add, None, v)
            pool = now[0].pool
            t3 = tt(RSTD[:, n:n + 1], VT[:, 0:1], MHALF[:, 0:1], ALU.pow, t2, *consts, q=pool)
            t4 = tt(VT[:, 1:2], RSTD[:, n:n + 1], RSTD[:, n:n + 1], ALU.mult, t3)
            t4 = stt(VT[:, 2:3], VT[:, 1:2], AGG[:, 1:2], VT[:, 3:4], ALU.mult, ALU.add, t4)
            t5 = tt(VT[:, 1:2], VT[:, 2:3], MHALF[:, 0:1], ALU.pow, t4, q=pool)
            t6 = tt(RMS[:, n:n + 1], VT[:, 1:2], RSTD[:, n:n + 1], ALU.mult, t5)
            return [t1, t3], t6

        general = part("gen")
        p1 = ExitStack()
        WH = sbp(p1, "g_WH", [128, 4, 2048], F32R)
        WL = sbp(p1, "g_WL", [128, 4, 2048], F32R)
        OH = sbp(p1, "g_OH", [128, 8, 512], F32R)
        OL = sbp(p1, "g_OL", [128, 8, 512], F32R)
        XPH = sbp(p1, "g_XPH", [128, 8, 66], F32R)
        XPL = sbp(p1, "g_XPL", [128, 8, 66], F32R)
        XH = sbp(p1, "g_XH", [128, 4, S], F32R)
        XL = sbp(p1, "g_XL", [128, 4, S], F32R)
        CH = sbp(p1, "g_CH", [128, 8, S], F32R)
        CL = sbp(p1, "g_CL", [128, 8, S], F32R)
        stage = Stage([sbp(p1, f"g_STG{i}", [128, 2048], F32) for i in range(2)], "g_st")
        STG = stage.slots
        XC = sbp(p1, "g_XC", [128, 8, S], F32)
        ZS = sbp(p1, "g_ZS", [128, 8, S], F32)
        DT = sbp(p1, "g_DT", [128, S], F32)
        AB = sbp(p1, "g_AB", [128, S], F32)
        U = sbp(p1, "g_U", [128, S], F32)
        ACC = sbp(p1, "g_ACC", [128, S], F32)
        PPH = sbp(p1, "g_PPH", [65, S], F32R)
        PPL = sbp(p1, "g_PPL", [65, S], F32R)
        CW = sbp(p1, "g_CW", [128, 8, 4], F32)
        CB = sbp(p1, "g_CB", [128, 8], F32)
        AC = sbp(p1, "g_AC", [128, 8, NS], F32)
        DC = sbp(p1, "g_DC", [128, 8], F32)
        DB = sbp(p1, "g_DB", [128, 8], F32)
        ONE = sbp(p1, "g_ONE", [128, 128], F32)
        MB = sbp(p1, "g_MB", [128, 2], F32)
        BST = sbp(p1, "g_BST", [128, 6], F32)
        AGG = sbp(p1, "g_AGG", [128, 2], F32)
        VT = sbp(p1, "g_VT", [128, 4], F32)

        s_w = Sem(sem("g_w"))
        lw = [dma(s_w, CW[:, :, :], convw.rearrange("(k p) j -> p k j", p=128)),
              dma(s_w, CB[:, :], convb),
              dma(s_w, AC[:, :, :], Alog.rearrange("(k p) j -> p k j", p=128)),
              dma(s_w, DC[:, :], Dp),
              dma(s_w, DB[:, :], dtb)][-1]

        t_w = []
        wv_ = WinT.rearrange("(k p) n -> p k n", p=128)
        for k in range(4):
            t_w += split_weights(stage, wv_[:, k, :], 2048, WH[:, k, :], WL[:, k, :])
        t_o = []
        ov_ = outWT.rearrange("(k p) n -> p k n", p=128)
        for k in range(2):
            t_o += split_weights(stage, ov_[:, 4 * k:4 * k + 4, :], 2048,
                                 OH[:, 4 * k:4 * k + 4, :].rearrange("p k n -> p (k n)"),
                                 OL[:, 4 * k:4 * k + 4, :].rearrange("p k n -> p (k n)"))
        t_p = split_weights(stage, WxT.rearrange("(k p) n -> p k n", p=128), 8 * 66,
                            XPH[:, :, :].rearrange("p k n -> p (k n)"), XPL[:, :, :].rearrange("p k n -> p (k n)"))
        e0 = activate(AC[:, :, :], AC[:, :, :], ACT.Exp, lw)
        t_ac = ts(AC[:, :, :], AC[:, :, :], -1.0, None, ALU.mult, None, e0)
        t_one = fill(ONE[:, :], 1.0 / DI)
        t_vt = fill(VT[:, 3:4], 1e-6)
        r0 = total(MB[:, 0:1], DB[:, :], ALU.add, AX.X, lw)
        i, p, w0 = bank((0, 1))
        m0 = mm(p[:, 0:1], ONE[:, :], MB[:, 0:1], True, True, r0, t_one, *w0)
        t_mb = vcopy(MB[:, 1:2], p[:, 0:1], m0)
        drains(i, t_mb)

        xv = x.rearrange("(b k p) d -> b p k d", k=4, p=128)
        G_T, G_W, G_B, G_O = (0, 1), (2, 3, 4), (5, 6), (7,)
        done_xh, done_c, done_y, done_xc, done_zs, done_pp, done_dt = [], [[] for _ in range(8)], [], [], [], [], []
        acc_free, h_free = [], []
        for b in range(NB):
            sl, dx = stage.load(xv[b], 2048)
            X = STG[sl][:, :].rearrange("p (k d) -> p k d", k=4)
            xn, t6 = [], t_vt
            for k in range(4):
                n = 4 * b + k
                two, t6 = stats(X[:, k, :], k, n, BST, AGG, VT, dx, t6)
                xn.append(ts(X[:, k, :], X[:, k, :], MEAN[:, n:n + 1], RSTD[:, n:n + 1], ALU.subtract, ALU.mult, *two))
            xs = []
            for d in range(4):
                i, p, w = bank(G_T)
                for k in range(4):
                    t = tr(p[:, 128 * k:128 * k + 128], X[:, k, 128 * d:128 * d + 128], idn[:, :], xn[k], *consts, *w)
                a = acopy(XH[:, d, :], p[:, :], t, *done_xh)
                v = tt(XL[:, d, :], p[:, :], XH[:, d, :].bitcast(F32), ALU.subtract, a)
                drains(i, v)
                xs += [a, v]
            x_free = [t]
            done_xh = []
            cs = []
            for m in range(16):
                i, p, w = bank(G_W)
                t = three(p[:, :], lambda k: WH[:, k, 128 * m:128 * m + 128], lambda k: WL[:, k, 128 * m:128 * m + 128],
                          lambda k: XH[:, k, :], lambda k: XL[:, k, :], 4, [*w, *xs, *t_w])
                if m < 8:
                    y = XC[:, m, :]
                    a = activate(y, p[:, :], ACT.Identity, t, lw, *done_xc, bias=CB[:, m:m + 1], scale=CW[:, m, 3:4])
                    for j in range(1, 4):
                        a = stt(y[:, j:], p[:, 0:S - j], CW[:, m, 3 - j:4 - j], y[:, j:], ALU.mult, ALU.add, a)
                    drains(i, a)
                    a = activate(y, y, ACT.Silu, a)
                    h = acopy(CH[:, m, :], y, a, *done_c[m])
                    l = tt(CL[:, m, :], y, CH[:, m, :].bitcast(F32), ALU.subtract, h)
                    cs += [h, l]
                else:
                    a = activate(ZS[:, m - 8, :], p[:, :], ACT.Silu, t, *done_zs)
                    drains(i, a)
                    zs = a
            done_xh = [t]
            i, p, w = bank(G_T)
            t = three(p[0:65, :], lambda k: XPH[:, k, 0:65], lambda k: XPL[:, k, 0:65],
                      lambda k: CH[:, k, :], lambda k: CL[:, k, :], 8, [*w, *cs, *t_p])
            pp = split(PPH[:, :], PPL[:, :], p[0:65, :], t, *done_pp)
            drains(i, pp[1])

            def spread(p, q, *waits):
                one = idr[0:65, q:q + 1].to_broadcast([65, 128])
                mm(p[:, :], one, PPH[:, :], True, False, *pp, *consts, *waits)
                return mm(p[:, :], one, PPL[:, :], False, True)

            i, p, w = bank(G_T)
            t = spread(p, 64, *w)
            a0 = activate(U[:, :], p[:, :], ACT.Abs, t, t_mb, *h_free, bias=MB[:, 1:2])
            r = activate(DT[:, :], p[:, :], ACT.Relu, t, *done_dt, bias=MB[:, 1:2])
            drains(i, r)
            a0 = activate(U[:, :], U[:, :], ACT.Exp, a0, scale=-1.0)
            v = ts(ACC[:, :], U[:, :], 1.0, None, ALU.add, None, a0, *acc_free)
            lnu = activate(AB[:, :], ACC[:, :], ACT.Ln, v)
            v = ts(ACC[:, :], ACC[:, :], -1.0, None, ALU.add, None, v, lnu)
            v = tt(U[:, :], U[:, :], ACC[:, :], ALU.subtract, v)
            v = tt(U[:, :], U[:, :], AB[:, :], ALU.add, v, lnu)
            dtk = tt(DT[:, :], DT[:, :], U[:, :], ALU.add, v, r)
            ab_free = [dtk]
            ys = []
            for d in range(8):
                X1 = XC[:, d, :]
                v = ts(ACC[:, :], X1, DC[:, d:d + 1], None, ALU.mult, None, lw, *acc_free, cs[-1], cs[2 * d])
                v = tt(X1, X1, DT[:, :], ALU.mult, v, dtk, cs[2 * d], cs[2 * d + 1])
                for s in range(NS):
                    ib, pb, wb = bank((5, 6))
                    tb = spread(pb, s, *wb)
                    ic, pc, wc = bank((2, 3))
                    tc = spread(pc, 32 + s, *wc)
                    ea = activate(AB[:, :], DT[:, :], ACT.Exp, dtk, t_ac, *ab_free, scale=AC[:, d, s:s + 1])
                    v = tt(U[:, :], X1, pb[:, :], ALU.mult, tb, v)
                    drains(ib, v)
                    v = scan(AB[:, :], AB[:, :], U[:, :], ea, v)
                    v = tt(AB[:, :], AB[:, :], pc[:, :], ALU.mult, v, tc)
                    drains(ic, v)
                    v = tt(ACC[:, :], ACC[:, :], AB[:, :], ALU.add, v)
                    ab_free = [v]
                v = tt(ACC[:, :], ACC[:, :], ZS[:, d, :], ALU.mult, v, zs)
                a = acopy(CH[:, d, :], ACC[:, :], v, t)
                l = tt(CL[:, d, :], ACC[:, :], CH[:, d, :].bitcast(F32), ALU.subtract, a)
                acc_free = [l, a]
                ys += [a, l]
            done_xc, done_zs, done_dt, done_pp, h_free = [v], [v], [v, ea], [tc], [l]
            so = []
            for k in range(4):
                i, p, w = bank(G_O)
                t = three(p[:, :], lambda q: CH[:, q, 128 * k:128 * k + 128], lambda q: CL[:, q, 128 * k:128 * k + 128],
                          lambda q: OH[:, q, :], lambda q: OL[:, q, :], 8, [*w, *ys, *t_o])
                a = acopy(X[:, k, :], p[:, :], t, *x_free)
                drains(i, a)
                so.append(a)
            for m in range(8):
                done_c[m] = [t]
            ds = dma(stage.sems[sl], s_d.rearrange("(b k p) d -> b p k d", k=4, p=128)[b], X, *so)
            stage.free[sl] = [ds]
        g_ends = [Landed(q.handle, q.n) for q in stage.sems]
        for q in general.queues()[:4]:
            q.ops[-1][2] = True
        p1.close()

        fast = part("fast")
        p1 = ExitStack()
        WH = sbp(p1, "WH", [128, 4, 2048], F32R)
        WL = sbp(p1, "WL", [128, 4, 2048], F32R)
        OH = sbp(p1, "OH", [128, 8, 512], F32R)
        OL = sbp(p1, "OL", [128, 8, 512], F32R)
        XPH = sbp(p1, "XPH", [128, 8, 66], F32R)
        XPL = sbp(p1, "XPL", [128, 8, 66], F32R)
        XH = sbp(p1, "XH", [128, 4, S], F32R)
        XL = sbp(p1, "XL", [128, 4, S], F32R)
        XC = sbp(p1, "XC", [128, 8, S], F32)
        ZS = sbp(p1, "ZS", [128, 8, S], F32)
        CW = sbp(p1, "CW", [128, 8, 4], F32)
        CB = sbp(p1, "CB", [128, 8], F32)
        DC = sbp(p1, "DC", [128, 8], F32)
        DB = sbp(p1, "DB", [128, 8], F32)
        AB_ = sbp(p1, "AB_", [128, NS], F32)
        A16 = sbp(p1, "A16", [NS, 1], F32)
        ONE = sbp(p1, "ONE", [128, 128], F32)
        ONE2 = sbp(p1, "ONE2", [NS, 384], F32)
        MB = sbp(p1, "MB", [128, 2], F32)
        BST = sbp(p1, "BST", [128, 6], F32)
        AGG = sbp(p1, "AGG", [128, 2], F32)
        VT = sbp(p1, "VT", [128, 4], F32)

        pw = ExitStack()
        wst = Stage([sbp(pw, f"WST{i}", [128, 2048], F32) for i in range(3)], "f_ws")
        s_w = Sem(sem("f_w"))
        dma(s_w, CW[:, :, :], convw.rearrange("(k p) j -> p k j", p=128))
        dma(s_w, CB[:, :], convb)
        dma(s_w, AB_[:, :], Alog[0:1, :].to_broadcast([128, NS]))
        dma(s_w, A16[:, :], arow)
        dma(s_w, DC[:, :], Dp)
        lw = dma(s_w, DB[:, :], dtb)
        t_w = []
        wv_ = WinT.rearrange("(k p) n -> p k n", p=128)
        for k in range(4):
            t_w += split_weights(wst, wv_[:, k, :], 2048, WH[:, k, :], WL[:, k, :])
        t_p = split_weights(wst, WxT.rearrange("(k p) n -> p k n", p=128), 8 * 66,
                            XPH[:, :, :].rearrange("p k n -> p (k n)"), XPL[:, :, :].rearrange("p k n -> p (k n)"))
        t_o = []
        ov_ = outWT.rearrange("(k p) n -> p k n", p=128)
        for k in range(2):
            t_o += split_weights(wst, ov_[:, 4 * k:4 * k + 4, :], 2048,
                                 OH[:, 4 * k:4 * k + 4, :].rearrange("p k n -> p (k n)"),
                                 OL[:, 4 * k:4 * k + 4, :].rearrange("p k n -> p (k n)"))
        laid = t_w + t_p + t_o
        pw.close()
        XT = Stage([sbp(p1, f"XF{i}", [128, DM], F32) for i in range(2)], "f_x")
        XT.free = [list(laid), list(laid)]
        CH = [sbp(p1, f"CH{i}", [128, S], F32R) for i in range(2)]
        CL = [sbp(p1, f"CL{i}", [128, S], F32R) for i in range(2)]
        YH = [sbp(p1, f"YH{i}", [128, S], F32R) for i in range(2)]
        YL = [sbp(p1, f"YL{i}", [128, S], F32R) for i in range(2)]
        NH_ = [sbp(p1, f"NH_{i}", [128, 4, 128], F32R) for i in range(2)]
        NL_ = [sbp(p1, f"NL_{i}", [128, 4, 128], F32R) for i in range(2)]
        TMP = sbp(p1, "TMP", [128, 2048], F32)
        DT = sbp(p1, "DT", [128, S], F32)
        DEL = sbp(p1, "DEL", [128, S], F32)
        MH = sbp(p1, "MH", [128, 4, S], F32R)
        ML = sbp(p1, "ML", [128, 4, S], F32R)
        PPH = sbp(p1, "PPH", [65, S], F32R)
        PPL = sbp(p1, "PPL", [65, S], F32R)
        CS = sbp(p1, "CS", [80, 768], F32R)
        BT = sbp(p1, "BT", [80, 384], F32R)
        BN = sbp(p1, "BN", [128, 3, NS], F32)
        PN = sbp(p1, "PN", [128, 4, 65], F32)
        DBN = sbp(p1, "DBN", [128, 4, NS], F32)
        KEEP = sbp(p1, "KEEP", [128, S], F32)
        G = [TMP[:, 0:512], TMP[:, 512:1024]]
        ACC, PF = TMP[:, 1024:1536], TMP[0:65, 1536:2048]
        CE, CF = TMP[0:NS, 0:768], TMP[0:NS, 1024:1536]
        jo = [0, 384, 640, 768]

        e0 = activate(AB_[:, :], AB_[:, :], ACT.Exp, lw)
        t_ab = ts(AB_[:, :], AB_[:, :], -1.0, None, ALU.mult, None, e0)
        e0 = activate(A16[:, :], A16[:, :], ACT.Exp, lw)
        t_a16 = ts(A16[:, :], A16[:, :], -1.0, None, ALU.mult, None, e0)
        t_one = fill(ONE[:, :], 1.0 / DI)
        t_one2 = fill(ONE2[:, :], 1.0)
        t_vt = fill(VT[:, 3:4], 1e-6)
        v = fill(KEEP[:, :], 1.0, *laid)
        t_keep = fill(KEEP[:, :].rearrange("p (c t) -> p c t", c=4)[:, :, 0], 0.0, v)
        t_z = [fill(CS[:, :], 0.0, *laid), fill(BT[:, :], 0.0, *laid)]
        r0 = total(MB[:, 0:1], DB[:, :], ALU.add, AX.X, lw)
        i, p, w0 = bank((0,))
        m0 = mm(p[:, 0:1], ONE[:, :], MB[:, 0:1], True, True, r0, t_one, *w0)
        t_mb = vcopy(MB[:, 1:2], p[:, 0:1], m0)
        drains(i, t_mb)
        xt_ = x.rearrange("(n p) d -> n p d", p=128)
        so_ = s_d.rearrange("(b k p) d -> b p k d", k=4, p=128)
        s_so = Sem(sem("s_so"))

        tmp_free = list(laid)
        xh_free, xh_done = [], [None] * 4
        ch_free, yh_free, nh_free = [[*laid], [*laid]], [[*laid], [*laid]], [[*laid], [*laid]]
        xc_free, zs_free = [[] for _ in range(8)], [[] for _ in range(8)]
        m_free, dt_free, del_free, pp_free, cs_free, bt_free, bn_free, pn_free = ([*laid] for _ in range(8))
        t6 = t_vt
        p_bank = [None]

        def normed(b, k):
            nonlocal t6
            n = 4 * b + k
            u, d = XT.load(xt_[n], DM)
            X = XT.slots[u][:, :]
            two, t6 = stats(X, k, n, BST, AGG, VT, d, t6)
            xn = ts(X, X, MEAN[:, n:n + 1], RSTD[:, n:n + 1], ALU.subtract, ALU.mult, *two)
            i, p, w = bank((4,))
            for d in range(4):
                t = tr(p[:, 128 * d:128 * d + 128], X[:, 128 * d:128 * d + 128], idn[:, :], xn, *consts, *w)
            XT.free[u] = [t]
            c = slice(128 * k, 128 * k + 128)
            p3 = p[:, :].rearrange("p (d t) -> p d t", d=4)
            xh_done[k] = split(XH[:, :, c], XL[:, :, c], p3, t, *xh_free)
            drains(i, xh_done[k][1])

        def project(m, group):
            c = slice(128 * m, 128 * m + 128)
            i, p, w = bank(group)
            t = three(p[:, :], lambda k: WH[:, k, c], lambda k: WL[:, k, c], lambda k: XH[:, k, :], lambda k: XL[:, k, :], 4,
                      [*w, *sum(xh_done, []), *t_w])
            return i, p, t

        def conv(d, i, p, t):
            y, u = XC[:, d, :], d % 2
            a = activate(y, p[:, :], ACT.Identity, t, lw, *xc_free[d], bias=CB[:, d:d + 1], scale=CW[:, d, 3:4])
            for j in range(1, 4):
                a = stt(y[:, j:], p[:, 0:S - j], CW[:, d, 3 - j:4 - j], y[:, j:], ALU.mult, ALU.add, a)
            drains(i, a)
            a = activate(y, y, ACT.Silu, a)
            return a, split(CH[u][:, :], CL[u][:, :], y, a, *ch_free[u])

        def rows(d, cs):
            u = d % 2
            if d == 0:
                p_bank[0] = bank((5,))
            i, p, w = p_bank[0]
            for n, (l_, r_) in enumerate(((XPH, CH), (XPH, CL), (XPL, CH))):
                t = mm(p[0:65, :], l_[:, d, 0:65], r_[u][:, :], d == 0 and n == 0, d == 7 and n == 2, *cs, *t_p, *w)
            ch_free[u] = [t]
            return t

        for k in range(4):
            normed(0, k)
        xcs = [None] * 8
        lag = None
        for d in range(8):
            xcs[d], cs = conv(d, *project(d, (0, 1)))
            if lag is not None:
                rows(*lag)
            lag = (d, cs)
        t_rows = rows(*lag)

        for b in range(NB):
            ib, pb, _ = p_bank[0]
            t_pf = acopy(PF, pb[0:65, :], t_rows, *tmp_free)
            pp = split(PPH[:, :], PPL[:, :], pb[0:65, :], t_rows, *pp_free)
            drains(ib, pp[1])

            def spread(p, q, *waits):
                one = idr[0:65, q:q + 1].to_broadcast([65, 128])
                mm(p[:, :], one, PPH[:, :], True, False, *pp, *consts, *waits)
                return mm(p[:, :], one, PPL[:, :], False, True)

            def gate(m):
                i, p, t = project(8 + m, (0, 1))
                zs_done[m] = activate(ZS[:, m, :], p[:, :], ACT.Silu, t, *zs_free[m])
                drains(i, zs_done[m])
                return t

            zs_done = [None] * 8
            gate(0)
            i, p, w = bank((4,))
            t = spread(p, 64, *w)
            gate(1)
            gate(2)
            e = activate(G[0], p[:, :], ACT.Abs, t, t_mb, *tmp_free, bias=MB[:, 1:2])
            r = activate(DT[:, :], p[:, :], ACT.Relu, t, *dt_free, bias=MB[:, 1:2])
            drains(i, r)
            e = activate(G[0], G[0], ACT.Exp, e, scale=-1.0)
            v = ts(G[1], G[0], 1.0, None, ALU.add, None, e, *tmp_free)
            ln = activate(ACC, G[1], ACT.Ln, v, *tmp_free)
            v = ts(G[1], G[1], -1.0, None, ALU.add, None, v, ln)
            v = tt(G[0], G[0], G[1], ALU.subtract, v)
            v = tt(DT[:, :], DT[:, :], G[0], ALU.add, v, r)
            t_dt = tt(DT[:, :], DT[:, :], ACC, ALU.add, v, ln)
            v = tt(DEL[:, :].rearrange("p (c t) -> p c t", c=4), DT[:, :].rearrange("p (c t) -> p c t", c=4),
                   UM[:, 0, :].unsqueeze(1).to_broadcast([128, 4, 128]), ALU.mult, t_dt, *consts, *del_free)
            t_del = scan(DEL[:, :], KEEP[:, :], DEL[:, :], v, t_keep)
            v = vcopy(PF[64:65, :], DT[64:65, :], t_dt, t_pf)
            i, p, w = bank((4,))
            for k in range(4):
                t = tr(p[:, 65 * k:65 * k + 65], PF[:, 128 * k:128 * k + 128], idn[0:65, 0:65], v, *w)
            a = acopy(PN[:, :, :], p[:, 0:260].rearrange("p (k q) -> p k q", k=4), t, *pn_free)
            drains(i, a)
            for k in range(4):
                dbn = ts(DBN[:, k, :], PN[:, k, 0:NS], PN[:, k, 64:65], None, ALU.mult, None, a, *pn_free)
            bn = []
            for J in range(3):
                c = activate(BN[:, J, :], AB_[:, :], ACT.Exp, t_del, t_ab, *bn_free, scale=DEL[:, 128 * J + 127:128 * J + 128])
                bn.append(c)
            v = tt(BN[:, :, :], BN[:, :, :], DBN[:, 0:3, :], ALU.mult, c, dbn)
            i, p, w = bank((4,))
            for J in range(3):
                t = tr(p[0:NS, 128 * J:128 * J + 128], BN[:, J, :], idn[:, :], v, *w)
            bn_free = [t]
            bt = [acopy(BT[64:64 + NS, :], p[0:NS, 0:384], t, *bt_free, *t_z)]
            bt += split(BT[0:NS, :], BT[32:32 + NS, :], p[0:NS, 0:384])
            drains(i, bt[-1])
            dj = []
            for J in range(3):
                n = 384 - 128 * J
                dj.append(scan(CE[:, jo[J]:jo[J + 1]], ONE2[0:NS, 0:n], DT[0:NS, 512 - n:512], t_dt, t_one2, v))
            t_cf = acopy(CF, PF[32:32 + NS, :], t_pf, t_dt)
            c = activate(CE, CE, ACT.Exp, dj[-1], t_a16, scale=A16[:, 0:1])
            for J in range(3):
                n = 384 - 128 * J
                v = tt(CE[:, jo[J]:jo[J + 1]], CE[:, jo[J]:jo[J + 1]], CF[:, 512 - n:512], ALU.mult, c, t_cf)
            cs = [acopy(CS[0:NS, :], CE, v, *cs_free, *t_z), acopy(CS[32:32 + NS, :], CE)]
            cs.append(tt(CS[64:64 + NS, :], CE, CS[0:NS, :].bitcast(F32), ALU.subtract, cs[0]))
            t_tmp = cs
            spans = [(bank((6,)), 0), (bank((7,)), 0), None]
            spans[2] = (spans[1][0], 256)
            off_ = []
            for J in range(3):
                (i, p, w), at = spans[J]
                n = 384 - 128 * J
                t = mm(p[:, at:at + n], BT[:, 128 * J:128 * J + 128], CS[:, jo[J]:jo[J + 1]], True, True, *bt, *cs, *w)
            for J in range(3):
                (i, p, w), at = spans[J]
                n = 384 - 128 * J
                mo = split(MH[:, J, 128:128 + n], ML[:, J, 128:128 + n], p[:, at:at + n], t, *m_free, *off_[-1:])
                drains(i, mo[1])
                off_ += mo
            bt_free = cs_free = [t]
            g_free = [[*t_tmp], [*t_tmp]]
            v = None
            for s in range(NS):
                u = s % 2
                i, p, w = bank((2, 3))
                t = spread(p, 32 + s, *w)
                a = activate(G[u], DEL[:, :], ACT.Exp, t_del, t_ab, *g_free[u], scale=AB_[:, s:s + 1])
                g = tt(G[u], G[u], p[:, :], ALU.mult, a, t)
                drains(i, g)
                for k in range(4):
                    c = slice(128 * k, 128 * k + 128)
                    if s == 0:
                        v = ts(ACC[:, c], G[u][:, c], DBN[:, k, s:s + 1], None, ALU.mult, None, g, dbn, *t_tmp)
                    else:
                        v = stt(ACC[:, c], G[u][:, c], DBN[:, k, s:s + 1], ACC[:, c], ALU.mult, ALU.add, g, v)
                g_free[u] = [v]
                if 1 <= s <= 5:
                    xh_free = [gate(2 + s)]
                elif s >= 8 and s % 2 == 0 and b + 1 < NB:
                    normed(b + 1, (s - 8) // 2)
            pp_free, del_free, dt_free, pn_free = [t], [a], [dj[-1], v], [v]
            A3 = ACC.rearrange("p (c t) -> p c t", c=4)
            v = tt(A3, A3, UM[:, 1, :].unsqueeze(1).to_broadcast([128, 4, 128]), ALU.mult, v)
            md = split(MH[:, :, 0:128], ML[:, :, 0:128], A3, v, *m_free)
            t_m = off_ + md
            tmp_free = [*md]
            outs = [bank((g,)) for g in (2, 3, 6, 7)]

            def turned(d):
                u = d % 2
                i, p, w = bank((4,))
                for k in range(4):
                    t = tr(p[:, 128 * k:128 * k + 128], XC[:, d, 128 * k:128 * k + 128], idn[:, :], xcs[d], *w)
                p3 = p[:, :].rearrange("p (k d) -> p k d", k=4)
                r = split(NH_[u][:, :, :], NL_[u][:, :, :], p3, t, *nh_free[u])
                drains(i, r[1])
                return t, r

            def project_out(d, ys):
                u = d % 2
                for k in range(4):
                    i, p, w = outs[k]
                    c = slice(128 * k, 128 * k + 128)
                    for n, (l_, r_) in enumerate(((YH, OH), (YH, OL), (YL, OH))):
                        t = mm(p[:, :], l_[u][:, c], r_[:, d, :], d == 0 and n == 0, d == 7 and n == 2, *ys, *t_o,
                               *(w if d == 0 else []))
                yh_free[u] = [t]
                return t

            nx = turned(0)
            lag_o = lag_r = None
            for d in range(8):
                u = d % 2
                t_x, xn_ = nx
                i, p, w = bank((1,))
                n = 0
                for J in range(4):
                    for l_, r_ in ((NH_, MH), (NH_, ML), (NL_, MH)):
                        n += 1
                        t = mm(p[:, 128 * J:512], l_[u][:, J, :], r_[:, J, 0:512 - 128 * J], n == 1, n == 12, *xn_, *t_m, *w)
                nh_free[u] = [t]
                X1 = XC[:, d, :]
                v = stt(X1, X1, DC[:, d:d + 1], p[:, :], ALU.mult, ALU.add, t, t_x, lw)
                drains(i, v)
                v = tt(X1, X1, ZS[:, d, :], ALU.mult, v, zs_done[d])
                zs_free[d] = [v]
                ys = split(YH[u][:, :], YL[u][:, :], X1, v, *yh_free[u])
                xc_free[d] = ys
                if d < 7:
                    nx = turned(d + 1)
                if b + 1 < NB:
                    xcs[d], cs = conv(d, *project(d, (0,)))
                    if lag_r is not None:
                        rows(*lag_r)
                    lag_r = (d, cs)
                if lag_o is not None:
                    project_out(*lag_o)
                lag_o = (d, ys)
            m_free = [t]
            if b + 1 < NB:
                t_rows = rows(*lag_r)
            t = project_out(*lag_o)
            o_ = []
            for k in range(4):
                i, p, w = outs[k]
                o_.append(acopy(ZS[:, 4 + k, :], p[:, :], t, *zs_free[4 + k]))
                drains(i, o_[-1])
            st_ = dma(s_so, so_[b], ZS[:, 4:8, :], *o_)
            for k in range(4, 8):
                zs_free[k] = [st_]
        f_ends = [st_] + [Landed(q.handle, q.n) for q in XT.sems]
        for q in fast.queues()[:4]:
            q.ops[-1][2] = True
        p1.close()

        rest = part("rest")
        p2 = ExitStack()
        MS = sbp(p2, "MS", [80, T], F32R)
        BS = sbp(p2, "BS", [80, FF], F32R)
        L2C = sbp(p2, "L2C", [128, 4], F32)
        p2b = ExitStack()
        stage = Stage([sbp(p2b, "STGB", [128, 2048], F32)], "a_st")
        STG2 = stage.slots
        QW = [sbp(p2b, f"QW{i}", [128, 4, 512], F32R) for i in range(4)]
        VW = [sbp(p2b, f"VW{i}", [128, 4, 256], F32R) for i in range(2)]
        AW = [sbp(p2b, f"AW{i}", [128, 4, R], F32R) for i in range(2)]
        RH = [sbp(p2b, f"RH{i}", [128, 4, S], F32R) for i in range(1)]
        RL = [sbp(p2b, f"RL{i}", [128, 4, S], F32R) for i in range(1)]
        QK = [sbp(p2b, f"QK{i}", [128, 4, S], F32R) for i in range(2)]
        QS = sbp(p2b, "QS", [97, NH, S], F32R)
        KS = sbp(p2b, "KS", [97, NH, S], F32R)
        VB = sbp(p2b, "VB", [128, 4, NH, 50], BF16)
        V1 = sbp(p2b, "V1", [128, 256], F32)
        PF = [sbp(p2b, f"PF{i}", [128, 1280], F32) for i in range(1)] * 2
        PH = [sbp(p2b, f"PH{i}", [128, 1280], F16) for i in range(2)]
        PL = [sbp(p2b, f"PL{i}", [128, 1280], F16) for i in range(2)]
        MX = sbp(p2b, "MX", [128, 4, NH], F32)
        NM = sbp(p2b, "NM", [NH, S], F32R)
        HA = sbp(p2b, "HA", [R, S], F32)
        TH = sbp(p2b, "TH", [R, S], F32)
        AO = sbp(p2b, "AO", [128, 400], F32)
        NU = sbp(p2b, "NU", [128, 8, R], F32)
        RD = sbp(p2b, "RD", [128, 8], F32)
        AM = sbp(p2b, "AM", [128, 4, R], F32)
        AM2 = sbp(p2b, "AM2", [128, R], F32)
        MT = [sbp(p2b, f"MT{i}", [128, 128], F32) for i in range(2)]
        MR = [sbp(p2b, f"MR{i}", [128, 128], F32R) for i in range(2)]
        L1C = sbp(p2b, "L1C", [128, 4], F32)
        WA_ = sbp(p2b, "WA_", [128, 4, R], F32)
        BD = sbp(p2b, "BD", [128, 4, 64], F32)
        AF = sbp(p2b, "AF", [128, 4, R], F32)

        s_w2 = Sem(sem("s_w2"))
        dma(s_w2, MT[0][:, :], maskt, *stage.free[0])
        dma(s_w2, MT[1][:, :], maskT)
        dma(s_w2, L1C[:, :], ln1)
        dma(s_w2, L2C[:, :], ln2)
        lw2 = dma(s_w2, AF[:, :, :], Aw.rearrange("(k p) r -> p k r", p=128))
        t_mr = [vcopy(MR[i][:, :], MT[i][:, :], lw2) for i in range(2)]
        t_q = []
        for n, src in enumerate((WqT, WkT)):
            i, d = stage.load(src.rearrange("(k p) n -> p k n", p=128), 2048)
            w = STG2[i][:, :].rearrange("p (k n) -> p k n", k=4)
            for k in range(4):
                t = ts(w[:, k, :], w[:, k, :], L1C[:, k:k + 1], None, ALU.mult, None, d, lw2)
                a = acopy(QW[2 * n][:, k, :], w[:, k, :], t)
                l = tt(QW[2 * n + 1][:, k, :], w[:, k, :], QW[2 * n][:, k, :].bitcast(F32), ALU.subtract, a)
                t_q += [a, l]
            stage.free[i] = [a, l]
        i, d = stage.load(Wo.rearrange("(k p) n -> p k n", p=128), 2048)
        w = STG2[i][:, :].rearrange("p (k n) -> p k n", k=4)
        z0 = fill(BD[:, :, :], 0.0)
        for e_ in range(4):
            ib, p, wb = bank((0, 1))
            for j in range(4):
                t = mm(p[:, 0:R], w[:, j, 128 * e_:128 * e_ + 128], AF[:, j, :], j == 0, j == 3, d, lw2, *wb)
            t = vcopy(WA_[:, e_, :], p[:, 0:R], t)
            drains(ib, t)
        stage.free[i] = [t]
        bd = []
        for e_ in range(4):
            for j in range(4):
                bd.append(vcopy(BD[32 * j:32 * j + 32, e_, R * j:R * j + R], WA_[32 * j:32 * j + 32, e_, :], z0, t))
        i, d = stage.load(Wv.rearrange("(k p) n -> p k n", p=128), 2048)
        w = STG2[i][:, :].rearrange("p (k n) -> p k n", k=4)
        t_v = []
        for k in range(4):
            ib, p, wb = bank((0, 1))
            for e_ in range(4):
                t = mm(p[:, 64 * e_:64 * e_ + 64], w[:, e_, 128 * k:128 * k + 128], BD[:, e_, :], True, True, d, *bd, *wb)
            v = ts(V1[:, :], p[:, 0:256], L1C[:, k:k + 1], None, ALU.mult, None, t, lw2, *t_v[-2:])
            drains(ib, v)
            a = acopy(VW[0][:, k, :], V1[:, :], v)
            l = tt(VW[1][:, k, :], V1[:, :], VW[0][:, k, :].bitcast(F32), ALU.subtract, a)
            t_v += [a, l]
        stage.free[i] = [v]
        t_a = []
        for k in range(4):
            t = ts(V1[:, 16 * k:16 * k + 16], AF[:, k, :], L2C[:, k:k + 1], None, ALU.mult, None, lw2, *t_v[-2:])
            a = acopy(AW[0][:, k, :], V1[:, 16 * k:16 * k + 16], t)
            l = tt(AW[1][:, k, :], V1[:, 16 * k:16 * k + 16], AW[0][:, k, :].bitcast(F32), ALU.subtract, a)
            t_a += [a, l]
        t_k1 = fill(KS[96:97, :, :], 1.0)
        t_vb = fill(VB[:, :, :, 48:50], 1.0)
        t_ms = [fill(MS[:, :], 0.0), fill(BS[:, :], 0.0)]
        i = 0
        d = dma(stage.sems[i], STG2[i][0:R, :], Bw, *stage.free[i])
        a = acopy(BS[0:16, :], STG2[i][0:R, :], d, *t_ms)
        a2 = acopy(BS[32:48, :], STG2[i][0:R, :], d)
        l = tt(BS[64:80, :], STG2[i][0:R, :], BS[0:16, :].bitcast(F32), ALU.subtract, a, t_ms[1])
        t_bs = [a2, l]
        stage.free[i] = [a2, l]

        SC = 1.0 / float(np.sqrt(np.float32(HD)))
        off = [0, 512, 896, 1152]
        G_P, G_S, G_A = (0, 1), (2, 3), (4, 5, 6, 7)
        s_stk, s_rst = Sem(sem("s_stk")), Sem(sem("s_rst"))
        free_qk, free_qs, free_ks, free_vb, free_r, free_nm, free_mx, free_ha = [], [], [], [], [], [], [], []
        pf_free, ph_free = [[], []], [[], []]
        v1_free = t_a[-2:]
        rd = []
        last_ms = []
        for b in range(NB):
            sl, dx = stage.load(xv[b], 2048)
            X = STG2[sl][:, :].rearrange("p (k d) -> p k d", k=4)
            xs = []
            for k in range(4):
                xs.append(ts(X[:, k, :], X[:, k, :], MEAN[:, 4 * b + k:4 * b + k + 1], RMS[:, 4 * b + k:4 * b + k + 1],
                             ALU.subtract, ALU.mult, dx))
            rr = []
            for d in range(4):
                i, p, w = bank(G_P)
                for k in range(4):
                    t = tr(p[:, 128 * k:128 * k + 128], X[:, k, 128 * d:128 * d + 128], idn[:, :], xs[k], *w)
                a = acopy(RH[0][:, d, :], p[:, :], t, *free_r)
                v = tt(RL[0][:, d, :], p[:, :], RH[0][:, d, :].bitcast(F32), ALU.subtract, a)
                drains(i, v)
                rr += [a, v]
            stage.free[sl] = [t]
            dma(s_rst, rh_d[b], RH[0][:, :, :], *rr)
            rd = [dma(s_rst, rl_d[b], RL[0][:, :, :])]
            rh, rl = (lambda k: RH[0][:, k, :]), (lambda k: RL[0][:, k, :])
            for n in range(2):
                qk = []
                for m in range(4):
                    i, p, w = bank(G_P)
                    t = three(p[:, :], lambda k: QW[2 * n][:, k, 128 * m:128 * m + 128],
                              lambda k: QW[2 * n + 1][:, k, 128 * m:128 * m + 128], rh, rl, 4, [*w, *rr, *t_q])
                    a = acopy(QK[0][:, m, :], p[:, :], t, *free_qk)
                    v = tt(QK[1][:, m, :], p[:, :], QK[0][:, m, :].bitcast(F32), ALU.subtract, a)
                    drains(i, v)
                    qk += [a, v]
                for slot in range(3):
                    part = QK[slot == (1, 2)[n]]
                    for j in range(4):
                        stk = dma(s_stk, (QS, KS)[n][32 * slot:32 * slot + 32, j::4, :], part[32 * j:32 * j + 32, :, :], *qk,
                                  *free_qs, *free_ks)
                free_qk = [stk]
            vb = []
            for j in range(4):
                i, p, w = bank(G_P)
                t = three(p[:, 0:256], lambda k: RH[0][:, k, 128 * j:128 * j + 128], lambda k: RL[0][:, k, 128 * j:128 * j + 128],
                          lambda k: VW[0][:, k, :], lambda k: VW[1][:, k, :], 4, [*w, *rr, *t_v])
                p3 = p[:, 0:256].rearrange("p (h r) -> p h r", r=R)
                v3 = V1[:, :].rearrange("p (h r) -> p h r", r=R)
                a = acopy(VB[:, j, :, 0:16], p3, t, *free_vb)
                v = tt(v3, p3, VB[:, j, :, 0:16], ALU.subtract, a, *v1_free)
                drains(i, v)
                v2 = vcopy(VB[:, j, :, 16:32], v3, v)
                v2 = tt(VB[:, j, :, 32:48], v3, VB[:, j, :, 16:32], ALU.subtract, v2)
                vb += [a, v2]
                v1_free = [v2]
            i, p, w = bank(G_P)
            t = three(p[0:R, :], lambda k: AW[0][:, k, :], lambda k: AW[1][:, k, :], rh, rl, 4, [*w, *rr, *t_a])
            t_ha = acopy(HA[:, :], p[0:R, :], t, *free_ha)
            drains(i, t_ha)
            free_r = [t, rd[0]]
            mxs = []
            for h in range(NH):
                for k in range(4):
                    i, p, w = bank(G_S)
                    n = 128 * (k + 1)
                    mm(p[:, 0:n], QS[0:96, h, 128 * k:n], KS[0:96, h, 0:n], True, False, *w, stk)
                    t = mm(p[:, n - 128:n], idr[:, :], MR[0][:, :], False, True, t_idr, *t_mr)
                    v = now[0].dve.add(lambda e, p=p, n=n, k=k, h=h: e.tensor_reduce(MX[:, k, h:h + 1], p[:, 0:n], AX.X, ALU.max),
                                [t, *free_mx])
                    drains(i, v)
            i, p, w = bank(G_P)
            for k in range(4):
                t = tr(p[0:NH, 128 * k:128 * k + 128], MX[:, k, :], idn[:, :], v, *w)
            free_mx = [t]
            a = activate(NM[:, :], p[0:NH, :], ACT.Identity, t, *free_nm, scale=-1.0)
            drains(i, a)
            stk2 = dma(s_stk, QS[96:97, :, :], NM[:, :], a, stk)
            free_nm = [stk2]
            am_prev = []
            for half in range(2):
                banks = []
                for k in range(4):
                    banks.append(bank(G_A))
                for h in range(8 * half, 8 * half + 8):
                    u = h % 2
                    es = []
                    for J in range(4):
                        i, p, w = bank(G_S)
                        n = 512 - 128 * J
                        mm(p[:, 0:n], KS[0:97, h, 128 * J:128 * J + 128], QS[0:97, h, 128 * J:512], True, False, *w, stk2, t_k1)
                        t = mm(p[:, 0:128], idr[:, :], MR[1][:, :], False, True)
                        a = activate(PF[u][:, off[J]:off[J] + n], p[:, 0:n], ACT.Exp, t, *pf_free[u], scale=SC)
                        drains(i, a)
                    free_qs = free_ks = [t]
                    v = vcopy(PH[u][:, :], PF[u][:, :], a, *ph_free[u])
                    v = tt(PL[u][:, :], PF[u][:, :], PH[u][:, :], ALU.subtract, v)
                    pf_free[0] = pf_free[1] = [v]
                    for k in range(4):
                        i, p, w = banks[k]
                        c0 = 50 * (h - 8 * half)
                        for J in range(k + 1):
                            o = off[J] + 128 * (k - J)
                            for q, P_ in enumerate((PH[u], PL[u])):
                                t = mm(p[:, c0:c0 + 50], P_[:, o:o + 128], VB[:, J, h, :], J == 0 and q == 0, J == k and q == 1,
                                       v, *vb, t_vb, *w)
                    ph_free[u] = [t]
                free_vb = [t]
                for k in range(4):
                    i, p, w = banks[k]
                    a = acopy(AO[:, :], p[:, 0:400], t, *am_prev)
                    drains(i, a)
                    A3 = AO[:, :].rearrange("p (h c) -> p h c", c=50)
                    v = tt(NU[:, :, :], A3[:, :, 0:16], A3[:, :, 16:32], ALU.add, a, *am_prev)
                    v = tt(NU[:, :, :], NU[:, :, :], A3[:, :, 32:48], ALU.add, v)
                    g = now[0].dve.add(lambda e, A3=A3: e.reciprocal(RD[:, :], A3[:, :, 48]), [a])
                    v = tt(NU[:, :, :], NU[:, :, :], RD[:, :].unsqueeze(2).to_broadcast([128, 8, R]), ALU.mult, v, g)
                    dst = AM[:, k, :] if half == 0 else AM2[:, :]
                    v = now[0].dve.add(lambda e, dst=dst: e.tensor_reduce(dst, NU[:, :, :].rearrange("p h r -> p r h"), AX.X, ALU.add),
                                [v, *last_ms])
                    am_prev = [v]
                    if half == 1:
                        v = tt(AM[:, k, :], AM[:, k, :], AM2[:, :], ALU.add, v)
                        am_prev = [v]
            i, p, w = bank(G_P)
            for k in range(4):
                t = tr(p[0:R, 128 * k:128 * k + 128], AM[:, k, :], idn[:, :], v, *w)
            a = activate(TH[:, :], p[0:R, :], ACT.Tanh, t, *last_ms)
            drains(i, a)
            v = stt(TH[:, :], TH[:, :], 0.1, HA[:, :], ALU.mult, ALU.mult, a, t_ha)
            free_ha = [v]
            c = slice(S * b, S * b + S)
            a = acopy(MS[0:16, c], TH[:, :], v, *t_ms)
            a2 = acopy(MS[64:80, c], TH[:, :], v)
            l = tt(MS[32:48, c], TH[:, :], MS[0:16, c].bitcast(F32), ALU.subtract, a)
            last_ms = [t, a2, l]
        end2 = [Token(w, len(w.ops) - 1) for w in rest.queues()[:4] if w.ops]
        r_stored = Landed(s_rst.handle, s_rst.n)
        x_loaded = [Landed(s.handle, s.n) for s in stage.sems]
        p2b.close()

        HF = FF // 2
        p3 = ExitStack()
        GW = [sbp(p3, f"GW{i}", [128, 4, HF], F32R) for i in range(2)]
        UW = [sbp(p3, f"UW{i}", [128, 4, HF], F32R) for i in range(2)]
        DW = [sbp(p3, f"DW{i}", [128, 8, DM], F32R) for i in range(2)]
        STG3 = [sbp(p3, f"STGC{i}", [128, 2048], F32) for i in range(1)]
        FH = [sbp(p3, f"FH{i}", [128, 4, S], F32R) for i in range(2)]
        FL = [sbp(p3, f"FL{i}", [128, 4, S], F32R) for i in range(2)]
        SG = [sbp(p3, f"SG{i}", [128, S], F32) for i in range(2)]
        GF = [sbp(p3, f"GF{i}", [128, S], F32) for i in range(2)]
        GH = [sbp(p3, f"GH{i}", [128, S], F32R) for i in range(3)]
        GL = [sbp(p3, f"GL{i}", [128, S], F32R) for i in range(3)]
        XT = [sbp(p3, f"XT{i}", [128, DM], F32) for i in range(2)]
        ST = [sbp(p3, f"ST{i}", [128, DM], F32) for i in range(2)]
        M1 = [sbp(p3, f"M1{i}", [128, DM], F32) for i in range(2)]
        XN = [sbp(p3, f"XN{i}", [128, DM], F32) for i in range(2)]
        s_r = [Sem(sem(f"s_r{i}")) for i in range(2)]
        s_t = [Sem(sem(f"s_t{i}")) for i in range(2)]
        s_m = [Sem(sem(f"s_m{i}")) for i in range(2)]
        s_wf = Sem(sem("s_wf"))
        stg_free = [*end2, *x_loaded]
        fr_free, gh_free, sg_free = [[r_stored, *end2], [r_stored, *end2]], [[], [], []], [[], []]
        xt_free, m1_free = [list(end2), list(end2)], [list(end2), list(end2)]
        wfree = list(end2)
        G_G, G_U, G_D = (0, 1), (2, 3), (4, 5, 6, 7)
        gn = 0
        xt2 = x.rearrange("(n p) d -> n p d", p=128)
        st2 = s_d.rearrange("(n p) d -> n p d", p=128)
        mt2 = m_d.rearrange("(n p) d -> n p d", p=128)
        ot2 = out.rearrange("(n p) d -> n p d", p=128)
        for half in range(2):
            tw = []
            for Wt, src in ((GW, WgT), (UW, WuT)):
                for kk in range(2):
                    d = dma(s_wf, STG3[0][:, :].rearrange("p (k m) -> p k m", k=2),
                            src.rearrange("(k p) m -> p k m", p=128)[:, 2 * kk:2 * kk + 2, HF * half:HF * half + HF], *stg_free)
                    stg_free = []
                    for k in (2 * kk, 2 * kk + 1):
                        w = STG3[0][:, HF * (k % 2):HF * (k % 2) + HF]
                        t = ts(w, w, L2C[:, k:k + 1], None, ALU.mult, None, d)
                        a = acopy(Wt[0][:, k, :], w, t, *wfree)
                        l = tt(Wt[1][:, k, :], w, Wt[0][:, k, :].bitcast(F32), ALU.subtract, a)
                        tw += [a, l]
                        stg_free += [a, l]
            for kk in range(2):
                d = dma(s_wf, STG3[0][:, :].rearrange("p (k m) -> p k m", k=4),
                        WdT.rearrange("(k p) m -> p k m", p=128)[:, 8 * half + 4 * kk:8 * half + 4 * kk + 4, :], *stg_free)
                hi = DW[0][:, 4 * kk:4 * kk + 4, :].rearrange("p k n -> p (k n)")
                lo = DW[1][:, 4 * kk:4 * kk + 4, :].rearrange("p k n -> p (k n)")
                a = acopy(hi, STG3[0][:, :], d, *wfree)
                l = tt(lo, STG3[0][:, :], hi.bitcast(F32), ALU.subtract, a)
                tw += [a, l]
                stg_free = [a, l]
            pend = None
            for b in range(NB):
                rb = b % 2
                dma(s_r[rb], FH[rb][:, :, :], rh_d[b], *fr_free[rb])
                dr = dma(s_r[rb], FL[rb][:, :, :], rl_d[b])
                acc = [None] * 4

                def down(f, g, tg, acc=acc):
                    for k in range(4):
                        if f == 0:
                            acc[k] = bank(G_D)
                        i, p, w = acc[k]
                        for q, (l_, r_) in enumerate(((GH[g], DW[0]), (GH[g], DW[1]), (GL[g], DW[0]))):
                            t = mm(p[:, :], l_[:, 128 * k:128 * k + 128], r_[:, f, :], f == 0 and q == 0, f == 7 and q == 2,
                                   *tg, *(w if f == 0 else []))
                    gh_free[g] = [t]
                    return t

                def finish(b, acc, t):
                    for k in range(4):
                        i, p, w = acc[k]
                        n = 4 * b + k
                        u = n % 2
                        if half == 0:
                            v = vcopy(M1[u][:, :], p[:, :], t, *m1_free[u])
                            drains(i, v)
                            m1_free[u] = [dma(s_m[u], mt2[n], M1[u][:, :], v)]
                        else:
                            dma(s_t[u], XT[u][:, :], xt2[n], *xt_free[u])
                            dma(s_t[u], ST[u][:, :], st2[n])
                            dl = dma(s_t[u], M1[u][:, :], mt2[n])
                            v = tt(M1[u][:, :], M1[u][:, :], p[:, :], ALU.add, t, dl)
                            drains(i, v)
                            z = ts(XN[u][:, :], XT[u][:, :], MEAN[:, n:n + 1], RSTD[:, n:n + 1], ALU.subtract, ALU.mult, dl,
                                   *xt_free[u])
                            v = tt(M1[u][:, :], M1[u][:, :], XN[u][:, :], ALU.add, v, z)
                            a = activate(M1[u][:, :], M1[u][:, :], ACT.Silu, v)
                            v = tt(M1[u][:, :], M1[u][:, :], ST[u][:, :], ALU.mult, a)
                            v = tt(M1[u][:, :], M1[u][:, :], XT[u][:, :], ALU.add, v)
                            xt_free[u] = [dma(s_t[u], ot2[n], M1[u][:, :], v)]

                for f in range(8):
                    i, p, w = bank(G_G)
                    c = slice(128 * f, 128 * f + 128)
                    xh, xl = (lambda k: FH[rb][:, k, :]), (lambda k: FL[rb][:, k, :])
                    three(p[:, :], lambda k: GW[0][:, k, c], lambda k: GW[1][:, k, c], xh, xl, 4, [*w, dr, *tw], close=False)
                    t = mm(p[:, :], BS[:, HF * half + 128 * f:HF * half + 128 * f + 128], MS[:, S * b:S * b + S], False, True,
                           *t_bs, *last_ms)
                    i2, p2_, w2 = bank(G_U)
                    t2 = three(p2_[:, :], lambda k: UW[0][:, k, c], lambda k: UW[1][:, k, c], xh, xl, 4, w2)
                    u, g = gn % 2, gn % 3
                    a = activate(SG[u][:, :], p[:, :], ACT.Silu, t, *sg_free[u])
                    drains(i, a)
                    v = tt(GF[u][:, :], SG[u][:, :], p2_[:, :], ALU.mult, a, t2)
                    drains(i2, v)
                    a = acopy(GH[g][:, :], GF[u][:, :], v, *gh_free[g])
                    l = tt(GL[g][:, :], GF[u][:, :], GH[g][:, :].bitcast(F32), ALU.subtract, a)
                    sg_free[u] = [l]
                    gn += 1
                    if pend is not None:
                        tdn = pend[0](*pend[1])
                        if pend[2] is not None:
                            pend[2](tdn)
                    fin = (lambda t, b=b, acc=acc: finish(b, acc, t)) if f == 7 else None
                    pend = (down, (f, g, [a, l]), fin)
                fr_free[rb] = [t2]
            tdn = pend[0](*pend[1])
            pend[2](tdn)
            wfree = [tdn]
            if half == 0:
                for u in range(2):
                    xt_free[u] = xt_free[u] + m1_free[0] + m1_free[1]
        final = [Landed(s.handle, s.n) for s in s_t + s_m + [s_rst] if s.n]
        p3.close()
        p2.close()
        rest.sp.ops.append([lambda e: e.nop(), final, False, None])

        for part_ in (first, general, fast, rest):
            for q in part_.queues():
                q.count()
        block = ctx.enter_context(nc.Block())

        def run(n, e):
            first.queues()[n].emit(e)
            e.wait_ge(*t_flag.value())
            differ = e.value_load(FLAG[0:1, 0:1], min_val=0, max_val=128)
            with e.If(differ != 0):
                last(general, g_ends, n, e)
            with e.Else():
                last(fast, f_ends, n, e)
            e.wait_ge(joined, 5)
            rest.queues()[n].emit(e)

        def last(branch, ends, n, e):
            q = branch.queues()[n]
            q.emit(e)
            if n == 4:
                for w in ends:
                    e.wait_ge(*w.value())
            elif q.ops:
                e.wait_ge(*Token(q, len(q.ops) - 1).value())
            e.sem_inc(joined, 1)

        @block.tensor
        def _(e):
            run(0, e)

        @block.scalar
        def _(e):
            run(1, e)

        @block.vector
        def _(e):
            run(2, e)

        @block.gpsimd
        def _(e):
            run(3, e)

        @block.sync
        def _(e):
            run(4, e)


def layout(a):
    a = {k.replace("L0_attn_", "a_").replace("L0_ffn_", "f_"): np.asarray(v) for k, v in a.items()}
    c = np.ascontiguousarray
    f = np.float32

    def col(v):
        return c(v.reshape(-1, 128).T)
    i, j = np.indices((128, 128))
    wx = np.zeros((DI, 66), f)
    for at, rows in ((0, slice(0, NS)), (32, slice(NS, 2 * NS)), (64, slice(2 * NS, 2 * NS + 1))):
        wx[:, at:at + rows.stop - rows.start] = a["a_W_x"].T[:, rows]
    return {
        "x": c(a["a_x"].reshape(T, DM)), "WinT": c(a["a_W_in"].T), "convw": c(a["a_conv_w"].reshape(DI, 4)),
        "convb": col(a["a_conv_b"]), "WxT": wx, "Alog": c(a["a_A_log"]), "dtb": col(a["a_dt_bias"]),
        "outWT": c(a["a_out_W"].T), "Dp": col(a["a_D"]), "ln1": col(a["f_ln1_w"]), "ln2": col(a["f_ln2_w"]),
        "WqT": c(a["f_Wq"].T), "WkT": c(a["f_Wk"].T), "Wv": c(a["f_Wv"]), "Wo": c(a["f_Wo"]), "Aw": c(a["f_A"]),
        "Bw": c(a["f_B"]), "WgT": c(a["f_W_in_base"].T), "WuT": c(a["f_W_up_base"].T), "WdT": c(a["f_W_down"].T),
        "ident": np.eye(128, dtype=f), "maskt": np.where(j <= i, 0.0, NEG).astype(f),
        "maskT": np.where(j >= i, 0.0, NEG).astype(f),
        "arow": c(a["a_A_log"][0].reshape(NS, 1)), "umask": np.stack([j > i, j >= i], 1).astype(f),
    }


def kernel(**inputs):
    from concourse import bacc
    from concourse.bass_utils import run_bass_kernel_spmd

    arrays = layout(inputs)
    nc = bacc.Bacc("TRN2", target_bir_lowering=False, num_devices=1, dynamic_dma_scratch_size=1024)
    feeds, args = {}, {}
    for name, a in arrays.items():
        feeds[f"in_{name}_dram"] = a
        args[name] = nc.dram_tensor(f"in_{name}_dram", a.shape, mybir.dt.from_np(a.dtype), kind="ExternalInput").ap()
    args["out"] = nc.dram_tensor("out_0_dram", (T, DM), F32, kind="ExternalOutput").ap()
    build(nc, **args)
    r = run_bass_kernel_spmd(nc, [feeds], core_ids=[0])
    return r.results[0]["out_0_dram"].reshape(NB, S, DM)
```

```python
from contextlib import ExitStack

import numpy as np

import concourse.bass as bass
from concourse import mybir

F32 = mybir.dt.float32
F32R = mybir.dt.float32r
BF16 = mybir.dt.bfloat16
F16 = mybir.dt.float16
ALU = mybir.AluOpType
ACT = mybir.ActivationFunctionType
AX = mybir.AxisListType

NB, S, DM, DI, NS, FF, NH, HD, R = 8, 512, 512, 1024, 16, 2048, 16, 32, 16
T = NB * S
NEG = -1.0e30


class Queue:

    def __init__(self, sem):
        self.sem, self.ops = sem, []

    def add(self, fn, waits):
        tok = Token(self, len(self.ops))
        for w in waits:
            w.wanted()
        self.ops.append([fn, waits, False, None])
        return tok

    def count(self):
        n = 0
        for op in self.ops:
            n += op[2]
            op[3] = n

    def emit(self, eng):
        seen = {}
        for fn, waits, marked, _ in self.ops:
            for w in waits:
                sem, value = w.value()
                if seen.get(id(sem), 0) < value:
                    eng.wait_ge(sem, value)
                    seen[id(sem)] = value
            ins = fn(eng)
            if marked:
                ins.then_inc(self.sem, 1)


class Token:
    def __init__(self, queue, at):
        self.queue, self.at = queue, at

    def wanted(self):
        self.queue.ops[self.at][2] = True

    def value(self):
        return self.queue.sem, self.queue.ops[self.at][3]


class Landed:

    def __init__(self, sem, n):
        self.sem, self.n = sem, n

    def wanted(self):
        pass

    def value(self):
        return self.sem, self.n


class Sem:
    def __init__(self, handle):
        self.handle, self.n = handle, 0


def build(nc, x, WinT, convw, convb, WxT, Alog, dtb, outWT, Dp, ln1, ln2, WqT, WkT, Wv, Wo, Aw, Bw, WgT, WuT, WdT,
          ident, umask, arow, maskt, maskT, out):
    ctx = ExitStack()
    with ctx:
        def sem(name):
            return ctx.enter_context(nc.semaphore(name))

        class Part:

            def __init__(self, name):
                self.pe, self.act, self.dve, self.pool, self.sp = (
                    Queue(sem(f"{name}_{n}")) for n in ("pe", "act", "dve", "pool", "sp"))

            def queues(self):
                return [self.pe, self.act, self.dve, self.pool, self.sp]

        now = [None]

        def part(name):
            now[0] = Part(name)
            for i in range(8):
                free[i] = []
            turn.clear()
            return now[0]

        def dma(s, dst, src, *waits):
            dst, src = (v.bitcast(F32) if v.dtype == F32R else v for v in (dst, src))
            s.n += 16
            n = s.n

            def go(e):
                e.dma_start(dst, src).then_inc(s.handle, 16)
            for w in waits:
                w.wanted()
            now[0].sp.ops.append([go, list(waits), False, None])
            return Landed(s.handle, n)

        def mm(o, l, r, a, z, *waits):
            return now[0].pe.add(lambda e: e.matmul(o, l, r, start=a, stop=z, skip_group_check=True), list(waits))

        def tr(o, i, idt, *waits):
            return now[0].pe.add(lambda e: e.transpose(o, i, idt), list(waits))

        def activate(o, i, f, *waits, bias=0.0, scale=1.0):
            return now[0].act.add(lambda e: e.activation(o, i, f, bias=bias, scale=scale), list(waits))

        def acopy(o, i, *waits):
            return now[0].act.add(lambda e: e.copy(o, i), list(waits))

        def tt(o, a, b, op, *waits, q=None):
            return (q or now[0].dve).add(lambda e: e.tensor_tensor(o, a, b, op), list(waits))

        def ts(o, a, s1, s2, op0, op1, *waits, q=None):
            if s2 is None:
                return (q or now[0].dve).add(lambda e: e.tensor_scalar(o, a, s1, None, op0), list(waits))
            return (q or now[0].dve).add(lambda e: e.tensor_scalar(o, a, s1, s2, op0, op1), list(waits))

        def stt(o, a, s, b, op0, op1, *waits):
            return now[0].dve.add(lambda e: e.scalar_tensor_tensor(out=o, in0=a, scalar=s, in1=b, op0=op0, op1=op1), list(waits))

        def vcopy(o, i, *waits, q=None):
            return (q or now[0].dve).add(lambda e: e.tensor_copy(o, i), list(waits))

        def total(o, i, op, axis, *waits):
            return now[0].dve.add(lambda e: e.tensor_reduce(o, i, axis, op), list(waits))

        def recip(o, i, *waits):
            return now[0].dve.add(lambda e: e.reciprocal(o, i), list(waits))

        def scan(o, a, b, *waits):
            return now[0].dve.add(lambda e: e.tensor_tensor_scan(o, a, b, 0.0, ALU.mult, ALU.add), list(waits))

        def fill(o, v, *waits, q=None):
            o = o.bitcast(F32) if o.dtype == F32R else o
            return (q or now[0].dve).add(lambda e: e.memset(o, v), list(waits))

        def sbp(c, name, shape, dt):
            return c.enter_context(nc.sbuf_tensor(name, shape, dt))

        PS = [ctx.enter_context(nc.psum_tensor(f"PS{i}", [128, 512], F32)) for i in range(8)]
        free = [[] for _ in range(8)]
        turn = {}

        def bank(group):
            k = turn.get(group, 0)
            turn[group] = k + 1
            i = group[k % len(group)]
            return i, PS[i], free[i]

        def drains(i, *toks):
            free[i] = list(toks)

        rh_d = nc.dram_tensor("rh_scratch", [NB, 128, 4, S], F32R, kind="Internal").ap()
        rl_d = nc.dram_tensor("rl_scratch", [NB, 128, 4, S], F32R, kind="Internal").ap()
        s_d = nc.dram_tensor("s_scratch", [T, DM], F32, kind="Internal").ap()
        m_d = nc.dram_tensor("m_scratch", [T, DM], F32, kind="Internal").ap()

        idn = sbp(ctx, "idn", [128, 128], F32)
        idr = sbp(ctx, "idr", [128, 128], F32R)
        UM = sbp(ctx, "UM", [128, 2, 128], F32)
        MEAN = sbp(ctx, "MEAN", [128, 32], F32)
        RSTD = sbp(ctx, "RSTD", [128, 32], F32)
        RMS = sbp(ctx, "RMS", [128, 32], F32)
        FLAG = sbp(ctx, "FLAG", [1, 1], mybir.dt.int32)
        joined = sem("joined")
        s_c = Sem(sem("s_c"))
        MHALF = sbp(ctx, "MHALF", [128, 4], F32)

        first = part("first")
        p0 = ExitStack()
        AL = sbp(p0, "AL", [128, 8, NS], F32)
        AR = sbp(p0, "AR", [128, NS], F32)
        NE = sbp(p0, "NE", [128, 2], F32)
        dma(s_c, idn[:, :], ident)
        dma(s_c, UM[:, :, :], umask)
        dma(s_c, AL[:, :, :], Alog.rearrange("(k p) j -> p k j", p=128))
        ld = dma(s_c, AR[:, :], Alog[0:1, :].to_broadcast([128, NS]))
        t_idr = vcopy(idr[:, :], idn[:, :], ld)
        t_mh = fill(MHALF[:, :], -0.5)
        v1 = fill(NE[:, 1:2], 1.0)
        v = tt(AL[:, :, :], AL[:, :, :], AR[:, :].unsqueeze(1).to_broadcast([128, 8, NS]), ALU.not_equal, ld)
        v = total(NE[:, 0:1], AL[:, :, :], ALU.max, AX.XY, v)
        t = mm(PS[0][0:1, 0:1], NE[:, 0:1], NE[:, 1:2], True, True, v, v1)
        t_flag = vcopy(FLAG[:, :], PS[0][0:1, 0:1], t)
        t_flag.wanted()
        p0.close()
        consts = [t_idr, t_mh, t_flag, ld]

        class Stage:

            def __init__(self, slots, name):
                self.slots, self.n = slots, 0
                self.sems = [Sem(sem(f"{name}{i}")) for i in range(len(slots))]
                self.free = [[] for _ in slots]

            def load(self, src, n, *waits):
                i = self.n % len(self.slots)
                self.n += 1
                dst = self.slots[i][:, 0:n]
                if len(src.shape) == 3:
                    dst = dst.rearrange("p (k m) -> p k m", k=src.shape[1])
                return i, dma(self.sems[i], dst, src, *self.free[i], *waits)

        def split(hi, lo, w, *waits, q=None):
            a = acopy(hi, w, *waits)
            return [a, tt(lo, w, hi.bitcast(F32), ALU.subtract, a, q=q)]

        def split_weights(stage, src, n, hi, lo, *waits):
            i, d = stage.load(src, n, *waits)
            stage.free[i] = split(hi, lo, stage.slots[i][:, 0:n], d)
            return stage.free[i]

        def three(pt, lh, ll, xh, xl, nk, waits, close=True):
            n, first = 3 * nk, True
            t = None
            for k in range(nk):
                for a, b in ((lh, xh), (lh, xl), (ll, xh)):
                    n -= 1
                    t = mm(pt, a(k), b(k), first, close and n == 0, *(waits if first else []))
                    first = False
            return t

        def stats(X, k, n, BST, AGG, VT, *waits):
            v = now[0].dve.add(lambda e: e.bn_stats(BST[:, :], X), list(waits))
            v = now[0].dve.add(lambda e: e.bn_aggr(AGG[:, :], BST[:, :]), [v])
            t1 = vcopy(MEAN[:, n:n + 1], AGG[:, 0:1], v)
            t2 = ts(VT[:, 0:1], AGG[:, 1:2], 1e-5, None, ALU.add, None, v)
            pool = now[0].pool
            t3 = tt(RSTD[:, n:n + 1], VT[:, 0:1], MHALF[:, 0:1], ALU.pow, t2, *consts, q=pool)
            t4 = tt(VT[:, 1:2], RSTD[:, n:n + 1], RSTD[:, n:n + 1], ALU.mult, t3)
            t4 = stt(VT[:, 2:3], VT[:, 1:2], AGG[:, 1:2], VT[:, 3:4], ALU.mult, ALU.add, t4)
            t5 = tt(VT[:, 1:2], VT[:, 2:3], MHALF[:, 0:1], ALU.pow, t4, q=pool)
            t6 = tt(RMS[:, n:n + 1], VT[:, 1:2], RSTD[:, n:n + 1], ALU.mult, t5)
            return [t1, t3], t6

        general = part("gen")
        p1 = ExitStack()
        WH = sbp(p1, "g_WH", [128, 4, 2048], F32R)
        WL = sbp(p1, "g_WL", [128, 4, 2048], F32R)
        OH = sbp(p1, "g_OH", [128, 8, 512], F32R)
        OL = sbp(p1, "g_OL", [128, 8, 512], F32R)
        XPH = sbp(p1, "g_XPH", [128, 8, 66], F32R)
        XPL = sbp(p1, "g_XPL", [128, 8, 66], F32R)
        XH = sbp(p1, "g_XH", [128, 4, S], F32R)
        XL = sbp(p1, "g_XL", [128, 4, S], F32R)
        CH = sbp(p1, "g_CH", [128, 8, S], F32R)
        CL = sbp(p1, "g_CL", [128, 8, S], F32R)
        stage = Stage([sbp(p1, f"g_STG{i}", [128, 2048], F32) for i in range(2)], "g_st")
        STG = stage.slots
        XC = sbp(p1, "g_XC", [128, 8, S], F32)
        ZS = sbp(p1, "g_ZS", [128, 8, S], F32)
        DT = sbp(p1, "g_DT", [128, S], F32)
        AB = sbp(p1, "g_AB", [128, S], F32)
        U = sbp(p1, "g_U", [128, S], F32)
        ACC = sbp(p1, "g_ACC", [128, S], F32)
        PPH = sbp(p1, "g_PPH", [65, S], F32R)
        PPL = sbp(p1, "g_PPL", [65, S], F32R)
        CW = sbp(p1, "g_CW", [128, 8, 4], F32)
        CB = sbp(p1, "g_CB", [128, 8], F32)
        AC = sbp(p1, "g_AC", [128, 8, NS], F32)
        DC = sbp(p1, "g_DC", [128, 8], F32)
        DB = sbp(p1, "g_DB", [128, 8], F32)
        ONE = sbp(p1, "g_ONE", [128, 128], F32)
        MB = sbp(p1, "g_MB", [128, 2], F32)
        BST = sbp(p1, "g_BST", [128, 6], F32)
        AGG = sbp(p1, "g_AGG", [128, 2], F32)
        VT = sbp(p1, "g_VT", [128, 4], F32)

        s_w = Sem(sem("g_w"))
        lw = [dma(s_w, CW[:, :, :], convw.rearrange("(k p) j -> p k j", p=128)),
              dma(s_w, CB[:, :], convb),
              dma(s_w, AC[:, :, :], Alog.rearrange("(k p) j -> p k j", p=128)),
              dma(s_w, DC[:, :], Dp),
              dma(s_w, DB[:, :], dtb)][-1]

        t_w = []
        wv_ = WinT.rearrange("(k p) n -> p k n", p=128)
        for k in range(4):
            t_w += split_weights(stage, wv_[:, k, :], 2048, WH[:, k, :], WL[:, k, :])
        t_o = []
        ov_ = outWT.rearrange("(k p) n -> p k n", p=128)
        for k in range(2):
            t_o += split_weights(stage, ov_[:, 4 * k:4 * k + 4, :], 2048,
                                 OH[:, 4 * k:4 * k + 4, :].rearrange("p k n -> p (k n)"),
                                 OL[:, 4 * k:4 * k + 4, :].rearrange("p k n -> p (k n)"))
        t_p = split_weights(stage, WxT.rearrange("(k p) n -> p k n", p=128), 8 * 66,
                            XPH[:, :, :].rearrange("p k n -> p (k n)"), XPL[:, :, :].rearrange("p k n -> p (k n)"))
        e0 = activate(AC[:, :, :], AC[:, :, :], ACT.Exp, lw)
        t_ac = ts(AC[:, :, :], AC[:, :, :], -1.0, None, ALU.mult, None, e0)
        t_one = fill(ONE[:, :], 1.0 / DI)
        t_vt = fill(VT[:, 3:4], 1e-6)
        r0 = total(MB[:, 0:1], DB[:, :], ALU.add, AX.X, lw)
        i, p, w0 = bank((0, 1))
        m0 = mm(p[:, 0:1], ONE[:, :], MB[:, 0:1], True, True, r0, t_one, *w0)
        t_mb = vcopy(MB[:, 1:2], p[:, 0:1], m0)
        drains(i, t_mb)

        xv = x.rearrange("(b k p) d -> b p k d", k=4, p=128)
        G_T, G_W, G_B, G_O = (0, 1), (2, 3, 4), (5, 6), (7,)
        done_xh, done_c, done_y, done_xc, done_zs, done_pp, done_dt = [], [[] for _ in range(8)], [], [], [], [], []
        acc_free, h_free = [], []
        for b in range(NB):
            sl, dx = stage.load(xv[b], 2048)
            X = STG[sl][:, :].rearrange("p (k d) -> p k d", k=4)
            xn, t6 = [], t_vt
            for k in range(4):
                n = 4 * b + k
                two, t6 = stats(X[:, k, :], k, n, BST, AGG, VT, dx, t6)
                xn.append(ts(X[:, k, :], X[:, k, :], MEAN[:, n:n + 1], RSTD[:, n:n + 1], ALU.subtract, ALU.mult, *two))
            xs = []
            for d in range(4):
                i, p, w = bank(G_T)
                for k in range(4):
                    t = tr(p[:, 128 * k:128 * k + 128], X[:, k, 128 * d:128 * d + 128], idn[:, :], xn[k], *consts, *w)
                a = acopy(XH[:, d, :], p[:, :], t, *done_xh)
                v = tt(XL[:, d, :], p[:, :], XH[:, d, :].bitcast(F32), ALU.subtract, a)
                drains(i, v)
                xs += [a, v]
            x_free = [t]
            done_xh = []
            cs = []
            for m in range(16):
                i, p, w = bank(G_W)
                t = three(p[:, :], lambda k: WH[:, k, 128 * m:128 * m + 128], lambda k: WL[:, k, 128 * m:128 * m + 128],
                          lambda k: XH[:, k, :], lambda k: XL[:, k, :], 4, [*w, *xs, *t_w])
                if m < 8:
                    y = XC[:, m, :]
                    a = activate(y, p[:, :], ACT.Identity, t, lw, *done_xc, bias=CB[:, m:m + 1], scale=CW[:, m, 3:4])
                    for j in range(1, 4):
                        a = stt(y[:, j:], p[:, 0:S - j], CW[:, m, 3 - j:4 - j], y[:, j:], ALU.mult, ALU.add, a)
                    drains(i, a)
                    a = activate(y, y, ACT.Silu, a)
                    h = acopy(CH[:, m, :], y, a, *done_c[m])
                    l = tt(CL[:, m, :], y, CH[:, m, :].bitcast(F32), ALU.subtract, h)
                    cs += [h, l]
                else:
                    a = activate(ZS[:, m - 8, :], p[:, :], ACT.Silu, t, *done_zs)
                    drains(i, a)
                    zs = a
            done_xh = [t]
            i, p, w = bank(G_T)
            t = three(p[0:65, :], lambda k: XPH[:, k, 0:65], lambda k: XPL[:, k, 0:65],
                      lambda k: CH[:, k, :], lambda k: CL[:, k, :], 8, [*w, *cs, *t_p])
            pp = split(PPH[:, :], PPL[:, :], p[0:65, :], t, *done_pp)
            drains(i, pp[1])

            def spread(p, q, *waits):
                one = idr[0:65, q:q + 1].to_broadcast([65, 128])
                mm(p[:, :], one, PPH[:, :], True, False, *pp, *consts, *waits)
                return mm(p[:, :], one, PPL[:, :], False, True)

            i, p, w = bank(G_T)
            t = spread(p, 64, *w)
            a0 = activate(U[:, :], p[:, :], ACT.Abs, t, t_mb, *h_free, bias=MB[:, 1:2])
            r = activate(DT[:, :], p[:, :], ACT.Relu, t, *done_dt, bias=MB[:, 1:2])
            drains(i, r)
            a0 = activate(U[:, :], U[:, :], ACT.Exp, a0, scale=-1.0)
            v = ts(ACC[:, :], U[:, :], 1.0, None, ALU.add, None, a0, *acc_free)
            lnu = activate(AB[:, :], ACC[:, :], ACT.Ln, v)
            v = ts(ACC[:, :], ACC[:, :], -1.0, None, ALU.add, None, v, lnu)
            v = tt(U[:, :], U[:, :], ACC[:, :], ALU.subtract, v)
            v = tt(U[:, :], U[:, :], AB[:, :], ALU.add, v, lnu)
            dtk = tt(DT[:, :], DT[:, :], U[:, :], ALU.add, v, r)
            ab_free = [dtk]
            ys = []
            for d in range(8):
                X1 = XC[:, d, :]
                v = ts(ACC[:, :], X1, DC[:, d:d + 1], None, ALU.mult, None, lw, *acc_free, cs[-1], cs[2 * d])
                v = tt(X1, X1, DT[:, :], ALU.mult, v, dtk, cs[2 * d], cs[2 * d + 1])
                for s in range(NS):
                    ib, pb, wb = bank((5, 6))
                    tb = spread(pb, s, *wb)
                    ic, pc, wc = bank((2, 3))
                    tc = spread(pc, 32 + s, *wc)
                    ea = activate(AB[:, :], DT[:, :], ACT.Exp, dtk, t_ac, *ab_free, scale=AC[:, d, s:s + 1])
                    v = tt(U[:, :], X1, pb[:, :], ALU.mult, tb, v)
                    drains(ib, v)
                    v = scan(AB[:, :], AB[:, :], U[:, :], ea, v)
                    v = tt(AB[:, :], AB[:, :], pc[:, :], ALU.mult, v, tc)
                    drains(ic, v)
                    v = tt(ACC[:, :], ACC[:, :], AB[:, :], ALU.add, v)
                    ab_free = [v]
                v = tt(ACC[:, :], ACC[:, :], ZS[:, d, :], ALU.mult, v, zs)
                a = acopy(CH[:, d, :], ACC[:, :], v, t)
                l = tt(CL[:, d, :], ACC[:, :], CH[:, d, :].bitcast(F32), ALU.subtract, a)
                acc_free = [l, a]
                ys += [a, l]
            done_xc, done_zs, done_dt, done_pp, h_free = [v], [v], [v, ea], [tc], [l]
            so = []
            for k in range(4):
                i, p, w = bank(G_O)
                t = three(p[:, :], lambda q: CH[:, q, 128 * k:128 * k + 128], lambda q: CL[:, q, 128 * k:128 * k + 128],
                          lambda q: OH[:, q, :], lambda q: OL[:, q, :], 8, [*w, *ys, *t_o])
                a = acopy(X[:, k, :], p[:, :], t, *x_free)
                drains(i, a)
                so.append(a)
            for m in range(8):
                done_c[m] = [t]
            ds = dma(stage.sems[sl], s_d.rearrange("(b k p) d -> b p k d", k=4, p=128)[b], X, *so)
            stage.free[sl] = [ds]
        g_ends = [Landed(q.handle, q.n) for q in stage.sems]
        for q in general.queues()[:4]:
            q.ops[-1][2] = True
        p1.close()

        fast = part("fast")
        p1 = ExitStack()
        WH = sbp(p1, "WH", [128, 4, 2048], F32R)
        WL = sbp(p1, "WL", [128, 4, 2048], F32R)
        OH = sbp(p1, "OH", [128, 8, 512], F32R)
        OL = sbp(p1, "OL", [128, 8, 512], F32R)
        XPH = sbp(p1, "XPH", [128, 8, 66], F32R)
        XPL = sbp(p1, "XPL", [128, 8, 66], F32R)
        XH = sbp(p1, "XH", [128, 4, S], F32R)
        XL = sbp(p1, "XL", [128, 4, S], F32R)
        XC = sbp(p1, "XC", [128, 8, S], F32)
        ZS = sbp(p1, "ZS", [128, 8, S], F32)
        CW = sbp(p1, "CW", [128, 8, 4], F32)
        CB = sbp(p1, "CB", [128, 8], F32)
        DC = sbp(p1, "DC", [128, 8], F32)
        DB = sbp(p1, "DB", [128, 8], F32)
        AB_ = sbp(p1, "AB_", [128, NS], F32)
        A16 = sbp(p1, "A16", [NS, 1], F32)
        ONE = sbp(p1, "ONE", [128, 128], F32)
        ONE2 = sbp(p1, "ONE2", [NS, 384], F32)
        MB = sbp(p1, "MB", [128, 2], F32)
        BST = sbp(p1, "BST", [128, 6], F32)
        AGG = sbp(p1, "AGG", [128, 2], F32)
        VT = sbp(p1, "VT", [128, 4], F32)

        pw = ExitStack()
        wst = Stage([sbp(pw, f"WST{i}", [128, 2048], F32) for i in range(3)], "f_ws")
        s_w = Sem(sem("f_w"))
        dma(s_w, CW[:, :, :], convw.rearrange("(k p) j -> p k j", p=128))
        dma(s_w, CB[:, :], convb)
        dma(s_w, AB_[:, :], Alog[0:1, :].to_broadcast([128, NS]))
        dma(s_w, A16[:, :], arow)
        dma(s_w, DC[:, :], Dp)
        lw = dma(s_w, DB[:, :], dtb)
        t_w = []
        wv_ = WinT.rearrange("(k p) n -> p k n", p=128)
        for k in range(4):
            t_w += split_weights(wst, wv_[:, k, :], 2048, WH[:, k, :], WL[:, k, :])
        t_p = split_weights(wst, WxT.rearrange("(k p) n -> p k n", p=128), 8 * 66,
                            XPH[:, :, :].rearrange("p k n -> p (k n)"), XPL[:, :, :].rearrange("p k n -> p (k n)"))
        t_o = []
        ov_ = outWT.rearrange("(k p) n -> p k n", p=128)
        for k in range(2):
            t_o += split_weights(wst, ov_[:, 4 * k:4 * k + 4, :], 2048,
                                 OH[:, 4 * k:4 * k + 4, :].rearrange("p k n -> p (k n)"),
                                 OL[:, 4 * k:4 * k + 4, :].rearrange("p k n -> p (k n)"))
        laid = t_w + t_p + t_o
        pw.close()
        XT = Stage([sbp(p1, f"XF{i}", [128, DM], F32) for i in range(2)], "f_x")
        XT.free = [list(laid), list(laid)]
        CH = [sbp(p1, f"CH{i}", [128, S], F32R) for i in range(2)]
        CL = [sbp(p1, f"CL{i}", [128, S], F32R) for i in range(2)]
        YH = [sbp(p1, f"YH{i}", [128, S], F32R) for i in range(2)]
        YL = [sbp(p1, f"YL{i}", [128, S], F32R) for i in range(2)]
        NH_ = [sbp(p1, f"NH_{i}", [128, 4, 128], F32R) for i in range(2)]
        NL_ = [sbp(p1, f"NL_{i}", [128, 4, 128], F32R) for i in range(2)]
        TMP = sbp(p1, "TMP", [128, 2048], F32)
        DT = sbp(p1, "DT", [128, S], F32)
        DEL = sbp(p1, "DEL", [128, S], F32)
        MH = sbp(p1, "MH", [128, 4, S], F32R)
        ML = sbp(p1, "ML", [128, 4, S], F32R)
        PPH = sbp(p1, "PPH", [65, S], F32R)
        PPL = sbp(p1, "PPL", [65, S], F32R)
        CS = sbp(p1, "CS", [80, 768], F32R)
        BT = sbp(p1, "BT", [80, 384], F32R)
        BN = sbp(p1, "BN", [128, 3, NS], F32)
        PN = sbp(p1, "PN", [128, 4, 65], F32)
        DBN = sbp(p1, "DBN", [128, 4, NS], F32)
        KEEP = sbp(p1, "KEEP", [128, S], F32)
        G = [TMP[:, 0:512], TMP[:, 512:1024]]
        ACC, PF = TMP[:, 1024:1536], TMP[0:65, 1536:2048]
        CE, CF = TMP[0:NS, 0:768], TMP[0:NS, 1024:1536]
        jo = [0, 384, 640, 768]

        e0 = activate(AB_[:, :], AB_[:, :], ACT.Exp, lw)
        t_ab = ts(AB_[:, :], AB_[:, :], -1.0, None, ALU.mult, None, e0)
        e0 = activate(A16[:, :], A16[:, :], ACT.Exp, lw)
        t_a16 = ts(A16[:, :], A16[:, :], -1.0, None, ALU.mult, None, e0)
        t_one = fill(ONE[:, :], 1.0 / DI)
        t_one2 = fill(ONE2[:, :], 1.0)
        t_vt = fill(VT[:, 3:4], 1e-6)
        v = fill(KEEP[:, :], 1.0, *laid)
        t_keep = fill(KEEP[:, :].rearrange("p (c t) -> p c t", c=4)[:, :, 0], 0.0, v)
        t_z = [fill(CS[:, :], 0.0, *laid), fill(BT[:, :], 0.0, *laid)]
        r0 = total(MB[:, 0:1], DB[:, :], ALU.add, AX.X, lw)
        i, p, w0 = bank((0,))
        m0 = mm(p[:, 0:1], ONE[:, :], MB[:, 0:1], True, True, r0, t_one, *w0)
        t_mb = vcopy(MB[:, 1:2], p[:, 0:1], m0)
        drains(i, t_mb)
        xt_ = x.rearrange("(n p) d -> n p d", p=128)
        so_ = s_d.rearrange("(b k p) d -> b p k d", k=4, p=128)
        s_so = Sem(sem("s_so"))

        tmp_free = list(laid)
        xh_free, xh_done = [], [None] * 4
        ch_free, yh_free, nh_free = [[*laid], [*laid]], [[*laid], [*laid]], [[*laid], [*laid]]
        xc_free, zs_free = [[] for _ in range(8)], [[] for _ in range(8)]
        m_free, dt_free, del_free, pp_free, cs_free, bt_free, bn_free, pn_free = ([*laid] for _ in range(8))
        t6 = t_vt
        p_bank = [None]

        def normed(b, k):
            nonlocal t6
            n = 4 * b + k
            u, d = XT.load(xt_[n], DM)
            X = XT.slots[u][:, :]
            two, t6 = stats(X, k, n, BST, AGG, VT, d, t6)
            xn = ts(X, X, MEAN[:, n:n + 1], RSTD[:, n:n + 1], ALU.subtract, ALU.mult, *two)
            i, p, w = bank((4,))
            for d in range(4):
                t = tr(p[:, 128 * d:128 * d + 128], X[:, 128 * d:128 * d + 128], idn[:, :], xn, *consts, *w)
            XT.free[u] = [t]
            c = slice(128 * k, 128 * k + 128)
            p3 = p[:, :].rearrange("p (d t) -> p d t", d=4)
            xh_done[k] = split(XH[:, :, c], XL[:, :, c], p3, t, *xh_free)
            drains(i, xh_done[k][1])

        def project(m, group):
            c = slice(128 * m, 128 * m + 128)
            i, p, w = bank(group)
            t = three(p[:, :], lambda k: WH[:, k, c], lambda k: WL[:, k, c], lambda k: XH[:, k, :], lambda k: XL[:, k, :], 4,
                      [*w, *sum(xh_done, []), *t_w])
            return i, p, t

        def conv(d, i, p, t):
            y, u = XC[:, d, :], d % 2
            a = activate(y, p[:, :], ACT.Identity, t, lw, *xc_free[d], bias=CB[:, d:d + 1], scale=CW[:, d, 3:4])
            for j in range(1, 4):
                a = stt(y[:, j:], p[:, 0:S - j], CW[:, d, 3 - j:4 - j], y[:, j:], ALU.mult, ALU.add, a)
            drains(i, a)
            a = activate(y, y, ACT.Silu, a)
            return a, split(CH[u][:, :], CL[u][:, :], y, a, *ch_free[u])

        def rows(d, cs):
            u = d % 2
            if d == 0:
                p_bank[0] = bank((5,))
            i, p, w = p_bank[0]
            for n, (l_, r_) in enumerate(((XPH, CH), (XPH, CL), (XPL, CH))):
                t = mm(p[0:65, :], l_[:, d, 0:65], r_[u][:, :], d == 0 and n == 0, d == 7 and n == 2, *cs, *t_p, *w)
            ch_free[u] = [t]
            return t

        for k in range(4):
            normed(0, k)
        xcs = [None] * 8
        lag = None
        for d in range(8):
            xcs[d], cs = conv(d, *project(d, (0, 1)))
            if lag is not None:
                rows(*lag)
            lag = (d, cs)
        t_rows = rows(*lag)

        for b in range(NB):
            ib, pb, _ = p_bank[0]
            t_pf = acopy(PF, pb[0:65, :], t_rows, *tmp_free)
            pp = split(PPH[:, :], PPL[:, :], pb[0:65, :], t_rows, *pp_free)
            drains(ib, pp[1])

            def spread(p, q, *waits):
                one = idr[0:65, q:q + 1].to_broadcast([65, 128])
                mm(p[:, :], one, PPH[:, :], True, False, *pp, *consts, *waits)
                return mm(p[:, :], one, PPL[:, :], False, True)

            def gate(m):
                i, p, t = project(8 + m, (0, 1))
                zs_done[m] = activate(ZS[:, m, :], p[:, :], ACT.Silu, t, *zs_free[m])
                drains(i, zs_done[m])
                return t

            zs_done = [None] * 8
            gate(0)
            i, p, w = bank((4,))
            t = spread(p, 64, *w)
            gate(1)
            gate(2)
            e = activate(G[0], p[:, :], ACT.Abs, t, t_mb, *tmp_free, bias=MB[:, 1:2])
            r = activate(DT[:, :], p[:, :], ACT.Relu, t, *dt_free, bias=MB[:, 1:2])
            drains(i, r)
            e = activate(G[0], G[0], ACT.Exp, e, scale=-1.0)
            v = ts(G[1], G[0], 1.0, None, ALU.add, None, e, *tmp_free)
            ln = activate(ACC, G[1], ACT.Ln, v, *tmp_free)
            v = ts(G[1], G[1], -1.0, None, ALU.add, None, v, ln)
            v = tt(G[0], G[0], G[1], ALU.subtract, v)
            v = tt(DT[:, :], DT[:, :], G[0], ALU.add, v, r)
            t_dt = tt(DT[:, :], DT[:, :], ACC, ALU.add, v, ln)
            v = tt(DEL[:, :].rearrange("p (c t) -> p c t", c=4), DT[:, :].rearrange("p (c t) -> p c t", c=4),
                   UM[:, 0, :].unsqueeze(1).to_broadcast([128, 4, 128]), ALU.mult, t_dt, *consts, *del_free)
            t_del = scan(DEL[:, :], KEEP[:, :], DEL[:, :], v, t_keep)
            v = vcopy(PF[64:65, :], DT[64:65, :], t_dt, t_pf)
            i, p, w = bank((4,))
            for k in range(4):
                t = tr(p[:, 65 * k:65 * k + 65], PF[:, 128 * k:128 * k + 128], idn[0:65, 0:65], v, *w)
            a = acopy(PN[:, :, :], p[:, 0:260].rearrange("p (k q) -> p k q", k=4), t, *pn_free)
            drains(i, a)
            for k in range(4):
                dbn = ts(DBN[:, k, :], PN[:, k, 0:NS], PN[:, k, 64:65], None, ALU.mult, None, a, *pn_free)
            bn = []
            for J in range(3):
                c = activate(BN[:, J, :], AB_[:, :], ACT.Exp, t_del, t_ab, *bn_free, scale=DEL[:, 128 * J + 127:128 * J + 128])
                bn.append(c)
            v = tt(BN[:, :, :], BN[:, :, :], DBN[:, 0:3, :], ALU.mult, c, dbn)
            i, p, w = bank((4,))
            for J in range(3):
                t = tr(p[0:NS, 128 * J:128 * J + 128], BN[:, J, :], idn[:, :], v, *w)
            bn_free = [t]
            bt = [acopy(BT[64:64 + NS, :], p[0:NS, 0:384], t, *bt_free, *t_z)]
            bt += split(BT[0:NS, :], BT[32:32 + NS, :], p[0:NS, 0:384])
            drains(i, bt[-1])
            dj = []
            for J in range(3):
                n = 384 - 128 * J
                dj.append(scan(CE[:, jo[J]:jo[J + 1]], ONE2[0:NS, 0:n], DT[0:NS, 512 - n:512], t_dt, t_one2, v))
            t_cf = acopy(CF, PF[32:32 + NS, :], t_pf, t_dt)
            c = activate(CE, CE, ACT.Exp, dj[-1], t_a16, scale=A16[:, 0:1])
            for J in range(3):
                n = 384 - 128 * J
                v = tt(CE[:, jo[J]:jo[J + 1]], CE[:, jo[J]:jo[J + 1]], CF[:, 512 - n:512], ALU.mult, c, t_cf)
            cs = [acopy(CS[0:NS, :], CE, v, *cs_free, *t_z), acopy(CS[32:32 + NS, :], CE)]
            cs.append(tt(CS[64:64 + NS, :], CE, CS[0:NS, :].bitcast(F32), ALU.subtract, cs[0]))
            t_tmp = cs
            spans = [(bank((6,)), 0), (bank((7,)), 0), None]
            spans[2] = (spans[1][0], 256)
            off_ = []
            for J in range(3):
                (i, p, w), at = spans[J]
                n = 384 - 128 * J
                t = mm(p[:, at:at + n], BT[:, 128 * J:128 * J + 128], CS[:, jo[J]:jo[J + 1]], True, True, *bt, *cs, *w)
            for J in range(3):
                (i, p, w), at = spans[J]
                n = 384 - 128 * J
                mo = split(MH[:, J, 128:128 + n], ML[:, J, 128:128 + n], p[:, at:at + n], t, *m_free, *off_[-1:])
                drains(i, mo[1])
                off_ += mo
            bt_free = cs_free = [t]
            g_free = [[*t_tmp], [*t_tmp]]
            v = None
            for s in range(NS):
                u = s % 2
                i, p, w = bank((2, 3))
                t = spread(p, 32 + s, *w)
                a = activate(G[u], DEL[:, :], ACT.Exp, t_del, t_ab, *g_free[u], scale=AB_[:, s:s + 1])
                g = tt(G[u], G[u], p[:, :], ALU.mult, a, t)
                drains(i, g)
                for k in range(4):
                    c = slice(128 * k, 128 * k + 128)
                    if s == 0:
                        v = ts(ACC[:, c], G[u][:, c], DBN[:, k, s:s + 1], None, ALU.mult, None, g, dbn, *t_tmp)
                    else:
                        v = stt(ACC[:, c], G[u][:, c], DBN[:, k, s:s + 1], ACC[:, c], ALU.mult, ALU.add, g, v)
                g_free[u] = [v]
                if 1 <= s <= 5:
                    xh_free = [gate(2 + s)]
                elif s >= 8 and s % 2 == 0 and b + 1 < NB:
                    normed(b + 1, (s - 8) // 2)
            pp_free, del_free, dt_free, pn_free = [t], [a], [dj[-1], v], [v]
            A3 = ACC.rearrange("p (c t) -> p c t", c=4)
            v = tt(A3, A3, UM[:, 1, :].unsqueeze(1).to_broadcast([128, 4, 128]), ALU.mult, v)
            md = split(MH[:, :, 0:128], ML[:, :, 0:128], A3, v, *m_free)
            t_m = off_ + md
            tmp_free = [*md]
            outs = [bank((g,)) for g in (2, 3, 6, 7)]

            def turned(d):
                u = d % 2
                i, p, w = bank((4,))
                for k in range(4):
                    t = tr(p[:, 128 * k:128 * k + 128], XC[:, d, 128 * k:128 * k + 128], idn[:, :], xcs[d], *w)
                p3 = p[:, :].rearrange("p (k d) -> p k d", k=4)
                r = split(NH_[u][:, :, :], NL_[u][:, :, :], p3, t, *nh_free[u])
                drains(i, r[1])
                return t, r

            def project_out(d, ys):
                u = d % 2
                for k in range(4):
                    i, p, w = outs[k]
                    c = slice(128 * k, 128 * k + 128)
                    for n, (l_, r_) in enumerate(((YH, OH), (YH, OL), (YL, OH))):
                        t = mm(p[:, :], l_[u][:, c], r_[:, d, :], d == 0 and n == 0, d == 7 and n == 2, *ys, *t_o,
                               *(w if d == 0 else []))
                yh_free[u] = [t]
                return t

            nx = turned(0)
            lag_o = lag_r = None
            for d in range(8):
                u = d % 2
                t_x, xn_ = nx
                i, p, w = bank((1,))
                n = 0
                for J in range(4):
                    for l_, r_ in ((NH_, MH), (NH_, ML), (NL_, MH)):
                        n += 1
                        t = mm(p[:, 128 * J:512], l_[u][:, J, :], r_[:, J, 0:512 - 128 * J], n == 1, n == 12, *xn_, *t_m, *w)
                nh_free[u] = [t]
                X1 = XC[:, d, :]
                v = stt(X1, X1, DC[:, d:d + 1], p[:, :], ALU.mult, ALU.add, t, t_x, lw)
                drains(i, v)
                v = tt(X1, X1, ZS[:, d, :], ALU.mult, v, zs_done[d])
                zs_free[d] = [v]
                ys = split(YH[u][:, :], YL[u][:, :], X1, v, *yh_free[u])
                xc_free[d] = ys
                if d < 7:
                    nx = turned(d + 1)
                if b + 1 < NB:
                    xcs[d], cs = conv(d, *project(d, (0,)))
                    if lag_r is not None:
                        rows(*lag_r)
                    lag_r = (d, cs)
                if lag_o is not None:
                    project_out(*lag_o)
                lag_o = (d, ys)
            m_free = [t]
            if b + 1 < NB:
                t_rows = rows(*lag_r)
            t = project_out(*lag_o)
            o_ = []
            for k in range(4):
                i, p, w = outs[k]
                o_.append(acopy(ZS[:, 4 + k, :], p[:, :], t, *zs_free[4 + k]))
                drains(i, o_[-1])
            st_ = dma(s_so, so_[b], ZS[:, 4:8, :], *o_)
            for k in range(4, 8):
                zs_free[k] = [st_]
        f_ends = [st_] + [Landed(q.handle, q.n) for q in XT.sems]
        for q in fast.queues()[:4]:
            q.ops[-1][2] = True
        p1.close()

        rest = part("rest")
        p2 = ExitStack()
        MS = sbp(p2, "MS", [80, T], F32R)
        BS = sbp(p2, "BS", [80, FF], F32R)
        L2C = sbp(p2, "L2C", [128, 4], F32)
        p2b = ExitStack()
        stage = Stage([sbp(p2b, "STGB", [128, 2048], F32)], "a_st")
        STG2 = stage.slots
        QW = [sbp(p2b, f"QW{i}", [128, 4, 512], F32R) for i in range(4)]
        VW = [sbp(p2b, f"VW{i}", [128, 4, 256], F32R) for i in range(2)]
        AW = [sbp(p2b, f"AW{i}", [128, 4, R], F32R) for i in range(2)]
        RH = [sbp(p2b, f"RH{i}", [128, 4, S], F32R) for i in range(1)]
        RL = [sbp(p2b, f"RL{i}", [128, 4, S], F32R) for i in range(1)]
        QT = [[[sbp(p2b, f"QT{n}{u}{i}", [128, S], F32R) for i in range(2)] for u in range(2)] for n in range(2)]
        QS = sbp(p2b, "QS", [97, NH, S], F32R)
        KS = sbp(p2b, "KS", [97, NH, S], F32R)
        VB = [sbp(p2b, f"VB{i}", [128, 4, NH, 50], BF16) for i in range(2)]
        V1 = sbp(p2b, "V1", [128, 256], F32)
        PF = [sbp(p2b, f"PF{i}", [128, 1280], F32) for i in range(2)]
        PH = [sbp(p2b, f"PH{i}", [128, 1280], F16) for i in range(2)]
        PL = [sbp(p2b, f"PL{i}", [128, 1280], F16) for i in range(2)]
        MX = [sbp(p2b, f"MX{i}", [128, 4, 4], F32) for i in range(2)]
        NM = [sbp(p2b, f"NM{i}", [4, S], F32R) for i in range(2)]
        HA = [sbp(p2b, f"HA{i}", [R, S], F32) for i in range(2)]
        TH = sbp(p2b, "TH", [R, S], F32)
        AO = sbp(p2b, "AO", [128, 800], F32)
        NU = sbp(p2b, "NU", [128, 16, R], F32)
        RD = sbp(p2b, "RD", [128, 16], F32)
        AM = sbp(p2b, "AM", [128, 4, R], F32)
        AM2 = sbp(p2b, "AM2", [128, 4, R], F32)
        MT = [sbp(p2b, f"MT{i}", [128, 128], F32) for i in range(2)]
        MR = [sbp(p2b, f"MR{i}", [128, 128], BF16) for i in range(2)]
        idb = sbp(p2b, "idb", [128, 128], BF16)
        L1C = sbp(p2b, "L1C", [128, 4], F32)
        WA_ = sbp(p2b, "WA_", [128, 4, R], F32)
        BD = sbp(p2b, "BD", [128, 4, 64], F32)
        AF = sbp(p2b, "AF", [128, 4, R], F32)

        s_w2 = Sem(sem("s_w2"))
        dma(s_w2, MT[0][:, :], maskt, *stage.free[0])
        dma(s_w2, MT[1][:, :], maskT)
        dma(s_w2, L1C[:, :], ln1)
        dma(s_w2, L2C[:, :], ln2)
        lw2 = dma(s_w2, AF[:, :, :], Aw.rearrange("(k p) r -> p k r", p=128))
        t_mr = [vcopy(MR[i][:, :], MT[i][:, :], lw2) for i in range(2)] + [vcopy(idb[:, :], idn[:, :], *consts)]
        t_q = []
        for n, src in enumerate((WqT, WkT)):
            i, d = stage.load(src.rearrange("(k p) n -> p k n", p=128), 2048)
            w = STG2[i][:, :].rearrange("p (k n) -> p k n", k=4)
            for k in range(4):
                t = ts(w[:, k, :], w[:, k, :], L1C[:, k:k + 1], None, ALU.mult, None, d, lw2)
                a = acopy(QW[2 * n][:, k, :], w[:, k, :], t)
                l = tt(QW[2 * n + 1][:, k, :], w[:, k, :], QW[2 * n][:, k, :].bitcast(F32), ALU.subtract, a)
                t_q += [a, l]
            stage.free[i] = [a, l]
        i, d = stage.load(Wo.rearrange("(k p) n -> p k n", p=128), 2048)
        w = STG2[i][:, :].rearrange("p (k n) -> p k n", k=4)
        z0 = fill(BD[:, :, :], 0.0)
        for e_ in range(4):
            ib, p, wb = bank((0, 1))
            for j in range(4):
                t = mm(p[:, 0:R], w[:, j, 128 * e_:128 * e_ + 128], AF[:, j, :], j == 0, j == 3, d, lw2, *wb)
            t = vcopy(WA_[:, e_, :], p[:, 0:R], t)
            drains(ib, t)
        stage.free[i] = [t]
        bd = []
        for e_ in range(4):
            for j in range(4):
                bd.append(vcopy(BD[32 * j:32 * j + 32, e_, R * j:R * j + R], WA_[32 * j:32 * j + 32, e_, :], z0, t))
        i, d = stage.load(Wv.rearrange("(k p) n -> p k n", p=128), 2048)
        w = STG2[i][:, :].rearrange("p (k n) -> p k n", k=4)
        t_v = []
        for k in range(4):
            ib, p, wb = bank((0, 1))
            for e_ in range(4):
                t = mm(p[:, 64 * e_:64 * e_ + 64], w[:, e_, 128 * k:128 * k + 128], BD[:, e_, :], True, True, d, *bd, *wb)
            v = ts(V1[:, :], p[:, 0:256], L1C[:, k:k + 1], None, ALU.mult, None, t, lw2, *t_v[-2:])
            drains(ib, v)
            a = acopy(VW[0][:, k, :], V1[:, :], v)
            l = tt(VW[1][:, k, :], V1[:, :], VW[0][:, k, :].bitcast(F32), ALU.subtract, a)
            t_v += [a, l]
        stage.free[i] = [v]
        t_a = []
        for k in range(4):
            t = ts(V1[:, 16 * k:16 * k + 16], AF[:, k, :], L2C[:, k:k + 1], None, ALU.mult, None, lw2, *t_v[-2:])
            a = acopy(AW[0][:, k, :], V1[:, 16 * k:16 * k + 16], t)
            l = tt(AW[1][:, k, :], V1[:, 16 * k:16 * k + 16], AW[0][:, k, :].bitcast(F32), ALU.subtract, a)
            t_a += [a, l]
        t_k1 = fill(KS[96:97, :, :], 1.0)
        for V in VB:
            t_vb = fill(V[:, :, :, 48:50], 1.0)
        t_ms = [fill(MS[:, :], 0.0), fill(BS[:, :], 0.0)]
        i = 0
        d = dma(stage.sems[i], STG2[i][0:R, :], Bw, *stage.free[i])
        a = acopy(BS[0:16, :], STG2[i][0:R, :], d, *t_ms)
        a2 = acopy(BS[32:48, :], STG2[i][0:R, :], d)
        l = tt(BS[64:80, :], STG2[i][0:R, :], BS[0:16, :].bitcast(F32), ALU.subtract, a, t_ms[1])
        t_bs = [a2, l]
        stage.free[i] = [a2, l]

        SC = 1.0 / float(np.sqrt(np.float32(HD)))
        off = [0, 512, 1024, 896]
        G_P, G_N, G_T, G_A = (0, 1), (2, 3), (4, 5), (6, 7)
        end1 = [Token(w, len(w.ops) - 1) for w in rest.queues()[:4] if w.ops]
        s_rst, s_xa = Sem(sem("s_rst")), stage.sems[0]
        s_qk = [[Sem(sem(f"s_qk{n}{r}")) for r in range(4)] for n in range(2)]
        s_nm = [Sem(sem(f"s_nm{r}")) for r in range(4)]
        x_free, xs, r_free, r_ready = [list(stage.free[0])], [], [[]], []
        slot_free, qt_free = [[] for _ in range(4)], [[[], []], [[], []]]
        pf_free, ph_free, vb_free = [list(end1), list(end1)], [[], []], [[], []]
        mx_free, nm_free, ha_free, am_free = [[], []], [[], []], [[], []], []
        v1_free, ao_free, nu_free, last_ms = t_a[-2:], [], [], []
        on_qk, on_nm, mx_ready, p_ready, vb_ready, ha_ready, x_ready, am_ready, pv_done = ({} for _ in range(9))
        pvs = [None, None]
        rh, rl = (lambda k: RH[0][:, k, :]), (lambda k: RL[0][:, k, :])

        def fetch(b):
            x_ready[b] = dma(s_xa, STG2[0][:, :].rearrange("p (k d) -> p k d", k=4), xv[b], *x_free[0])

        def normal(b, ds):
            X = STG2[0][:, :].rearrange("p (k d) -> p k d", k=4)
            if ds[0] == 0:
                xs[:] = [ts(X[:, k, :], X[:, k, :], MEAN[:, 4 * b + k:4 * b + k + 1], RMS[:, 4 * b + k:4 * b + k + 1],
                            ALU.subtract, ALU.mult, x_ready[b], q=rest.pool) for k in range(4)]
                r_ready.clear()
            for d in ds:
                i, p, w = bank(G_P)
                for k in range(4):
                    t = tr(p[:, 128 * k:128 * k + 128], X[:, k, 128 * d:128 * d + 128], idn[:, :], xs[k], *w)
                r = split(RH[0][:, d, :], RL[0][:, d, :], p[:, :], t, *r_free[0])
                drains(i, r[1])
                r_ready.extend(r)
            if ds[-1] == 3:
                x_free[0] = [t]
                if b + 1 < NB:
                    fetch(b + 1)
                dma(s_rst, rh_d[b], RH[0][:, :, :], *r_ready)
                r_free[0] = [dma(s_rst, rl_d[b], RL[0][:, :, :])]

        def project(w, n):
            u, c = w % 2, slice(128 * (w % 4), 128 * (w % 4) + 128)
            i, p, wb = bank(G_P)
            t = three(p[:, :], lambda k: QW[2 * n][:, k, c], lambda k: QW[2 * n + 1][:, k, c], rh, rl, 4, [*wb, *r_ready, *t_q])
            pair = split(QT[n][u][0][:, :], QT[n][u][1][:, :], p[:, :], t, *qt_free[n][u])
            drains(i, pair[1])
            if n == 1 and w % 4 == 3:
                r_free[0] = r_free[0] + [t]
            return pair

        def stack(w, n, pair):
            r, u = w % 4, w % 2
            for slot in range(3):
                src = QT[n][u][slot == (1, 2)[n]]
                for j in range(4):
                    d = dma(s_qk[n][r], (QS, KS)[n][32 * slot:32 * slot + 32, 4 * r + j, :], src[32 * j:32 * j + 32, :], *pair,
                            *slot_free[r], *on_nm.get(w - 4, []))
            on_qk[w, n] = d
            qt_free[n][u] = [d]

        def values(b, js):
            for j in js:
                i, p, w = bank(G_P)
                c = slice(128 * j, 128 * j + 128)
                t = three(p[:, 0:256], lambda k: RH[0][:, k, c], lambda k: RL[0][:, k, c],
                          lambda k: VW[0][:, k, :], lambda k: VW[1][:, k, :], 4, [*w, *r_ready, *t_v])
                p3 = p[:, 0:256].rearrange("p (h r) -> p h r", r=R)
                v3 = V1[:, :].rearrange("p (h r) -> p h r", r=R)
                V = VB[b % 2]
                a = acopy(V[:, j, :, 0:16], p3, t, *vb_free[b % 2])
                v = tt(v3, p3, V[:, j, :, 0:16], ALU.subtract, a, *v1_free)
                drains(i, v)
                v2 = vcopy(V[:, j, :, 16:32], v3, v, q=rest.pool)
                v2 = tt(V[:, j, :, 32:48], v3, V[:, j, :, 16:32], ALU.subtract, v2, q=rest.pool)
                vb_ready.setdefault(b, []).extend([a, v2])
                v1_free[:] = [v2]

        def low_rank(b):
            i, p, w = bank(G_P)
            t = three(p[0:R, :], lambda k: AW[0][:, k, :], lambda k: AW[1][:, k, :], rh, rl, 4, [*w, *r_ready, *t_a])
            ha_ready[b] = acopy(HA[b % 2][:, :], p[0:R, :], t, *ha_free[b % 2])
            drains(i, ha_ready[b])
            r_free[0] = r_free[0] + [t]

        def largest(g, ks):
            w, j = divmod(g, 4)
            h, u, at = 4 * (w % 4) + j, w % 2, 0
            i, p, wb = bank(G_N)
            spans = []
            for k in ks:
                n = 128 * k + 128
                mm(p[:, at:at + n], QS[0:96, h, 128 * k:n], KS[0:96, h, 0:n], True, False, *wb, on_qk[w, 0], on_qk[w, 1])
                t = mm(p[:, at + n - 128:at + n], idb[:, :], MR[0][:, :], False, True, *t_mr)
                spans.append((k, at, n))
                at += n
            for k, at, n in spans:
                v = total(MX[u][:, k, j:j + 1], p[:, at:at + n], ALU.max, AX.X, t, *mx_free[u])
            drains(i, v)
            mx_ready[w] = v

        def largest_in(w):
            u, r = w % 2, w % 4
            i, p, wb = bank(G_P)
            for k in range(4):
                t = tr(p[0:4, 128 * k:128 * k + 128], MX[u][:, k, :], idn[:, :], mx_ready[w], *wb)
            mx_free[u] = [t]
            a = activate(NM[u][:, :], p[0:4, :], ACT.Identity, t, *nm_free[u], scale=-1.0)
            drains(i, a)
            d = dma(s_nm[r], QS[96:97, 4 * r:4 * r + 4, :], NM[u][:, :], a, *slot_free[r])
            nm_free[u] = [d]
            on_nm[w] = [d]

        def weights(g, Js):
            w, j = divmod(g, 4)
            r, u, at = w % 4, g % 2, 0
            i, p, wb = bank(G_T)
            for J in Js:
                n = 512 - 128 * J
                mm(p[:, at:at + n], KS[0:97, 4 * r + j, 128 * J:128 * J + 128], QS[0:97, 4 * r + j, 128 * J:512], True, False, *wb,
                   *on_nm[w], on_qk[w, 0], on_qk[w, 1], t_k1)
                t = mm(p[:, at:at + 128], idb[:, :], MR[1][:, :], False, True, *t_mr)
                at += n
            o = off[Js[0]]
            a = activate(PF[u][:, o:o + at], p[:, 0:at], ACT.Exp, t, *pf_free[u], scale=SC)
            drains(i, a)
            if Js[-1] == 2:
                p_ready[g] = acopy(PH[u][:, :], PF[u][:, :], a, *ph_free[u])
                if j == 3:
                    slot_free[r] = [t]

        def remainder(g):
            u = g % 2
            p_ready[g] = pf_free[u] = [tt(PL[u][:, c], PF[u][:, c], PH[u][:, c], ALU.subtract, p_ready[g], *ph_free[u], q=q)
                                       for c, q in ((slice(0, 1024), rest.dve), (slice(1024, 1280), rest.pool))]

        def mixed(g):
            w, j = divmod(g, 4)
            b, u, h = w // 4, g % 2, g % 16
            if j == 0:
                pvs[:] = [bank(G_A), bank(G_A)]
            for k in range(4):
                i, p, wb = pvs[k // 2]
                c0 = 200 * (k % 2) + 50 * j
                for J in range(k + 1):
                    o = off[J] + 128 * (k - J)
                    for q, P_ in enumerate((PH[u], PL[u])):
                        t = mm(p[:, c0:c0 + 50], P_[:, o:o + 128], VB[b % 2][:, J, h, :], J == 0 and q == 0, J == k and q == 1,
                               *p_ready[g], *vb_ready[b], t_vb, *wb)
            ph_free[u] = [t]
            pv_done[w] = t

        def summed(w):
            b, t = w // 4, pv_done[w]
            for q in range(2):
                i, p, wb = pvs[q]
                a = acopy(AO[:, 400 * q:400 * q + 400], p[:, 0:400], t, *ao_free)
                drains(i, a)
            A3 = AO[:, :].rearrange("p (h c) -> p h c", c=50)
            n = tt(NU[:, :, :], A3[:, :, 0:16], A3[:, :, 16:32], ALU.add, a, *nu_free, q=rest.pool)
            n = tt(NU[:, :, :], NU[:, :, :], A3[:, :, 32:48], ALU.add, n, q=rest.pool)
            g = recip(RD[:, :], A3[:, :, 48], a, *nu_free)
            ao_free[:] = [n, g]
            v = tt(NU[:, :, :], NU[:, :, :], RD[:, :].unsqueeze(2).to_broadcast([128, 16, R]), ALU.mult, n, g)
            dst = AM2 if w % 4 else AM
            v = total(dst[:, :, :], NU[:, :, :].rearrange("p (k h) r -> p k r h", k=4), ALU.add, AX.X, v, *am_free)
            nu_free[:] = [v]
            if w % 4:
                v = tt(AM[:, :, :], AM[:, :, :], AM2[:, :, :], ALU.add, v)
            am_free[:] = am_ready[b] = [v]
            if w % 4 == 3:
                vb_free[b % 2] = [t]

        def modulation(b):
            i, p, w = bank(G_P)
            for k in range(4):
                t = tr(p[0:R, 128 * k:128 * k + 128], AM[:, k, :], idn[:, :], *am_ready[b], *w)
            am_free[:] = [t]
            a = activate(TH[:, :], p[0:R, :], ACT.Tanh, t, *last_ms)
            drains(i, a)
            v = stt(TH[:, :], TH[:, :], 0.1, HA[b % 2][:, :], ALU.mult, ALU.mult, a, ha_ready[b])
            ha_free[b % 2] = [v]
            c = slice(S * b, S * b + S)
            a = acopy(MS[0:16, c], TH[:, :], v, *t_ms)
            a2 = acopy(MS[64:80, c], TH[:, :], v)
            l = tt(MS[32:48, c], TH[:, :], MS[0:16, c].bitcast(F32), ALU.subtract, a)
            last_ms[:] = [a2, l]

        fetch(0)
        heads = NH * NB
        for g in range(-16, heads + 4):
            for Js, ks in zip(((0,), (1, 3), (2,)), ((3,), (2, 0), (1,))):
                if 0 <= g < heads:
                    weights(g, Js)
                if 0 <= g + 6 < heads:
                    largest(g + 6, ks)
                if ks == (3,) and 0 <= g - 1 < heads:
                    remainder(g - 1)
            if g >= 5 and (g - 1) % 4 == 0:
                summed((g - 5) // 4)
            if (g + 2) % 4 == 0 and 0 <= g + 2 < heads:
                largest_in((g + 2) // 4)
            if (g + 16) % 16 in (0, 1) and g + 16 < heads:
                normal((g + 16) // 16, ((0, 1), (2, 3))[(g + 16) % 16])
            if (g + 7) % 16 in (0, 1) and 0 <= g + 7 < heads:
                values((g + 7) // 16, ((0, 1), (2, 3))[(g + 7) % 16])
            if (g + 5) % 16 == 0 and 0 <= g + 5 < heads:
                low_rank((g + 5) // 16)
            if (g + 15) % 4 == 0 and 0 <= g + 15 < heads:
                pair = project((g + 15) // 4, 0)
            if (g + 13) % 4 == 0 and 0 <= g + 13 < heads:
                stack((g + 13) // 4, 0, pair)
                stack((g + 13) // 4, 1, project((g + 13) // 4, 1))
            if 0 <= g - 1 < heads:
                mixed(g - 1)
            if (g - 19) % 16 == 0 and g >= 19:
                modulation((g - 19) // 16)
        end2 = [Token(w, len(w.ops) - 1) for w in rest.queues()[:4] if w.ops]
        r_stored = Landed(s_rst.handle, s_rst.n)
        x_loaded = [Landed(s.handle, s.n) for s in stage.sems]
        p2b.close()

        HF = FF // 2
        p3 = ExitStack()
        GW = [sbp(p3, f"GW{i}", [128, 4, HF], F32R) for i in range(2)]
        UW = [sbp(p3, f"UW{i}", [128, 4, HF], F32R) for i in range(2)]
        DW = [sbp(p3, f"DW{i}", [128, 8, DM], F32R) for i in range(2)]
        STG3 = [sbp(p3, f"STGC{i}", [128, 3, 512], F32) for i in range(2)]
        FH = [sbp(p3, f"FH{i}", [128, 4, S], F32R) for i in range(2)]
        FL = [sbp(p3, f"FL{i}", [128, 4, S], F32R) for i in range(2)]
        SG = [sbp(p3, f"SG{i}", [128, S], F32) for i in range(2)]
        GF = [sbp(p3, f"GF{i}", [128, S], F32) for i in range(2)]
        GH = [sbp(p3, f"GH{i}", [128, S], F32R) for i in range(3)]
        GL = [sbp(p3, f"GL{i}", [128, S], F32R) for i in range(3)]
        XT = [sbp(p3, f"XT{i}", [128, DM], F32) for i in range(4)]
        ST = [sbp(p3, f"ST{i}", [128, DM], F32) for i in range(4)]
        M1 = [sbp(p3, f"M1{i}", [128, DM], F32) for i in range(4)]
        XN = [sbp(p3, f"XN{i}", [128, DM], F32) for i in range(2)]
        s_r = [Sem(sem(f"s_r{i}")) for i in range(2)]
        s_t = [Sem(sem(f"s_t{i}")) for i in range(4)]
        s_m = [Sem(sem(f"s_m{i}")) for i in range(4)]
        s_wf = [Sem(sem(f"s_wf{i}")) for i in range(2)]
        stg_free = [[*end2, *x_loaded], [*end2, *x_loaded]]
        fr_free, gh_free, sg_free = [[r_stored, *end2], [r_stored, *end2]], [[], [], []], [[], []]
        xt_free, m1_free, xn_free = [list(end2) for _ in range(4)], [list(end2) for _ in range(4)], [[], []]
        tw, loaded = {}, [None] * 4
        G_G, G_U, G_D = (0, 1), (2, 3), (4, 5, 6, 7)
        gn = 0
        xt2 = x.rearrange("(n p) d -> n p d", p=128)
        st2 = s_d.rearrange("(n p) d -> n p d", p=128)
        mt2 = m_d.rearrange("(n p) d -> n p d", p=128)
        ot2 = out.rearrange("(n p) d -> n p d", p=128)
        wd2 = WdT.rearrange("(f p) m -> f p m", p=128)
        l2b = L2C[:, :].unsqueeze(2).to_broadcast([128, 4, 128])

        def slice_of(n, *waits):
            u, f = n % 2, n % 8
            c = slice(128 * f, 128 * f + 128)
            S3 = STG3[u]
            dma(s_wf[u], S3[:, 0, :], WgT[n], *stg_free[u])
            dma(s_wf[u], S3[:, 1, :], WuT[n])
            d = dma(s_wf[u], S3[:, 2, :], wd2[n])
            tw[n] = []
            for j, Wt in ((0, GW), (1, UW)):
                w = S3[:, j, :].rearrange("p (k m) -> p k m", k=4)
                t = tt(w, w, l2b, ALU.mult, d)
                tw[n] += split(Wt[0][:, :, c], Wt[1][:, :, c], w, t, *waits)
            tw[n] += split(DW[0][:, f, :], DW[1][:, f, :], S3[:, 2, :], d, *waits)
            stg_free[u] = tw[n]

        for n in range(8):
            slice_of(n, *end2)
        for half in range(2):
            pend = None
            for b in range(NB):
                rb = b % 2
                dma(s_r[rb], FH[rb][:, :, :], rh_d[b], *fr_free[rb])
                dr = dma(s_r[rb], FL[rb][:, :, :], rl_d[b])
                acc = [None] * 4

                def down(f, g, tg, acc=acc):
                    for k in range(4):
                        if f == 0:
                            acc[k] = bank(G_D)
                        i, p, w = acc[k]
                        for q, (l_, r_) in enumerate(((GH[g], DW[0]), (GH[g], DW[1]), (GL[g], DW[0]))):
                            t = mm(p[:, :], l_[:, 128 * k:128 * k + 128], r_[:, f, :], f == 0 and q == 0, f == 7 and q == 2,
                                   *tg, *(w if f == 0 else []))
                    gh_free[g] = [t]
                    return t

                def fetched(b):
                    for u in range(4):
                        n = 4 * b + u
                        dma(s_t[u], XT[u][:, :], xt2[n], *xt_free[u])
                        dma(s_t[u], ST[u][:, :], st2[n])
                        loaded[u] = dma(s_t[u], M1[u][:, :], mt2[n])

                def finish(b, acc, t):
                    for k in range(4):
                        i, p, w = acc[k]
                        n, u = 4 * b + k, k
                        if half == 0:
                            v = vcopy(M1[u][:, :], p[:, :], t, *m1_free[u])
                            drains(i, v)
                            m1_free[u] = [dma(s_m[u], mt2[n], M1[u][:, :], v)]
                        else:
                            dl = loaded[u]
                            v = tt(M1[u][:, :], M1[u][:, :], p[:, :], ALU.add, t, dl)
                            drains(i, v)
                            z = ts(XN[k % 2][:, :], XT[u][:, :], MEAN[:, n:n + 1], RSTD[:, n:n + 1], ALU.subtract, ALU.mult, dl,
                                   *xn_free[k % 2])
                            v = tt(M1[u][:, :], M1[u][:, :], XN[k % 2][:, :], ALU.add, v, z)
                            xn_free[k % 2] = [v]
                            a = activate(M1[u][:, :], M1[u][:, :], ACT.Silu, v)
                            v = tt(M1[u][:, :], M1[u][:, :], ST[u][:, :], ALU.mult, a)
                            v = tt(M1[u][:, :], M1[u][:, :], XT[u][:, :], ALU.add, v)
                            xt_free[u] = [dma(s_t[u], ot2[n], M1[u][:, :], v)]

                for f in range(8):
                    i, p, w = bank(G_G)
                    c = slice(128 * f, 128 * f + 128)
                    xh, xl = (lambda k: FH[rb][:, k, :]), (lambda k: FL[rb][:, k, :])
                    three(p[:, :], lambda k: GW[0][:, k, c], lambda k: GW[1][:, k, c], xh, xl, 4, [*w, dr, *tw[8 * half + f]], close=False)
                    t = mm(p[:, :], BS[:, HF * half + 128 * f:HF * half + 128 * f + 128], MS[:, S * b:S * b + S], False, True,
                           *t_bs, *last_ms)
                    i2, p2_, w2 = bank(G_U)
                    t2 = three(p2_[:, :], lambda k: UW[0][:, k, c], lambda k: UW[1][:, k, c], xh, xl, 4, w2)
                    u, g = gn % 2, gn % 3
                    a = activate(SG[u][:, :], p[:, :], ACT.Silu, t, *sg_free[u])
                    drains(i, a)
                    v = tt(GF[u][:, :], SG[u][:, :], p2_[:, :], ALU.mult, a, t2)
                    drains(i2, v)
                    a = acopy(GH[g][:, :], GF[u][:, :], v, *gh_free[g])
                    l = tt(GL[g][:, :], GF[u][:, :], GH[g][:, :].bitcast(F32), ALU.subtract, a)
                    sg_free[u] = [l]
                    gn += 1
                    if pend is not None:
                        tdn = pend[0](*pend[1])
                        if pend[2] is not None:
                            pend[2](tdn)
                    fin = (lambda t, b=b, acc=acc: finish(b, acc, t)) if f == 7 else None
                    pend = (down, (f, g, [a, l]), fin)
                    if half == 1 and f == 2:
                        fetched(b)
                    if half == 0 and b == NB - 1 and f > 0:
                        slice_of(7 + f, t2, tdn)
                fr_free[rb] = [t2]
            tdn = pend[0](*pend[1])
            pend[2](tdn)
            if half == 0:
                slice_of(15, tdn)
                for u in range(4):
                    xt_free[u] = xt_free[u] + m1_free[u]
        final = [Landed(s.handle, s.n) for s in s_t + s_m + [s_rst] if s.n]
        p3.close()
        p2.close()
        rest.sp.ops.append([lambda e: e.nop(), final, False, None])

        for part_ in (first, general, fast, rest):
            for q in part_.queues():
                q.count()
        block = ctx.enter_context(nc.Block())

        def run(n, e):
            first.queues()[n].emit(e)
            e.wait_ge(*t_flag.value())
            differ = e.value_load(FLAG[0:1, 0:1], min_val=0, max_val=128)
            with e.If(differ != 0):
                last(general, g_ends, n, e)
            with e.Else():
                last(fast, f_ends, n, e)
            e.wait_ge(joined, 5)
            rest.queues()[n].emit(e)

        def last(branch, ends, n, e):
            q = branch.queues()[n]
            q.emit(e)
            if n == 4:
                for w in ends:
                    e.wait_ge(*w.value())
            elif q.ops:
                e.wait_ge(*Token(q, len(q.ops) - 1).value())
            e.sem_inc(joined, 1)

        @block.tensor
        def _(e):
            run(0, e)

        @block.scalar
        def _(e):
            run(1, e)

        @block.vector
        def _(e):
            run(2, e)

        @block.gpsimd
        def _(e):
            run(3, e)

        @block.sync
        def _(e):
            run(4, e)


def layout(a):
    a = {k.replace("L0_attn_", "a_").replace("L0_ffn_", "f_"): np.asarray(v) for k, v in a.items()}
    c = np.ascontiguousarray
    f = np.float32

    def col(v):
        return c(v.reshape(-1, 128).T)

    def tiled(v):
        return c(v.reshape(16, 128, 4, 128).transpose(0, 3, 2, 1).reshape(16, 128, 512))
    i, j = np.indices((128, 128))
    wx = np.zeros((DI, 66), f)
    for at, rows in ((0, slice(0, NS)), (32, slice(NS, 2 * NS)), (64, slice(2 * NS, 2 * NS + 1))):
        wx[:, at:at + rows.stop - rows.start] = a["a_W_x"].T[:, rows]
    return {
        "x": c(a["a_x"].reshape(T, DM)), "WinT": c(a["a_W_in"].T), "convw": c(a["a_conv_w"].reshape(DI, 4)),
        "convb": col(a["a_conv_b"]), "WxT": wx, "Alog": c(a["a_A_log"]), "dtb": col(a["a_dt_bias"]),
        "outWT": c(a["a_out_W"].T), "Dp": col(a["a_D"]), "ln1": col(a["f_ln1_w"]), "ln2": col(a["f_ln2_w"]),
        "WqT": c(a["f_Wq"].T), "WkT": c(a["f_Wk"].T), "Wv": c(a["f_Wv"]), "Wo": c(a["f_Wo"]), "Aw": c(a["f_A"]),
        "Bw": c(a["f_B"]), "WgT": tiled(a["f_W_in_base"]), "WuT": tiled(a["f_W_up_base"]), "WdT": c(a["f_W_down"].T),
        "ident": np.eye(128, dtype=f), "maskt": np.where(j <= i, 0.0, NEG).astype(f),
        "maskT": np.where(j >= i, 0.0, NEG).astype(f),
        "arow": c(a["a_A_log"][0].reshape(NS, 1)), "umask": np.stack([j > i, j >= i], 1).astype(f),
    }


def kernel(**inputs):
    from concourse import bacc
    from concourse.bass_utils import run_bass_kernel_spmd

    arrays = layout(inputs)
    nc = bacc.Bacc("TRN2", target_bir_lowering=False, num_devices=1, dynamic_dma_scratch_size=1024)
    feeds, args = {}, {}
    for name, a in arrays.items():
        feeds[f"in_{name}_dram"] = a
        args[name] = nc.dram_tensor(f"in_{name}_dram", a.shape, mybir.dt.from_np(a.dtype), kind="ExternalInput").ap()
    args["out"] = nc.dram_tensor("out_0_dram", (T, DM), F32, kind="ExternalOutput").ap()
    build(nc, **args)
    r = run_bass_kernel_spmd(nc, [feeds], core_ids=[0])
    return r.results[0]["out_0_dram"].reshape(NB, S, DM)
```

```python
from contextlib import ExitStack

import numpy as np

import concourse.bass as bass
from concourse import mybir

F32 = mybir.dt.float32
F32R = mybir.dt.float32r
BF16 = mybir.dt.bfloat16
F16 = mybir.dt.float16
ALU = mybir.AluOpType
ACT = mybir.ActivationFunctionType
AX = mybir.AxisListType

NB, S, DM, DI, NS, FF, NH, HD, R = 8, 512, 512, 1024, 16, 2048, 16, 32, 16
T = NB * S
NEG = -1.0e30


class Queue:

    def __init__(self, sem):
        self.sem, self.ops = sem, []

    def add(self, fn, waits):
        tok = Token(self, len(self.ops))
        for w in waits:
            w.wanted()
        self.ops.append([fn, waits, False, None])
        return tok

    def count(self):
        n = 0
        for op in self.ops:
            n += op[2]
            op[3] = n

    def emit(self, eng):
        seen = {}
        for fn, waits, marked, _ in self.ops:
            for w in waits:
                sem, value = w.value()
                if seen.get(id(sem), 0) < value:
                    eng.wait_ge(sem, value)
                    seen[id(sem)] = value
            ins = fn(eng)
            if marked:
                ins.then_inc(self.sem, 1)


class Token:
    def __init__(self, queue, at):
        self.queue, self.at = queue, at

    def wanted(self):
        self.queue.ops[self.at][2] = True

    def value(self):
        return self.queue.sem, self.queue.ops[self.at][3]


class Landed:

    def __init__(self, sem, n):
        self.sem, self.n = sem, n

    def wanted(self):
        pass

    def value(self):
        return self.sem, self.n


class Sem:
    def __init__(self, handle):
        self.handle, self.n = handle, 0


def build(nc, x, WinT, convw, convb, WxT, Alog, dtb, outWT, Dp, ln1, ln2, WqT, WkT, Wv, Wo, Aw, Bw, WgT, WuT, WdT,
          ident, umask, arow, maskt, maskT, out):
    ctx = ExitStack()
    with ctx:
        def sem(name):
            return ctx.enter_context(nc.semaphore(name))

        class Part:

            def __init__(self, name):
                self.pe, self.act, self.dve, self.pool, self.sp = (
                    Queue(sem(f"{name}_{n}")) for n in ("pe", "act", "dve", "pool", "sp"))

            def queues(self):
                return [self.pe, self.act, self.dve, self.pool, self.sp]

        now = [None]

        def part(name):
            now[0] = Part(name)
            for i in range(8):
                free[i] = []
            turn.clear()
            return now[0]

        def dma(s, dst, src, *waits):
            dst, src = (v.bitcast(F32) if v.dtype == F32R else v for v in (dst, src))
            s.n += 16
            n = s.n

            def go(e):
                e.dma_start(dst, src).then_inc(s.handle, 16)
            for w in waits:
                w.wanted()
            now[0].sp.ops.append([go, list(waits), False, None])
            return Landed(s.handle, n)

        def mm(o, l, r, a, z, *waits):
            return now[0].pe.add(lambda e: e.matmul(o, l, r, start=a, stop=z, skip_group_check=True), list(waits))

        def tr(o, i, idt, *waits):
            return now[0].pe.add(lambda e: e.transpose(o, i, idt), list(waits))

        def activate(o, i, f, *waits, bias=0.0, scale=1.0):
            return now[0].act.add(lambda e: e.activation(o, i, f, bias=bias, scale=scale), list(waits))

        def acopy(o, i, *waits):
            return now[0].act.add(lambda e: e.copy(o, i), list(waits))

        def tt(o, a, b, op, *waits, q=None):
            return (q or now[0].dve).add(lambda e: e.tensor_tensor(o, a, b, op), list(waits))

        def ts(o, a, s1, s2, op0, op1, *waits, q=None):
            if s2 is None:
                return (q or now[0].dve).add(lambda e: e.tensor_scalar(o, a, s1, None, op0), list(waits))
            return (q or now[0].dve).add(lambda e: e.tensor_scalar(o, a, s1, s2, op0, op1), list(waits))

        def stt(o, a, s, b, op0, op1, *waits):
            return now[0].dve.add(lambda e: e.scalar_tensor_tensor(out=o, in0=a, scalar=s, in1=b, op0=op0, op1=op1), list(waits))

        def vcopy(o, i, *waits, q=None):
            return (q or now[0].dve).add(lambda e: e.tensor_copy(o, i), list(waits))

        def total(o, i, op, axis, *waits):
            return now[0].dve.add(lambda e: e.tensor_reduce(o, i, axis, op), list(waits))

        def recip(o, i, *waits):
            return now[0].dve.add(lambda e: e.reciprocal(o, i), list(waits))

        def bn_stats(o, i, *waits):
            return now[0].dve.add(lambda e: e.bn_stats(o, i), list(waits))

        def bn_aggr(o, i, *waits):
            return now[0].dve.add(lambda e: e.bn_aggr(o, i), list(waits))

        def scan(o, a, b, *waits):
            return now[0].dve.add(lambda e: e.tensor_tensor_scan(o, a, b, 0.0, ALU.mult, ALU.add), list(waits))

        def fill(o, v, *waits, q=None):
            o = o.bitcast(F32) if o.dtype == F32R else o
            return (q or now[0].dve).add(lambda e: e.memset(o, v), list(waits))

        def sbp(c, name, shape, dt):
            return c.enter_context(nc.sbuf_tensor(name, shape, dt))

        PS = [ctx.enter_context(nc.psum_tensor(f"PS{i}", [128, 512], F32)) for i in range(8)]
        free = [[] for _ in range(8)]
        turn = {}

        def bank(group):
            k = turn.get(group, 0)
            turn[group] = k + 1
            i = group[k % len(group)]
            return i, PS[i], free[i]

        def drains(i, *toks):
            free[i] = list(toks)

        rh_d = nc.dram_tensor("rh_scratch", [NB, 128, 4, S], F32R, kind="Internal").ap()
        rl_d = nc.dram_tensor("rl_scratch", [NB, 128, 4, S], F32R, kind="Internal").ap()
        s_d = nc.dram_tensor("s_scratch", [T, DM], F32, kind="Internal").ap()
        m_d = nc.dram_tensor("m_scratch", [T, DM], F32, kind="Internal").ap()

        idn = sbp(ctx, "idn", [128, 128], F32)
        idr = sbp(ctx, "idr", [128, 128], F32R)
        UM = sbp(ctx, "UM", [128, 2, 128], F32)
        MEAN = sbp(ctx, "MEAN", [128, 32], F32)
        RSTD = sbp(ctx, "RSTD", [128, 32], F32)
        RMS = sbp(ctx, "RMS", [128, 32], F32)
        FLAG = sbp(ctx, "FLAG", [1, 1], mybir.dt.int32)
        joined = sem("joined")
        s_c = Sem(sem("s_c"))
        MHALF = sbp(ctx, "MHALF", [128, 4], F32)

        first = part("first")
        p0 = ExitStack()
        AL = sbp(p0, "AL", [128, 8, NS], F32)
        AR = sbp(p0, "AR", [128, NS], F32)
        NE = sbp(p0, "NE", [128, 2], F32)
        dma(s_c, idn[:, :], ident)
        dma(s_c, UM[:, :, :], umask)
        dma(s_c, AL[:, :, :], Alog.rearrange("(k p) j -> p k j", p=128))
        ld = dma(s_c, AR[:, :], Alog[0:1, :].to_broadcast([128, NS]))
        t_idr = vcopy(idr[:, :], idn[:, :], ld)
        t_mh = fill(MHALF[:, :], -0.5)
        v1 = fill(NE[:, 1:2], 1.0)
        v = tt(AL[:, :, :], AL[:, :, :], AR[:, :].unsqueeze(1).to_broadcast([128, 8, NS]), ALU.not_equal, ld)
        v = total(NE[:, 0:1], AL[:, :, :], ALU.max, AX.XY, v)
        t = mm(PS[0][0:1, 0:1], NE[:, 0:1], NE[:, 1:2], True, True, v, v1)
        t_flag = vcopy(FLAG[:, :], PS[0][0:1, 0:1], t)
        t_flag.wanted()
        p0.close()
        consts = [t_idr, t_mh, t_flag, ld]

        class Stage:

            def __init__(self, slots, name):
                self.slots, self.n = slots, 0
                self.sems = [Sem(sem(f"{name}{i}")) for i in range(len(slots))]
                self.free = [[] for _ in slots]

            def load(self, src, n, *waits):
                i = self.n % len(self.slots)
                self.n += 1
                dst = self.slots[i][:, 0:n]
                if len(src.shape) == 3:
                    dst = dst.rearrange("p (k m) -> p k m", k=src.shape[1])
                return i, dma(self.sems[i], dst, src, *self.free[i], *waits)

        def split(hi, lo, w, *waits, q=None):
            a = acopy(hi, w, *waits)
            return [a, tt(lo, w, hi.bitcast(F32), ALU.subtract, a, q=q)]

        def split_weights(stage, src, n, hi, lo, *waits):
            i, d = stage.load(src, n, *waits)
            stage.free[i] = split(hi, lo, stage.slots[i][:, 0:n], d)
            return stage.free[i]

        def three(pt, lh, ll, xh, xl, nk, waits, close=True):
            n, first = 3 * nk, True
            t = None
            for k in range(nk):
                for a, b in ((lh, xh), (lh, xl), (ll, xh)):
                    n -= 1
                    t = mm(pt, a(k), b(k), first, close and n == 0, *(waits if first else []))
                    first = False
            return t

        def stats(X, k, n, BST, AGG, VT, *waits):
            v = bn_stats(BST[:, :], X, *waits)
            v = bn_aggr(AGG[:, :], BST[:, :], v)
            t1 = vcopy(MEAN[:, n:n + 1], AGG[:, 0:1], v)
            t2 = ts(VT[:, 0:1], AGG[:, 1:2], 1e-5, None, ALU.add, None, v)
            pool = now[0].pool
            t3 = tt(RSTD[:, n:n + 1], VT[:, 0:1], MHALF[:, 0:1], ALU.pow, t2, *consts, q=pool)
            t4 = tt(VT[:, 1:2], RSTD[:, n:n + 1], RSTD[:, n:n + 1], ALU.mult, t3)
            t4 = stt(VT[:, 2:3], VT[:, 1:2], AGG[:, 1:2], VT[:, 3:4], ALU.mult, ALU.add, t4)
            t5 = tt(VT[:, 1:2], VT[:, 2:3], MHALF[:, 0:1], ALU.pow, t4, q=pool)
            t6 = tt(RMS[:, n:n + 1], VT[:, 1:2], RSTD[:, n:n + 1], ALU.mult, t5)
            return [t1, t3], t6

        general = part("gen")
        p1 = ExitStack()
        WH = sbp(p1, "g_WH", [128, 4, 2048], F32R)
        WL = sbp(p1, "g_WL", [128, 4, 2048], F32R)
        OH = sbp(p1, "g_OH", [128, 8, 512], F32R)
        OL = sbp(p1, "g_OL", [128, 8, 512], F32R)
        XPH = sbp(p1, "g_XPH", [128, 8, 66], F32R)
        XPL = sbp(p1, "g_XPL", [128, 8, 66], F32R)
        XH = sbp(p1, "g_XH", [128, 4, S], F32R)
        XL = sbp(p1, "g_XL", [128, 4, S], F32R)
        CH = sbp(p1, "g_CH", [128, 8, S], F32R)
        CL = sbp(p1, "g_CL", [128, 8, S], F32R)
        stage = Stage([sbp(p1, f"g_STG{i}", [128, 2048], F32) for i in range(2)], "g_st")
        STG = stage.slots
        XC = sbp(p1, "g_XC", [128, 8, S], F32)
        ZS = sbp(p1, "g_ZS", [128, 8, S], F32)
        DT = sbp(p1, "g_DT", [128, S], F32)
        AB = sbp(p1, "g_AB", [128, S], F32)
        U = sbp(p1, "g_U", [128, S], F32)
        ACC = sbp(p1, "g_ACC", [128, S], F32)
        PPH = sbp(p1, "g_PPH", [65, S], F32R)
        PPL = sbp(p1, "g_PPL", [65, S], F32R)
        CW = sbp(p1, "g_CW", [128, 8, 4], F32)
        CB = sbp(p1, "g_CB", [128, 8], F32)
        AC = sbp(p1, "g_AC", [128, 8, NS], F32)
        DC = sbp(p1, "g_DC", [128, 8], F32)
        DB = sbp(p1, "g_DB", [128, 8], F32)
        ONE = sbp(p1, "g_ONE", [128, 128], F32)
        MB = sbp(p1, "g_MB", [128, 2], F32)
        BST = sbp(p1, "g_BST", [128, 6], F32)
        AGG = sbp(p1, "g_AGG", [128, 2], F32)
        VT = sbp(p1, "g_VT", [128, 4], F32)

        s_w = Sem(sem("g_w"))
        lw = [dma(s_w, CW[:, :, :], convw.rearrange("(k p) j -> p k j", p=128)),
              dma(s_w, CB[:, :], convb),
              dma(s_w, AC[:, :, :], Alog.rearrange("(k p) j -> p k j", p=128)),
              dma(s_w, DC[:, :], Dp),
              dma(s_w, DB[:, :], dtb)][-1]

        t_w = []
        wv_ = WinT.rearrange("(k p) n -> p k n", p=128)
        for k in range(4):
            t_w += split_weights(stage, wv_[:, k, :], 2048, WH[:, k, :], WL[:, k, :])
        t_o = []
        ov_ = outWT.rearrange("(k p) n -> p k n", p=128)
        for k in range(2):
            t_o += split_weights(stage, ov_[:, 4 * k:4 * k + 4, :], 2048,
                                 OH[:, 4 * k:4 * k + 4, :].rearrange("p k n -> p (k n)"),
                                 OL[:, 4 * k:4 * k + 4, :].rearrange("p k n -> p (k n)"))
        t_p = split_weights(stage, WxT.rearrange("(k p) n -> p k n", p=128), 8 * 66,
                            XPH[:, :, :].rearrange("p k n -> p (k n)"), XPL[:, :, :].rearrange("p k n -> p (k n)"))
        e0 = activate(AC[:, :, :], AC[:, :, :], ACT.Exp, lw)
        t_ac = ts(AC[:, :, :], AC[:, :, :], -1.0, None, ALU.mult, None, e0)
        t_one = fill(ONE[:, :], 1.0 / DI)
        t_vt = fill(VT[:, 3:4], 1e-6)
        r0 = total(MB[:, 0:1], DB[:, :], ALU.add, AX.X, lw)
        i, p, w0 = bank((0, 1))
        m0 = mm(p[:, 0:1], ONE[:, :], MB[:, 0:1], True, True, r0, t_one, *w0)
        t_mb = vcopy(MB[:, 1:2], p[:, 0:1], m0)
        drains(i, t_mb)

        xv = x.rearrange("(b k p) d -> b p k d", k=4, p=128)
        G_T, G_W, G_O = (0, 1), (2, 3, 4), (7,)
        done_xh, done_c, done_xc, done_zs, done_pp, done_dt = [], [[] for _ in range(8)], [], [], [], []
        acc_free, h_free = [], []
        for b in range(NB):
            sl, dx = stage.load(xv[b], 2048)
            X = STG[sl][:, :].rearrange("p (k d) -> p k d", k=4)
            xn, t6 = [], t_vt
            for k in range(4):
                n = 4 * b + k
                two, t6 = stats(X[:, k, :], k, n, BST, AGG, VT, dx, t6)
                xn.append(ts(X[:, k, :], X[:, k, :], MEAN[:, n:n + 1], RSTD[:, n:n + 1], ALU.subtract, ALU.mult, *two))
            xs = []
            for d in range(4):
                i, p, w = bank(G_T)
                for k in range(4):
                    t = tr(p[:, 128 * k:128 * k + 128], X[:, k, 128 * d:128 * d + 128], idn[:, :], xn[k], *consts, *w)
                a = acopy(XH[:, d, :], p[:, :], t, *done_xh)
                v = tt(XL[:, d, :], p[:, :], XH[:, d, :].bitcast(F32), ALU.subtract, a)
                drains(i, v)
                xs += [a, v]
            x_free = [t]
            done_xh = []
            cs = []
            for m in range(16):
                i, p, w = bank(G_W)
                t = three(p[:, :], lambda k: WH[:, k, 128 * m:128 * m + 128], lambda k: WL[:, k, 128 * m:128 * m + 128],
                          lambda k: XH[:, k, :], lambda k: XL[:, k, :], 4, [*w, *xs, *t_w])
                if m < 8:
                    y = XC[:, m, :]
                    a = activate(y, p[:, :], ACT.Identity, t, lw, *done_xc, bias=CB[:, m:m + 1], scale=CW[:, m, 3:4])
                    for j in range(1, 4):
                        a = stt(y[:, j:], p[:, 0:S - j], CW[:, m, 3 - j:4 - j], y[:, j:], ALU.mult, ALU.add, a)
                    drains(i, a)
                    a = activate(y, y, ACT.Silu, a)
                    h = acopy(CH[:, m, :], y, a, *done_c[m])
                    l = tt(CL[:, m, :], y, CH[:, m, :].bitcast(F32), ALU.subtract, h)
                    cs += [h, l]
                else:
                    a = activate(ZS[:, m - 8, :], p[:, :], ACT.Silu, t, *done_zs)
                    drains(i, a)
                    zs = a
            done_xh = [t]
            i, p, w = bank(G_T)
            t = three(p[0:65, :], lambda k: XPH[:, k, 0:65], lambda k: XPL[:, k, 0:65],
                      lambda k: CH[:, k, :], lambda k: CL[:, k, :], 8, [*w, *cs, *t_p])
            pp = split(PPH[:, :], PPL[:, :], p[0:65, :], t, *done_pp)
            drains(i, pp[1])

            def spread(p, q, *waits):
                one = idr[0:65, q:q + 1].to_broadcast([65, 128])
                mm(p[:, :], one, PPH[:, :], True, False, *pp, *consts, *waits)
                return mm(p[:, :], one, PPL[:, :], False, True)

            i, p, w = bank(G_T)
            t = spread(p, 64, *w)
            a0 = activate(U[:, :], p[:, :], ACT.Abs, t, t_mb, *h_free, bias=MB[:, 1:2])
            r = activate(DT[:, :], p[:, :], ACT.Relu, t, *done_dt, bias=MB[:, 1:2])
            drains(i, r)
            a0 = activate(U[:, :], U[:, :], ACT.Exp, a0, scale=-1.0)
            v = ts(ACC[:, :], U[:, :], 1.0, None, ALU.add, None, a0, *acc_free)
            lnu = activate(AB[:, :], ACC[:, :], ACT.Ln, v)
            v = ts(ACC[:, :], ACC[:, :], -1.0, None, ALU.add, None, v, lnu)
            v = tt(U[:, :], U[:, :], ACC[:, :], ALU.subtract, v)
            v = tt(U[:, :], U[:, :], AB[:, :], ALU.add, v, lnu)
            dtk = tt(DT[:, :], DT[:, :], U[:, :], ALU.add, v, r)
            ab_free = [dtk]
            ys = []
            for d in range(8):
                X1 = XC[:, d, :]
                v = ts(ACC[:, :], X1, DC[:, d:d + 1], None, ALU.mult, None, lw, *acc_free, cs[-1], cs[2 * d])
                v = tt(X1, X1, DT[:, :], ALU.mult, v, dtk, cs[2 * d], cs[2 * d + 1])
                for s in range(NS):
                    ib, pb, wb = bank((5, 6))
                    tb = spread(pb, s, *wb)
                    ic, pc, wc = bank((2, 3))
                    tc = spread(pc, 32 + s, *wc)
                    ea = activate(AB[:, :], DT[:, :], ACT.Exp, dtk, t_ac, *ab_free, scale=AC[:, d, s:s + 1])
                    v = tt(U[:, :], X1, pb[:, :], ALU.mult, tb, v)
                    drains(ib, v)
                    v = scan(AB[:, :], AB[:, :], U[:, :], ea, v)
                    v = tt(AB[:, :], AB[:, :], pc[:, :], ALU.mult, v, tc)
                    drains(ic, v)
                    v = tt(ACC[:, :], ACC[:, :], AB[:, :], ALU.add, v)
                    ab_free = [v]
                v = tt(ACC[:, :], ACC[:, :], ZS[:, d, :], ALU.mult, v, zs)
                a = acopy(CH[:, d, :], ACC[:, :], v, t)
                l = tt(CL[:, d, :], ACC[:, :], CH[:, d, :].bitcast(F32), ALU.subtract, a)
                acc_free = [l, a]
                ys += [a, l]
            done_xc, done_zs, done_dt, done_pp, h_free = [v], [v], [v, ea], [tc], [l]
            so = []
            for k in range(4):
                i, p, w = bank(G_O)
                t = three(p[:, :], lambda q: CH[:, q, 128 * k:128 * k + 128], lambda q: CL[:, q, 128 * k:128 * k + 128],
                          lambda q: OH[:, q, :], lambda q: OL[:, q, :], 8, [*w, *ys, *t_o])
                a = acopy(X[:, k, :], p[:, :], t, *x_free)
                drains(i, a)
                so.append(a)
            for m in range(8):
                done_c[m] = [t]
            ds = dma(stage.sems[sl], s_d.rearrange("(b k p) d -> b p k d", k=4, p=128)[b], X, *so)
            stage.free[sl] = [ds]
        g_ends = [Landed(q.handle, q.n) for q in stage.sems]
        for q in general.queues()[:4]:
            q.ops[-1][2] = True
        p1.close()

        fast = part("fast")
        p1 = ExitStack()
        WH = sbp(p1, "WH", [128, 4, 2048], F32R)
        WL = sbp(p1, "WL", [128, 4, 2048], F32R)
        OH = sbp(p1, "OH", [128, 8, 512], F32R)
        OL = sbp(p1, "OL", [128, 8, 512], F32R)
        XPH = sbp(p1, "XPH", [128, 8, 66], F32R)
        XPL = sbp(p1, "XPL", [128, 8, 66], F32R)
        XH = sbp(p1, "XH", [128, 4, S], F32R)
        XL = sbp(p1, "XL", [128, 4, S], F32R)
        XC = sbp(p1, "XC", [128, 8, S], F32)
        ZS = sbp(p1, "ZS", [128, 8, S], F32)
        CW = sbp(p1, "CW", [128, 8, 4], F32)
        CB = sbp(p1, "CB", [128, 8], F32)
        DC = sbp(p1, "DC", [128, 8], F32)
        DB = sbp(p1, "DB", [128, 8], F32)
        AB_ = sbp(p1, "AB_", [128, NS], F32)
        A16 = sbp(p1, "A16", [NS, 1], F32)
        ONE = sbp(p1, "ONE", [128, 128], F32)
        ONE2 = sbp(p1, "ONE2", [NS, 1], F32)
        MB = sbp(p1, "MB", [128, 2], F32)
        BST = sbp(p1, "BST", [128, 4, 6], F32)
        AGG = sbp(p1, "AGG", [128, 4, 2], F32)
        VT = sbp(p1, "VT", [128, 3, 4], F32)

        pw = ExitStack()
        wst = Stage([sbp(pw, f"WST{i}", [128, 2048], F32) for i in range(3)], "f_ws")
        s_w = Sem(sem("f_w"))
        dma(s_w, CW[:, :, :], convw.rearrange("(k p) j -> p k j", p=128))
        dma(s_w, CB[:, :], convb)
        dma(s_w, AB_[:, :], Alog[0:1, :].to_broadcast([128, NS]))
        dma(s_w, A16[:, :], arow)
        dma(s_w, DC[:, :], Dp)
        lw = dma(s_w, DB[:, :], dtb)
        t_w = []
        wv_ = WinT.rearrange("(k p) n -> p k n", p=128)
        for k in range(4):
            t_w += split_weights(wst, wv_[:, k, :], 2048, WH[:, k, :], WL[:, k, :])
        t_p = split_weights(wst, WxT.rearrange("(k p) n -> p k n", p=128), 8 * 66,
                            XPH[:, :, :].rearrange("p k n -> p (k n)"), XPL[:, :, :].rearrange("p k n -> p (k n)"))
        t_o = []
        ov_ = outWT.rearrange("(k p) n -> p k n", p=128)
        for k in range(2):
            t_o += split_weights(wst, ov_[:, 4 * k:4 * k + 4, :], 2048,
                                 OH[:, 4 * k:4 * k + 4, :].rearrange("p k n -> p (k n)"),
                                 OL[:, 4 * k:4 * k + 4, :].rearrange("p k n -> p (k n)"))
        laid = t_w + t_p + t_o
        pw.close()
        XT = Stage([sbp(p1, f"XF{i}", [128, DM], F32) for i in range(4)], "f_x")
        XT.free = [list(laid) for _ in range(4)]
        CH = [sbp(p1, f"CH{i}", [128, S], F32R) for i in range(2)]
        CL = [sbp(p1, f"CL{i}", [128, S], F32R) for i in range(2)]
        YH = [sbp(p1, f"YH{i}", [128, S], F32R) for i in range(2)]
        YL = [sbp(p1, f"YL{i}", [128, S], F32R) for i in range(2)]
        NH_ = [sbp(p1, f"NH_{i}", [128, 4, 128], F32R) for i in range(2)]
        NL_ = [sbp(p1, f"NL_{i}", [128, 4, 128], F32R) for i in range(2)]
        TMP = sbp(p1, "TMP", [128, 2048], F32)
        DT = sbp(p1, "DT", [128, S], F32)
        DEL = sbp(p1, "DEL", [128, S], F32)
        MH = sbp(p1, "MH", [128, 4, S], F32R)
        ML = sbp(p1, "ML", [128, 4, S], F32R)
        PPH = sbp(p1, "PPH", [65, S], F32R)
        PPL = sbp(p1, "PPL", [65, S], F32R)
        CS = sbp(p1, "CS", [80, 768], F32R)
        BT = sbp(p1, "BT", [80, 384], F32R)
        BN = sbp(p1, "BN", [128, 3, NS], F32)
        PN = sbp(p1, "PN", [128, 4, 65], F32)
        DBN = sbp(p1, "DBN", [128, 4, NS], F32)
        KEEP = sbp(p1, "KEEP", [128, 1], F32)
        G = [TMP[:, 0:512], TMP[:, 512:1024], TMP[:, 1536:2048]]
        ACC, PF = TMP[:, 1024:1536], TMP[0:65, 1536:2048]
        CE, CF = TMP[0:NS, 0:768], TMP[0:NS, 1024:1536]
        jo = [0, 384, 640, 768]

        e0 = activate(AB_[:, :], AB_[:, :], ACT.Exp, lw)
        t_ab = ts(AB_[:, :], AB_[:, :], -1.0, None, ALU.mult, None, e0)
        e0 = activate(A16[:, :], A16[:, :], ACT.Exp, lw)
        t_a16 = ts(A16[:, :], A16[:, :], -1.0, None, ALU.mult, None, e0)
        t_one = fill(ONE[:, :], 1.0 / DI)
        t_one2 = fill(ONE2[:, :], 1.0)
        t_keep = fill(KEEP[:, :], 1.0)
        t_z = [fill(CS[:, :], 0.0, *laid), fill(BT[:, :], 0.0, *laid)]
        r0 = total(MB[:, 0:1], DB[:, :], ALU.add, AX.X, lw)
        i, p, w0 = bank((0,))
        m0 = mm(p[:, 0:1], ONE[:, :], MB[:, 0:1], True, True, r0, t_one, *w0)
        t_mb = vcopy(MB[:, 1:2], p[:, 0:1], m0)
        drains(i, t_mb)
        xt_ = x.rearrange("(n p) d -> n p d", p=128)
        so_ = s_d.rearrange("(b k p) d -> b p k d", k=4, p=128)
        s_so = Sem(sem("s_so"))

        tmp_free = list(laid)
        xh_free, xh_done = [], [None] * 4
        ch_free, yh_free, nh_free = [[*laid], [*laid]], [[*laid], [*laid]], [[*laid], [*laid]]
        xc_free, zs_free = [[] for _ in range(8)], [[] for _ in range(8)]
        m_free, dt_free, del_free, pp_free, cs_free, bt_free, bn_free, pn_free = ([*laid] for _ in range(8))
        x_in, x_norm, x_low, vt_free = [None] * 4, [], [], []
        p_bank = [None]

        def fetched(b):
            for k in range(4):
                x_in[k] = XT.load(xt_[4 * b + k], DM)[1]

        def deviations(b, step):
            c = slice(4 * b, 4 * b + 4)
            half = MHALF[:, 0:4]
            if step == 0:
                for k in range(4):
                    v = bn_stats(BST[:, k, :], XT.slots[k][:, :], x_in[k], *vt_free)
                    v = bn_aggr(AGG[:, k, :], BST[:, k, :], v, *vt_free)
                m = vcopy(MEAN[:, c], AGG[:, :, 0], v)
                v = ts(VT[:, 0, :], AGG[:, :, 1], 1e-5, None, ALU.add, None, v)
                x_norm[:] = [m, tt(RSTD[:, c], VT[:, 0, :], half, ALU.pow, v, *consts, q=fast.pool)]
            elif step == 1:
                v = tt(VT[:, 1, :], RSTD[:, c], RSTD[:, c], ALU.mult, *x_norm)
                v = tt(VT[:, 1, :], VT[:, 1, :], AGG[:, :, 1], ALU.mult, v)
                v = ts(VT[:, 1, :], VT[:, 1, :], 1e-6, None, ALU.add, None, v)
                vt_free[:] = [tt(VT[:, 2, :], VT[:, 1, :], half, ALU.pow, v, q=fast.pool)]
            else:
                vt_free[:] = [tt(RMS[:, c], VT[:, 2, :], RSTD[:, c], ALU.mult, *vt_free, *x_norm)]

        def normed(b, k):
            n, X = 4 * b + k, XT.slots[k][:, :]
            xn = ts(X, X, MEAN[:, n:n + 1], RSTD[:, n:n + 1], ALU.subtract, ALU.mult, *x_norm)
            i, p, w = bank((4,))
            for d in range(4):
                t = tr(p[:, 128 * d:128 * d + 128], X[:, 128 * d:128 * d + 128], idn[:, :], xn, *consts, *w)
            XT.free[k] = [t]
            p3 = p[:, :].rearrange("p (d t) -> p d t", d=4)
            x_low[:] = [k, i, p3, t]

        def normed_hi():
            k, i, p3, t = x_low
            c = slice(128 * k, 128 * k + 128)
            x_low[3] = acopy(XH[:, :, c], p3, t, *xh_free)

        def lowered():
            k, i, p3, a = x_low
            c = slice(128 * k, 128 * k + 128)
            xh_done[k] = [a, tt(XL[:, :, c], p3, XH[:, :, c].bitcast(F32), ALU.subtract, a, *xh_free)]
            drains(i, xh_done[k][1])

        def project(m, group):
            c = slice(128 * m, 128 * m + 128)
            i, p, w = bank(group)
            t = three(p[:, :], lambda k: WH[:, k, c], lambda k: WL[:, k, c], lambda k: XH[:, k, :], lambda k: XL[:, k, :], 4,
                      [*w, *sum(xh_done, []), *t_w])
            return i, p, t

        def conv(d, i, p, t):
            y, u = XC[:, d, :], d % 2
            a = activate(y, p[:, :], ACT.Identity, t, lw, *xc_free[d], bias=CB[:, d:d + 1], scale=CW[:, d, 3:4])
            for j in range(1, 4):
                a = stt(y[:, j:], p[:, 0:S - j], CW[:, d, 3 - j:4 - j], y[:, j:], ALU.mult, ALU.add, a)
            drains(i, a)
            a = activate(y, y, ACT.Silu, a)
            return a, split(CH[u][:, :], CL[u][:, :], y, a, *ch_free[u])

        def rows(d, cs):
            u = d % 2
            if d == 0:
                p_bank[0] = bank((5,))
            i, p, w = p_bank[0]
            for n, (l_, r_) in enumerate(((XPH, CH), (XPH, CL), (XPL, CH))):
                t = mm(p[0:65, :], l_[:, d, 0:65], r_[u][:, :], d == 0 and n == 0, d == 7 and n == 2, *cs, *t_p, *w)
            ch_free[u] = [t]
            return t

        fetched(0)
        for q in range(3):
            deviations(0, q)
        for k in range(4):
            normed(0, k)
            normed_hi()
            lowered()
        xcs = [None] * 8
        lag = None
        for d in range(8):
            xcs[d], cs = conv(d, *project(d, (0, 1)))
            if lag is not None:
                rows(*lag)
            lag = (d, cs)
        t_rows = rows(*lag)

        for b in range(NB):
            ib, pb, _ = p_bank[0]
            t_pf = acopy(PF, pb[0:65, :], t_rows, *tmp_free)
            pp = split(PPH[:, :], PPL[:, :], pb[0:65, :], t_rows, *pp_free)
            drains(ib, pp[1])

            def spread(p, q, *waits):
                one = idr[0:65, q:q + 1].to_broadcast([65, 128])
                mm(p[:, :], one, PPH[:, :], True, False, *pp, *consts, *waits)
                return mm(p[:, :], one, PPL[:, :], False, True)

            zs_done, gates = [None] * 8, []

            def gate(m):
                i, p, t = project(8 + m, (0, 1))
                gates.append((m, i, p, t))
                return t

            def gated():
                m, i, p, t = gates.pop(0)
                zs_done[m] = acopy(ZS[:, m, :], p[:, :], t, *zs_free[m])
                drains(i, zs_done[m])

            gate(0)
            i, p, w = bank((4,))
            t = spread(p, 64, *w)
            gate(1)
            e = activate(G[0], p[:, :], ACT.Abs, t, t_mb, *tmp_free, bias=MB[:, 1:2])
            r = activate(DT[:, :], p[:, :], ACT.Relu, t, *dt_free, bias=MB[:, 1:2])
            drains(i, r)
            gated()
            gate(2)
            e = activate(G[0], G[0], ACT.Exp, e, scale=-1.0)
            v = ts(G[1], G[0], 1.0, None, ALU.add, None, e, *tmp_free)
            ln = activate(ACC, G[1], ACT.Ln, v, *tmp_free)
            gated()
            gate(3)
            v = ts(G[1], G[1], -1.0, None, ALU.add, None, v, ln)
            v = tt(G[0], G[0], G[1], ALU.subtract, v)
            v = tt(DT[:, :], DT[:, :], G[0], ALU.add, v, r)
            t_dt = tt(DT[:, :], DT[:, :], ACC, ALU.add, v, ln)
            v = tt(DEL[:, :].rearrange("p (c t) -> p c t", c=4), DT[:, :].rearrange("p (c t) -> p c t", c=4),
                   UM[:, 0, :].unsqueeze(1).to_broadcast([128, 4, 128]), ALU.mult, t_dt, *consts, *del_free)
            for k in range(4):
                c = slice(128 * k, 128 * k + 128)
                t_del = scan(DEL[:, c], KEEP[:, :].to_broadcast([128, 128]), DEL[:, c], v, t_keep)
            v = vcopy(PF[64:65, :], DT[64:65, :], t_dt, t_pf)
            i, p, w = bank((4,))
            for k in range(4):
                t = tr(p[:, 65 * k:65 * k + 65], PF[:, 128 * k:128 * k + 128], idn[0:65, 0:65], v, *w)
            t_pn = t
            a = acopy(PN[:, :, :], p[:, 0:260].rearrange("p (k q) -> p k q", k=4), t, *pn_free)
            drains(i, a)
            for k in range(4):
                dbn = ts(DBN[:, k, :], PN[:, k, 0:NS], PN[:, k, 64:65], None, ALU.mult, None, a, *pn_free)
            gated()
            gate(4)
            bn = []
            for J in range(3):
                c = activate(BN[:, J, :], AB_[:, :], ACT.Exp, t_del, t_ab, *bn_free, scale=DEL[:, 128 * J + 127:128 * J + 128])
                bn.append(c)
            v = tt(BN[:, :, :], BN[:, :, :], DBN[:, 0:3, :], ALU.mult, c, dbn)
            i, p, w = bank((4,))
            for J in range(3):
                t = tr(p[0:NS, 128 * J:128 * J + 128], BN[:, J, :], idn[:, :], v, *w)
            bn_free = [t]
            gated()
            gate(5)
            bt = [acopy(BT[64:64 + NS, :], p[0:NS, 0:384], t, *bt_free, *t_z)]
            bt += split(BT[0:NS, :], BT[32:32 + NS, :], p[0:NS, 0:384])
            drains(i, bt[-1])
            dj = []
            for J in range(3):
                n = 384 - 128 * J
                dj.append(scan(CE[:, jo[J]:jo[J + 1]], ONE2[:, :].to_broadcast([NS, n]), DT[0:NS, 512 - n:512], t_dt, t_one2, v))
            t_cf = acopy(CF, PF[32:32 + NS, :], t_pf, t_dt)
            c = activate(CE, CE, ACT.Exp, dj[-1], t_a16, scale=A16[:, 0:1])
            for J in range(3):
                n = 384 - 128 * J
                v = tt(CE[:, jo[J]:jo[J + 1]], CE[:, jo[J]:jo[J + 1]], CF[:, 512 - n:512], ALU.mult, c, t_cf)
            cs = [acopy(CS[0:NS, :], CE, v, *cs_free, *t_z), acopy(CS[32:32 + NS, :], CE)]
            cs.append(tt(CS[64:64 + NS, :], CE, CS[0:NS, :].bitcast(F32), ALU.subtract, cs[0]))
            t_tmp = [*cs, t_cf, t_pn]
            spans = [(bank((6,)), 0), (bank((7,)), 0), None]
            spans[2] = (spans[1][0], 256)
            off_ = []
            for J in range(3):
                (i, p, w), at = spans[J]
                n = 384 - 128 * J
                t = mm(p[:, at:at + n], BT[:, 128 * J:128 * J + 128], CS[:, jo[J]:jo[J + 1]], True, True, *bt, *cs, *w)
            for J in range(3):
                (i, p, w), at = spans[J]
                n = 384 - 128 * J
                mo = split(MH[:, J, 128:128 + n], ML[:, J, 128:128 + n], p[:, at:at + n], t, *m_free, *off_[-1:])
                drains(i, mo[1])
                off_ += mo
            bt_free = cs_free = [t]
            g_free = [[*t_tmp] for _ in range(3)]
            v, ahead = None, []

            def spread_out(s):
                i, p, w = bank((2, 3))
                ahead.append((i, p, spread(p, 32 + s, *w)))

            spread_out(0)
            for s in range(NS):
                u = s % 3
                i, p, t = ahead.pop(0)
                if s + 1 < NS:
                    spread_out(s + 1)
                a = activate(G[u], DEL[:, :], ACT.Exp, t_del, t_ab, *g_free[u], scale=AB_[:, s:s + 1])
                if s in (0, 1, 3, 5):
                    gated()
                if s in (0, 2):
                    xh_free = [gate(6 + s // 2)]
                if b + 1 < NB and s >= 9 and s % 2:
                    normed_hi()
                o = ACC if s == 0 else G[u]
                for k in range(4):
                    c = slice(128 * k, 128 * k + 128)
                    g = stt(o[:, c], G[u][:, c], DBN[:, k, s:s + 1], p[:, c], ALU.mult, ALU.mult, a, t, dbn, *t_tmp)
                drains(i, g)
                v = g if s == 0 else tt(ACC, ACC, G[u], ALU.add, g, v, q=fast.pool)
                g_free[u] = [v]
                if b + 1 < NB:
                    if s == 0:
                        fetched(b + 1)
                    if s in (5, 7, 9):
                        deviations(b + 1, (s - 5) // 2)
                    if s >= 8 and s % 2 == 0:
                        normed(b + 1, (s - 8) // 2)
                    elif s >= 8:
                        lowered()
            pp_free, del_free, dt_free, pn_free = [t], [a], [dj[-1], g], [g]
            A3 = ACC.rearrange("p (c t) -> p c t", c=4)
            v = tt(A3, A3, UM[:, 1, :].unsqueeze(1).to_broadcast([128, 4, 128]), ALU.mult, v)
            md = split(MH[:, :, 0:128], ML[:, :, 0:128], A3, v, *m_free)
            t_m = off_ + md
            tmp_free = [*md]
            outs = [bank((g,)) for g in (2, 3, 6, 7)]

            def turned(d):
                u = d % 2
                i, p, w = bank((4,))
                for k in range(4):
                    t = tr(p[:, 128 * k:128 * k + 128], XC[:, d, 128 * k:128 * k + 128], idn[:, :], xcs[d], *w)
                p3 = p[:, :].rearrange("p (k d) -> p k d", k=4)
                r = split(NH_[u][:, :, :], NL_[u][:, :, :], p3, t, *nh_free[u])
                drains(i, r[1])
                return t, r

            def project_out(d, ys):
                u = d % 2
                for k in range(4):
                    i, p, w = outs[k]
                    c = slice(128 * k, 128 * k + 128)
                    for n, (l_, r_) in enumerate(((YH, OH), (YH, OL), (YL, OH))):
                        t = mm(p[:, :], l_[u][:, c], r_[:, d, :], d == 0 and n == 0, d == 7 and n == 2, *ys, *t_o,
                               *(w if d == 0 else []))
                yh_free[u] = [t]
                return t

            nx = turned(0)
            lag_o = lag_r = None
            for d in range(8):
                u = d % 2
                t_x, xn_ = nx
                i, p, w = bank((1,))
                n = 0
                for J in range(4):
                    for l_, r_ in ((NH_, MH), (NH_, ML), (NL_, MH)):
                        n += 1
                        t = mm(p[:, 128 * J:512], l_[u][:, J, :], r_[:, J, 0:512 - 128 * J], n == 1, n == 12, *xn_, *t_m, *w)
                nh_free[u] = [t]
                X1 = XC[:, d, :]
                z = activate(ZS[:, d, :], ZS[:, d, :], ACT.Silu, zs_done[d])
                v = stt(X1, X1, DC[:, d:d + 1], p[:, :], ALU.mult, ALU.add, t, t_x, lw)
                drains(i, v)
                v = tt(X1, X1, ZS[:, d, :], ALU.mult, v, z)
                zs_free[d] = [v]
                ys = split(YH[u][:, :], YL[u][:, :], X1, v, *yh_free[u])
                xc_free[d] = ys
                if d < 7:
                    nx = turned(d + 1)
                if b + 1 < NB:
                    xcs[d], cs = conv(d, *project(d, (0,)))
                    if lag_r is not None:
                        rows(*lag_r)
                    lag_r = (d, cs)
                if lag_o is not None:
                    project_out(*lag_o)
                lag_o = (d, ys)
            m_free = [t]
            if b + 1 < NB:
                t_rows = rows(*lag_r)
            t = project_out(*lag_o)
            o_ = []
            for k in range(4):
                i, p, w = outs[k]
                o_.append(acopy(ZS[:, 4 + k, :], p[:, :], t, *zs_free[4 + k]))
                drains(i, o_[-1])
            st_ = dma(s_so, so_[b], ZS[:, 4:8, :], *o_)
            for k in range(4, 8):
                zs_free[k] = [st_]
        f_ends = [st_] + [Landed(q.handle, q.n) for q in XT.sems]
        for q in fast.queues()[:4]:
            q.ops[-1][2] = True
        p1.close()

        rest = part("rest")
        p2 = ExitStack()
        MS = sbp(p2, "MS", [80, T], F32R)
        BS = sbp(p2, "BS", [80, FF], F32R)
        L2C = sbp(p2, "L2C", [128, 4], F32)
        p2b = ExitStack()
        STGB = sbp(p2b, "STGB", [128, 2048], F32)
        QW = [sbp(p2b, f"QW{i}", [128, 4, 512], F32R) for i in range(4)]
        VW = [sbp(p2b, f"VW{i}", [128, 4, 256], F32R) for i in range(2)]
        AW = [sbp(p2b, f"AW{i}", [128, 4, R], F32R) for i in range(2)]
        QT = [[[sbp(p2b, f"QT{n}{u}{i}", [128, S], F32R) for i in range(2)] for u in range(2)] for n in range(2)]
        QS = sbp(p2b, "QS", [97, NH, S], F32R)
        KS = sbp(p2b, "KS", [97, NH, S], F32R)
        VB = [sbp(p2b, f"VB{i}", [128, 4, NH, 50], BF16) for i in range(2)]
        V1 = sbp(p2b, "V1", [128, 2, 256], F32)
        PF = [sbp(p2b, f"PF{i}", [128, 1280], F32) for i in range(2)]
        PH = [sbp(p2b, f"PH{i}", [128, 1280], F16) for i in range(2)]
        PL = [sbp(p2b, f"PL{i}", [128, 1280], F16) for i in range(2)]
        MX = [sbp(p2b, f"MX{i}", [128, 4, 4], F32) for i in range(2)]
        NM = [sbp(p2b, f"NM{i}", [4, S], F32R) for i in range(2)]
        HA = [sbp(p2b, f"HA{i}", [R, S], F32) for i in range(2)]
        TH = sbp(p2b, "TH", [R, S], F32)
        RD = sbp(p2b, "RD", [128, 16], F32)
        AM = sbp(p2b, "AM", [128, 4, R], F32)
        AM2 = sbp(p2b, "AM2", [128, 4, R], F32)
        MR = [sbp(p2b, f"MR{i}", [128, 128], BF16) for i in range(2)]
        idb = sbp(p2b, "idb", [128, 128], BF16)
        L1C = sbp(p2b, "L1C", [128, 4], F32)
        AF = sbp(p2b, "AF", [128, 4, R], F32)

        pw = ExitStack()
        stage = Stage([STGB] + [sbp(pw, f"STGA{i}", [128, 2048], F32) for i in range(2)], "a_st")
        MT = [sbp(pw, f"MT{i}", [128, 128], F32) for i in range(2)]
        WA_ = sbp(pw, "WA_", [128, 4, R], F32)
        BD = sbp(pw, "BD", [128, 4, 64], F32)
        stage.n = 1
        STG2 = stage.slots
        s_w2 = Sem(sem("s_w2"))
        dma(s_w2, MT[0][:, :], maskt, *stage.free[0])
        dma(s_w2, MT[1][:, :], maskT)
        dma(s_w2, L1C[:, :], ln1)
        dma(s_w2, L2C[:, :], ln2)
        lw2 = dma(s_w2, AF[:, :, :], Aw.rearrange("(k p) r -> p k r", p=128))
        t_mr = [vcopy(MR[i][:, :], MT[i][:, :], lw2) for i in range(2)] + [vcopy(idb[:, :], idn[:, :], *consts)]
        t_k1 = t_vb = fill(KS[96:97, :, :], 1.0, q=rest.pool)
        for V in VB:
            t_vb = fill(V[:, :, :, 48:50], 1.0, t_vb, q=rest.pool)
        t_ms = [fill(MS[:, :], 0.0, t_vb, q=rest.pool)]
        t_ms += [fill(BS[:, :], 0.0, *t_ms, q=rest.pool)]
        t_q = []

        def parts_of(n, i, d):
            w = STG2[i][:, :].rearrange("p (k n) -> p k n", k=4)
            l1b = L1C[:, :].unsqueeze(2).to_broadcast([128, 4, 512])
            t = tt(w, w, l1b, ALU.mult, d, lw2)
            stage.free[i] = split(QW[2 * n][:, :, :], QW[2 * n + 1][:, :, :], w, t)
            t_q.extend(stage.free[i])

        ld_o, ld_v, ld_q = (stage.load(src.rearrange("(k p) n -> p k n", p=128), 2048) for src in (Wo, Wv, WqT))
        i, d = ld_o
        w = STG2[i][:, :].rearrange("p (k n) -> p k n", k=4)
        z0 = fill(BD[:, :, :], 0.0)
        for e_ in range(4):
            ib, p, wb = bank((0, 1))
            for j in range(4):
                t = mm(p[:, 0:R], w[:, j, 128 * e_:128 * e_ + 128], AF[:, j, :], j == 0, j == 3, d, lw2, *wb)
            t = vcopy(WA_[:, e_, :], p[:, 0:R], t)
            drains(ib, t)
        stage.free[i] = [t]
        bd = []
        for e_ in range(4):
            for j in range(4):
                bd.append(vcopy(BD[32 * j:32 * j + 32, e_, R * j:R * j + R], WA_[32 * j:32 * j + 32, e_, :], z0, t))
        parts_of(0, *ld_q)
        i, d = ld_v
        w = STG2[i][:, :].rearrange("p (k n) -> p k n", k=4)
        t_v = []
        for k in range(4):
            ib, p, wb = bank((0, 1))
            for e_ in range(4):
                t = mm(p[:, 64 * e_:64 * e_ + 64], w[:, e_, 128 * k:128 * k + 128], BD[:, e_, :], True, True, d, *bd, *wb)
            v = ts(V1[:, 0, :], p[:, 0:256], L1C[:, k:k + 1], None, ALU.mult, None, t, lw2, *t_v[-2:])
            drains(ib, v)
            a = acopy(VW[0][:, k, :], V1[:, 0, :], v)
            l = tt(VW[1][:, k, :], V1[:, 0, :], VW[0][:, k, :].bitcast(F32), ALU.subtract, a)
            t_v += [a, l]
        stage.free[i] = [v]
        parts_of(1, *stage.load(WkT.rearrange("(k p) n -> p k n", p=128), 2048))
        t_a = []
        for k in range(4):
            t = ts(V1[:, 0, 16 * k:16 * k + 16], AF[:, k, :], L2C[:, k:k + 1], None, ALU.mult, None, lw2, *t_v[-2:])
            a = acopy(AW[0][:, k, :], V1[:, 0, 16 * k:16 * k + 16], t)
            l = tt(AW[1][:, k, :], V1[:, 0, 16 * k:16 * k + 16], AW[0][:, k, :].bitcast(F32), ALU.subtract, a)
            t_a += [a, l]
        i = 2
        d = dma(stage.sems[i], STG2[i][0:R, :], Bw, *stage.free[i])
        a = acopy(BS[0:16, :], STG2[i][0:R, :], d, *t_ms)
        a2 = acopy(BS[32:48, :], STG2[i][0:R, :], d)
        l = tt(BS[64:80, :], STG2[i][0:R, :], BS[0:16, :].bitcast(F32), ALU.subtract, a, t_ms[1])
        t_bs = [a2, l]
        stage.free[i] = [a2, l]

        pw.close()
        RH = [sbp(p2b, "RH", [128, 4, S], F32R)]
        RL = [sbp(p2b, "RL", [128, 4, S], F32R)]
        NU = sbp(p2b, "NU", [128, 16, R], F32)
        AO = sbp(p2b, "AO", [128, 800], F32)

        SC = 1.0 / float(np.sqrt(np.float32(HD)))
        off = [0, 512, 1024, 896]
        G_P, G_N, G_T, G_A = (0, 1), (2, 3), (4, 5), (6, 7)
        end1 = [Token(w, len(w.ops) - 1) for w in rest.queues()[:4] if w.ops]
        s_rst, s_xa = Sem(sem("s_rst")), stage.sems[0]
        s_qk = [[Sem(sem(f"s_qk{n}{r}")) for r in range(4)] for n in range(2)]
        s_nm = [Sem(sem(f"s_nm{r}")) for r in range(4)]
        x_free, xs, r_free, r_ready = [list(stage.free[0])], [None] * 4, [list(end1)], []
        slot_free, qt_free = [[] for _ in range(4)], [[[], []], [[], []]]
        pf_free, ph_free, vb_free = [list(end1), list(end1)], [[], []], [[], []]
        mx_free, nm_free, ha_free, am_free = [[], []], [[], []], [[], []], []
        v1_free, ao_free, nu_free, last_ms = [t_a[-2:], t_a[-2:]], list(end1), list(end1), []
        on_qk, on_nm, mx_ready, p_ready, vb_ready, ha_ready, x_ready, am_ready, pv_done = ({} for _ in range(9))
        pvs, over = [None, None], []
        rh, rl = (lambda k: RH[0][:, k, :]), (lambda k: RL[0][:, k, :])

        def fetch(b):
            x_ready[b] = dma(s_xa, STG2[0][:, :].rearrange("p (k d) -> p k d", k=4), xv[b], *x_free[0])

        def scaled(b, k):
            X, n = STG2[0][:, 512 * k:512 * k + 512], 4 * b + k
            xs[k] = ts(X, X, MEAN[:, n:n + 1], RMS[:, n:n + 1], ALU.subtract, ALU.mult, x_ready[b], q=rest.pool)

        def normal(b, ds):
            X = STG2[0][:, :].rearrange("p (k d) -> p k d", k=4)
            if ds[0] == 0:
                r_ready.clear()
            for d in ds:
                i, p, w = bank(G_P)
                for k in range(4):
                    t = tr(p[:, 128 * k:128 * k + 128], X[:, k, 128 * d:128 * d + 128], idn[:, :], xs[k], *w)
                r = split(RH[0][:, d, :], RL[0][:, d, :], p[:, :], t, *r_free[0])
                drains(i, r[1])
                r_ready.extend(r)
            if ds[-1] == 3:
                x_free[0] = [t]
                if b + 1 < NB:
                    fetch(b + 1)
                dma(s_rst, rh_d[b], RH[0][:, :, :], *r_ready)
                r_free[0] = [dma(s_rst, rl_d[b], RL[0][:, :, :])]

        def project(w, n):
            u, c = w % 2, slice(128 * (w % 4), 128 * (w % 4) + 128)
            i, p, wb = bank(G_P)
            t = three(p[:, :], lambda k: QW[2 * n][:, k, c], lambda k: QW[2 * n + 1][:, k, c], rh, rl, 4, [*wb, *r_ready, *t_q])
            pair = split(QT[n][u][0][:, :], QT[n][u][1][:, :], p[:, :], t, *qt_free[n][u])
            drains(i, pair[1])
            if n == 1 and w % 4 == 3:
                r_free[0] = r_free[0] + [t]
                over[:] = [t]
            return pair

        def stack(w, n, pair):
            r, u = w % 4, w % 2
            for slot in range(3):
                src = QT[n][u][slot == (1, 2)[n]]
                for j in range(4):
                    d = dma(s_qk[n][r], (QS, KS)[n][32 * slot:32 * slot + 32, 4 * r + j, :], src[32 * j:32 * j + 32, :], *pair,
                            *slot_free[r], *on_nm.get(w - 4, []))
            on_qk[w, n] = d
            qt_free[n][u] = [d]

        def values(b, js):
            for j in js:
                i, p, w = bank(G_P)
                c = slice(128 * j, 128 * j + 128)
                t = three(p[:, 0:256], lambda k: RH[0][:, k, c], lambda k: RL[0][:, k, c],
                          lambda k: VW[0][:, k, :], lambda k: VW[1][:, k, :], 4, [*w, *r_ready, *t_v])
                p3 = p[:, 0:256].rearrange("p (h r) -> p h r", r=R)
                v3 = V1[:, j % 2, :].rearrange("p (h r) -> p h r", r=R)
                V = VB[b % 2]
                a = acopy(V[:, j, :, 0:16], p3, t, *vb_free[b % 2])
                v = tt(v3, p3, V[:, j, :, 0:16], ALU.subtract, a, *v1_free[j % 2])
                drains(i, v)
                v2 = vcopy(V[:, j, :, 16:32], v3, v, q=rest.pool)
                v2 = tt(V[:, j, :, 32:48], v3, V[:, j, :, 16:32], ALU.subtract, v2, q=rest.pool)
                vb_ready.setdefault(b, []).extend([a, v2])
                v1_free[j % 2] = [v2]

        def low_rank(b):
            i, p, w = bank(G_P)
            t = three(p[0:R, :], lambda k: AW[0][:, k, :], lambda k: AW[1][:, k, :], rh, rl, 4, [*w, *r_ready, *t_a])
            ha_ready[b] = acopy(HA[b % 2][:, :], p[0:R, :], t, *ha_free[b % 2])
            drains(i, ha_ready[b])
            r_free[0] = r_free[0] + [t]

        def largest(g, ks):
            w, j = divmod(g, 4)
            h, u, at = 4 * (w % 4) + j, w % 2, 0
            i, p, wb = bank(G_N)
            spans = []
            for k in ks:
                n = 128 * k + 128
                mm(p[:, at:at + n], QS[0:96, h, 128 * k:n], KS[0:96, h, 0:n], True, False, *wb, on_qk[w, 0], on_qk[w, 1])
                t = mm(p[:, at + n - 128:at + n], idb[:, :], MR[0][:, :], False, True, *t_mr)
                spans.append((k, at, n))
                at += n
            for k, at, n in spans:
                v = total(MX[u][:, k, j:j + 1], p[:, at:at + n], ALU.max, AX.X, t, *mx_free[u])
            drains(i, v)
            mx_ready[w] = v

        def largest_in(w):
            u, r = w % 2, w % 4
            i, p, wb = bank(G_P)
            for k in range(4):
                t = tr(p[0:4, 128 * k:128 * k + 128], MX[u][:, k, :], idn[:, :], mx_ready[w], *wb)
            mx_free[u] = [t]
            a = activate(NM[u][:, :], p[0:4, :], ACT.Identity, t, *nm_free[u], scale=-1.0)
            drains(i, a)
            d = dma(s_nm[r], QS[96:97, 4 * r:4 * r + 4, :], NM[u][:, :], a, *slot_free[r])
            nm_free[u] = [d]
            on_nm[w] = [d]

        def weights(g, Js):
            w, j = divmod(g, 4)
            r, u, at = w % 4, g % 2, 0
            i, p, wb = bank(G_T)
            for J in Js:
                n = 512 - 128 * J
                mm(p[:, at:at + n], KS[0:97, 4 * r + j, 128 * J:128 * J + 128], QS[0:97, 4 * r + j, 128 * J:512], True, False, *wb,
                   *on_nm[w], on_qk[w, 0], on_qk[w, 1], t_k1)
                t = mm(p[:, at:at + 128], idb[:, :], MR[1][:, :], False, True, *t_mr)
                at += n
            o = off[Js[0]]
            a = activate(PF[u][:, o:o + at], p[:, 0:at], ACT.Exp, t, *pf_free[u], scale=SC)
            drains(i, a)
            if Js[-1] == 2:
                p_ready[g] = acopy(PH[u][:, :], PF[u][:, :], a, *ph_free[u])
                if j == 3:
                    slot_free[r] = [t]

        def remainder(g):
            u = g % 2
            p_ready[g] = pf_free[u] = [tt(PL[u][:, c], PF[u][:, c], PH[u][:, c], ALU.subtract, p_ready[g], *ph_free[u], q=q)
                                       for c, q in ((slice(0, 1024), rest.dve), (slice(1024, 1280), rest.pool))]

        def mixed(g):
            w, j = divmod(g, 4)
            b, u, h = w // 4, g % 2, g % 16
            if j == 0:
                pvs[:] = [bank(G_A), bank(G_A)]
            for k in range(4):
                i, p, wb = pvs[k // 2]
                c0 = 200 * (k % 2) + 50 * j
                for J in range(k + 1):
                    o = off[J] + 128 * (k - J)
                    for q, P_ in enumerate((PH[u], PL[u])):
                        t = mm(p[:, c0:c0 + 50], P_[:, o:o + 128], VB[b % 2][:, J, h, :], J == 0 and q == 0, J == k and q == 1,
                               *p_ready[g], *vb_ready[b], t_vb, *wb)
            ph_free[u] = [t]
            pv_done[w] = t

        def summed(w):
            b, t = w // 4, pv_done[w]
            for q in range(2):
                i, p, wb = pvs[q]
                a = acopy(AO[:, 400 * q:400 * q + 400], p[:, 0:400], t, *ao_free)
                drains(i, a)
            A3 = AO[:, :].rearrange("p (h c) -> p h c", c=50)
            n = tt(NU[:, :, :], A3[:, :, 0:16], A3[:, :, 16:32], ALU.add, a, *nu_free, q=rest.pool)
            n = tt(NU[:, :, :], NU[:, :, :], A3[:, :, 32:48], ALU.add, n, q=rest.pool)
            g = recip(RD[:, :], A3[:, :, 48], a, *nu_free)
            ao_free[:] = [n, g]
            v = tt(NU[:, :, :], NU[:, :, :], RD[:, :].unsqueeze(2).to_broadcast([128, 16, R]), ALU.mult, n, g)
            dst = AM2 if w % 4 else AM
            v = total(dst[:, :, :], NU[:, :, :].rearrange("p (k h) r -> p k r h", k=4), ALU.add, AX.X, v, *am_free)
            nu_free[:] = [v]
            if w % 4:
                v = tt(AM[:, :, :], AM[:, :, :], AM2[:, :, :], ALU.add, v)
            am_free[:] = am_ready[b] = [v]
            if w % 4 == 3:
                vb_free[b % 2] = [t]

        def modulation(b):
            i, p, w = bank(G_P)
            for k in range(4):
                t = tr(p[0:R, 128 * k:128 * k + 128], AM[:, k, :], idn[:, :], *am_ready[b], *w)
            am_free[:] = [t]
            a = activate(TH[:, :], p[0:R, :], ACT.Tanh, t, *last_ms)
            drains(i, a)
            v = stt(TH[:, :], TH[:, :], 0.1, HA[b % 2][:, :], ALU.mult, ALU.mult, a, ha_ready[b])
            ha_free[b % 2] = [v]
            c = slice(S * b, S * b + S)
            a = acopy(MS[0:16, c], TH[:, :], v, *t_ms)
            a2 = acopy(MS[64:80, c], TH[:, :], v)
            l = tt(MS[32:48, c], TH[:, :], MS[0:16, c].bitcast(F32), ALU.subtract, a)
            last_ms[:] = [a2, l]

        fetch(0)
        heads = NH * NB
        for g in range(-20, heads + 4):
            if (g + 15) % 16 == 0 and g + 15 < heads:
                normal((g + 15) // 16, (2, 3))
            for Js, ks in zip(((0,), (1, 3), (2,)), ((3,), (2, 0), (1,))):
                if 0 <= g < heads:
                    weights(g, Js)
                if 0 <= g + 6 < heads:
                    largest(g + 6, ks)
                if ks == (3,) and 0 <= g - 1 < heads:
                    remainder(g - 1)
            if g >= 5 and (g - 1) % 4 == 0:
                summed((g - 5) // 4)
            if (g + 2) % 4 == 0 and 0 <= g + 2 < heads:
                largest_in((g + 2) // 4)
            if (g + 20) % 16 < 4 and g + 20 < heads:
                scaled((g + 20) // 16, (g + 20) % 16)
            if (g + 16) % 16 == 0 and g + 16 < heads:
                normal((g + 16) // 16, (0, 1))
            if (g + 9) % 16 < 4 and 0 <= g + 9 < heads:
                values((g + 9) // 16, ((g + 9) % 16,))
            if (g + 5) % 16 == 0 and 0 <= g + 5 < heads:
                low_rank((g + 5) // 16)
            if (g + 15) % 4 == 0 and 0 <= g + 15 < heads:
                pair = project((g + 15) // 4, 0)
            if (g + 13) % 4 == 0 and 0 <= g + 13 < heads:
                stack((g + 13) // 4, 0, pair)
                stack((g + 13) // 4, 1, project((g + 13) // 4, 1))
            if 0 <= g - 1 < heads:
                mixed(g - 1)
            if (g - 19) % 16 == 0 and g >= 19:
                modulation((g - 19) // 16)
        end2 = [Token(w, len(w.ops) - 1) for w in rest.queues()[:4] if w.ops]
        r_stored = Landed(s_rst.handle, s_rst.n)
        x_loaded = [Landed(s.handle, s.n) for s in stage.sems]
        p2b.close()

        HF = FF // 2
        p3 = ExitStack()
        STG3 = [sbp(p3, f"STGC{i}", [128, 3, 512], F32) for i in range(2)]
        FH = [sbp(p3, f"FH{i}", [128, 4, S], F32R) for i in range(2)]
        FL = [sbp(p3, f"FL{i}", [128, 4, S], F32R) for i in range(2)]
        GW = [sbp(p3, f"GW{i}", [128, 4, HF], F32R) for i in range(2)]
        UW = [sbp(p3, f"UW{i}", [128, 4, HF], F32R) for i in range(2)]
        DW = [sbp(p3, f"DW{i}", [128, 8, DM], F32R) for i in range(2)]
        SG = [sbp(p3, f"SG{i}", [128, S], F32) for i in range(2)]
        GF = [sbp(p3, f"GF{i}", [128, S], F32) for i in range(2)]
        GH = [sbp(p3, f"GH{i}", [128, S], F32R) for i in range(3)]
        GL = [sbp(p3, f"GL{i}", [128, S], F32R) for i in range(3)]
        XT = [sbp(p3, f"XT{i}", [128, DM], F32) for i in range(4)]
        ST = [sbp(p3, f"ST{i}", [128, DM], F32) for i in range(4)]
        M1 = [sbp(p3, f"M1{i}", [128, DM], F32) for i in range(4)]
        XN = [sbp(p3, f"XN{i}", [128, DM], F32) for i in range(2)]
        s_r = [Sem(sem(f"s_r{i}")) for i in range(2)]
        s_t = [Sem(sem(f"s_t{i}")) for i in range(4)]
        s_m = [Sem(sem(f"s_m{i}")) for i in range(4)]
        s_wf = [Sem(sem(f"s_wf{i}")) for i in range(2)]
        stg_free = [[*over, *x_loaded], [*over, *x_loaded]]
        fr_free, gh_free, sg_free = [[r_stored, *over], [r_stored, *over]], [[], [], []], [[], []]
        xt_free, m1_free, xn_free = [list(end2) for _ in range(4)], [list(end2) for _ in range(4)], [[], []]
        tw, loaded, summed = {}, [None] * 4, [None] * 4
        G_G, G_U, G_D = (0, 1), (2, 3), (4, 5, 6, 7)
        gn = 0
        xt2 = x.rearrange("(n p) d -> n p d", p=128)
        st2 = s_d.rearrange("(n p) d -> n p d", p=128)
        mt2 = m_d.rearrange("(n p) d -> n p d", p=128)
        ot2 = out.rearrange("(n p) d -> n p d", p=128)
        wd2 = WdT.rearrange("(f p) m -> f p m", p=128)
        l2b = L2C[:, :].unsqueeze(2).to_broadcast([128, 4, 128])

        def slice_of(n, *waits):
            u, f = n % 2, n % 8
            c = slice(128 * f, 128 * f + 128)
            S3 = STG3[u]
            dma(s_wf[u], S3[:, 0, :], WgT[n], *stg_free[u])
            dma(s_wf[u], S3[:, 1, :], WuT[n])
            d = dma(s_wf[u], S3[:, 2, :], wd2[n])
            tw[n] = []
            for j, Wt in ((0, GW), (1, UW)):
                w = S3[:, j, :].rearrange("p (k m) -> p k m", k=4)
                t = tt(w, w, l2b, ALU.mult, d)
                tw[n] += split(Wt[0][:, :, c], Wt[1][:, :, c], w, t, *waits)
            tw[n] += split(DW[0][:, f, :], DW[1][:, f, :], S3[:, 2, :], d, *waits)
            stg_free[u] = tw[n]

        def rows_in(b):
            dma(s_r[b % 2], FH[b % 2][:, :, :], rh_d[b], *fr_free[b % 2])
            return dma(s_r[b % 2], FL[b % 2][:, :, :], rl_d[b])

        slice_of(0, *end2)
        dr = rows_in(0)
        slice_of(1, *end2)
        for half in range(2):
            pend = None
            for b in range(NB):
                rb = b % 2
                if half or b:
                    dr = dr_next
                acc = [None] * 4

                def down(f, g, tg, acc=acc):
                    for k in range(4):
                        if f == 0:
                            acc[k] = bank(G_D)
                        i, p, w = acc[k]
                        for q, (l_, r_) in enumerate(((GH[g], DW[0]), (GH[g], DW[1]), (GL[g], DW[0]))):
                            t = mm(p[:, :], l_[:, 128 * k:128 * k + 128], r_[:, f, :], f == 0 and q == 0, f == 7 and q == 2,
                                   *tg, *(w if f == 0 else []))
                    gh_free[g] = [t]
                    return t

                def written(b, u):
                    n = 4 * b + u
                    z = ts(XN[u % 2][:, :], XT[u][:, :], MEAN[:, n:n + 1], RSTD[:, n:n + 1], ALU.subtract, ALU.mult, loaded[u],
                           *xn_free[u % 2], q=rest.pool)
                    v = tt(M1[u][:, :], M1[u][:, :], XN[u % 2][:, :], ALU.add, summed[u], z)
                    xn_free[u % 2] = [v]
                    a = activate(M1[u][:, :], M1[u][:, :], ACT.Silu, v)
                    v = tt(M1[u][:, :], M1[u][:, :], ST[u][:, :], ALU.mult, a)
                    v = tt(M1[u][:, :], M1[u][:, :], XT[u][:, :], ALU.add, v)
                    xt_free[u] = [dma(s_t[u], ot2[n], M1[u][:, :], v)]

                def fetched(b):
                    for u in range(4):
                        n = 4 * b + u
                        dma(s_t[u], XT[u][:, :], xt2[n], *xt_free[u])
                        dma(s_t[u], ST[u][:, :], st2[n])
                        loaded[u] = dma(s_t[u], M1[u][:, :], mt2[n])

                def finish(b, acc, t):
                    for k in range(4):
                        i, p, w = acc[k]
                        n, u = 4 * b + k, k
                        if half == 0:
                            v = vcopy(M1[u][:, :], p[:, :], t, *m1_free[u])
                            drains(i, v)
                            m1_free[u] = [dma(s_m[u], mt2[n], M1[u][:, :], v)]
                        else:
                            dl = loaded[u]
                            v = tt(M1[u][:, :], M1[u][:, :], p[:, :], ALU.add, t, dl)
                            drains(i, v)
                            summed[u] = v

                for f in range(8):
                    i, p, w = bank(G_G)
                    c = slice(128 * f, 128 * f + 128)
                    xh, xl = (lambda k: FH[rb][:, k, :]), (lambda k: FL[rb][:, k, :])
                    three(p[:, :], lambda k: GW[0][:, k, c], lambda k: GW[1][:, k, c], xh, xl, 4, [*w, dr, *tw[8 * half + f]], close=False)
                    t = mm(p[:, :], BS[:, HF * half + 128 * f:HF * half + 128 * f + 128], MS[:, S * b:S * b + S], False, True,
                           *t_bs, *last_ms)
                    i2, p2_, w2 = bank(G_U)
                    t2 = three(p2_[:, :], lambda k: UW[0][:, k, c], lambda k: UW[1][:, k, c], xh, xl, 4, w2)
                    u, g = gn % 2, gn % 3
                    a = activate(SG[u][:, :], p[:, :], ACT.Silu, t, *sg_free[u])
                    drains(i, a)
                    v = tt(GF[u][:, :], SG[u][:, :], p2_[:, :], ALU.mult, a, t2)
                    drains(i2, v)
                    a = acopy(GH[g][:, :], GF[u][:, :], v, *gh_free[g])
                    l = tt(GL[g][:, :], GF[u][:, :], GH[g][:, :].bitcast(F32), ALU.subtract, a)
                    sg_free[u] = [l]
                    gn += 1
                    if pend is not None:
                        tdn = pend[0](*pend[1])
                        if pend[2] is not None:
                            pend[2](tdn)
                    fin = (lambda t, b=b, acc=acc: finish(b, acc, t)) if f == 7 else None
                    pend = (down, (f, g, [a, l]), fin)
                    if f == 0 and (half == 0 or b + 1 < NB):
                        dr_next = rows_in((b + 1) % NB)
                    if half == 1 and 1 <= f <= 4 and b > 0:
                        written(b - 1, f - 1)
                    if half == 0 and b == 0 and f < 6:
                        slice_of(f + 2, *end2)
                    if half == 1 and f == 5:
                        fetched(b)
                    if half == 0 and b == NB - 1 and f > 0:
                        slice_of(7 + f, t2, tdn)
                fr_free[rb] = [t2]
            tdn = pend[0](*pend[1])
            pend[2](tdn)
            if half == 0:
                slice_of(15, tdn)
                for u in range(4):
                    xt_free[u] = xt_free[u] + m1_free[u]
        for u in range(4):
            written(NB - 1, u)
        final = [Landed(s.handle, s.n) for s in s_t + s_m + [s_rst] if s.n]
        p3.close()
        p2.close()
        rest.sp.ops.append([lambda e: e.nop(), final, False, None])

        for part_ in (first, general, fast, rest):
            for q in part_.queues():
                q.count()
        block = ctx.enter_context(nc.Block())

        def run(n, e):
            first.queues()[n].emit(e)
            e.wait_ge(*t_flag.value())
            differ = e.value_load(FLAG[0:1, 0:1], min_val=0, max_val=128)
            with e.If(differ != 0):
                last(general, g_ends, n, e)
            with e.Else():
                last(fast, f_ends, n, e)
            e.wait_ge(joined, 5)
            rest.queues()[n].emit(e)

        def last(branch, ends, n, e):
            q = branch.queues()[n]
            q.emit(e)
            if n == 4:
                for w in ends:
                    e.wait_ge(*w.value())
            elif q.ops:
                e.wait_ge(*Token(q, len(q.ops) - 1).value())
            e.sem_inc(joined, 1)

        @block.tensor
        def _(e):
            run(0, e)

        @block.scalar
        def _(e):
            run(1, e)

        @block.vector
        def _(e):
            run(2, e)

        @block.gpsimd
        def _(e):
            run(3, e)

        @block.sync
        def _(e):
            run(4, e)


def layout(a):
    a = {k.replace("L0_attn_", "a_").replace("L0_ffn_", "f_"): np.asarray(v) for k, v in a.items()}
    c = np.ascontiguousarray
    f = np.float32

    def col(v):
        return c(v.reshape(-1, 128).T)

    def tiled(v):
        return c(v.reshape(16, 128, 4, 128).transpose(0, 3, 2, 1).reshape(16, 128, 512))
    i, j = np.indices((128, 128))
    wx = np.zeros((DI, 66), f)
    for at, rows in ((0, slice(0, NS)), (32, slice(NS, 2 * NS)), (64, slice(2 * NS, 2 * NS + 1))):
        wx[:, at:at + rows.stop - rows.start] = a["a_W_x"].T[:, rows]
    return {
        "x": c(a["a_x"].reshape(T, DM)), "WinT": c(a["a_W_in"].T), "convw": c(a["a_conv_w"].reshape(DI, 4)),
        "convb": col(a["a_conv_b"]), "WxT": wx, "Alog": c(a["a_A_log"]), "dtb": col(a["a_dt_bias"]),
        "outWT": c(a["a_out_W"].T), "Dp": col(a["a_D"]), "ln1": col(a["f_ln1_w"]), "ln2": col(a["f_ln2_w"]),
        "WqT": c(a["f_Wq"].T), "WkT": c(a["f_Wk"].T), "Wv": c(a["f_Wv"]), "Wo": c(a["f_Wo"]), "Aw": c(a["f_A"]),
        "Bw": c(a["f_B"]), "WgT": tiled(a["f_W_in_base"]), "WuT": tiled(a["f_W_up_base"]), "WdT": c(a["f_W_down"].T),
        "ident": np.eye(128, dtype=f), "maskt": np.where(j <= i, 0.0, NEG).astype(f),
        "maskT": np.where(j >= i, 0.0, NEG).astype(f),
        "arow": c(a["a_A_log"][0].reshape(NS, 1)), "umask": np.stack([j > i, j >= i], 1).astype(f),
    }


def kernel(**inputs):
    from concourse import bacc
    from concourse.bass_utils import run_bass_kernel_spmd

    arrays = layout(inputs)
    nc = bacc.Bacc("TRN2", target_bir_lowering=False, num_devices=1, dynamic_dma_scratch_size=1024)
    feeds, args = {}, {}
    for name, a in arrays.items():
        feeds[f"in_{name}_dram"] = a
        args[name] = nc.dram_tensor(f"in_{name}_dram", a.shape, mybir.dt.from_np(a.dtype), kind="ExternalInput").ap()
    args["out"] = nc.dram_tensor("out_0_dram", (T, DM), F32, kind="ExternalOutput").ap()
    build(nc, **args)
    r = run_bass_kernel_spmd(nc, [feeds], core_ids=[0])
    return r.results[0]["out_0_dram"].reshape(NB, S, DM)
```
